# Optimizing a Trainium2 kernel written in Bass

```python
import numpy as np
import jax
import jax.numpy as jnp

def _softmax(x, axis=-1):
    return jax.nn.softmax(x, axis=axis)

def _gelu(x):
    return jax.nn.gelu(x, approximate=True)

def _silu(x):
    return jax.nn.silu(x)

def _sigmoid(x):
    return jax.nn.sigmoid(x)

def _layernorm(x, axis=-1, eps=1e-05):
    m = jnp.mean(x, axis=axis, keepdims=True)
    v = jnp.var(x, axis=axis, keepdims=True)
    return (x - m) / jnp.sqrt(v + eps)

def _scatter_add(tgt, idx, src, axis=0):
    return tgt.at[idx].add(src)

def _segment_sum(src, seg, n):
    return jax.ops.segment_sum(src, seg, n)
kernel_name = 'mk_gnn_preln_d4_gnn_r8_8dee88'

def setup_inputs(seed: int=0):
    np.random.seed(seed)
    _w = jnp.asarray

    def _rec_inputs():
        import jax
        import jax.numpy as jnp
        _gk = jax.random.key(seed)
        x = -0.000202 + 1 * jax.random.normal(jax.random.fold_in(_gk, 1), (12500, 128), jnp.float32)
        src = jax.random.randint(jax.random.fold_in(_gk, 2), (200000,), 0, 12500, jnp.int32)
        dst = jax.random.randint(jax.random.fold_in(_gk, 3), (200000,), 0, 12500, jnp.int32)
        _o = jnp.argsort(dst, stable=True)
        src = src[_o]
        dst = dst[_o]
        edge_attr_128 = -6.47781e-05 + 0.999943 * jax.random.normal(jax.random.fold_in(_gk, 12), (200000, 128), jnp.float32)
        edge_weight = jax.random.uniform(jax.random.fold_in(_gk, 14), (200000,), jnp.float32, 0.0, 0.999998)
        return (x, src, dst, edge_attr_128, edge_weight)
    x, src, dst, edge_attr_128, edge_weight = _rec_inputs()

    def _L0_gnn_setup():
        import jax, jax.numpy as jnp
        import numpy as np
        N_NODES = 6250
        key = jax.random.key(seed)
        ks = jax.random.split(key, 8)
        x = jax.random.normal(ks[0], (N_NODES, 128), dtype=jnp.float32)
        edge_attr = jax.random.normal(ks[1], (200000, 128), dtype=jnp.float32)
        u = jax.random.normal(ks[2], (1, 16), dtype=jnp.float32)
        d_in = 128 + 128 + 16
        W1 = jax.random.normal(ks[3], (d_in, 1024), dtype=jnp.float32) * (1.0 / np.sqrt(d_in))
        b1 = jnp.zeros((1024,), dtype=jnp.float32)
        W2 = jax.random.normal(ks[4], (1024, 128), dtype=jnp.float32) * (1.0 / np.sqrt(1024))
        b2 = jnp.zeros((128,), dtype=jnp.float32)
        edge_index = jax.random.randint(ks[5], (2, 200000), 0, N_NODES, dtype=jnp.int64)
        return {'x': x, 'edge_attr': edge_attr, 'u': u, 'W1': W1, 'b1': b1, 'W2': W2, 'b2': b2, 'edge_index': edge_index}
    _L0_gnn_all = _L0_gnn_setup()
    _L0_gnn_in = {k: v for k, v in _L0_gnn_all.items() if k in ('u', 'W1', 'b1', 'W2', 'b2')}
    del _L0_gnn_all

    def _L1_gnn_setup():
        import jax, jax.numpy as jnp
        import numpy as np
        N_NODES = 6250
        N_EDGES = 80000
        D_IN = 128
        D_OUT = 128
        key = jax.random.key(seed)
        ks = jax.random.split(key, 8)
        scale_in = 1.0 / np.sqrt(D_IN)
        return {'x': jax.random.normal(ks[0], (N_NODES, D_IN), dtype=jnp.float32), 'r_feat': jax.random.normal(ks[1], (N_EDGES, D_IN), dtype=jnp.float32), 'src': jax.random.randint(ks[2], (N_EDGES,), 0, N_NODES), 'dst': jax.random.randint(ks[3], (N_EDGES,), 0, N_NODES), 'w': jax.random.normal(ks[4], (D_OUT, D_IN), dtype=jnp.float32) * scale_in, 'w_r': jax.random.normal(ks[5], (D_OUT, D_IN), dtype=jnp.float32) * scale_in, 'att_w': jax.random.normal(ks[6], (3 * D_OUT,), dtype=jnp.float32) * (1.0 / np.sqrt(3 * D_OUT)), 'loop_w': jax.random.normal(ks[7], (D_OUT, D_OUT), dtype=jnp.float32) * (1.0 / np.sqrt(D_OUT))}
    _L1_gnn_all = _L1_gnn_setup()
    _L1_gnn_in = {k: v for k, v in _L1_gnn_all.items() if k in ('w', 'w_r', 'att_w', 'loop_w')}
    del _L1_gnn_all

    def _L2_gnn_setup():
        import jax, jax.numpy as jnp
        import numpy as np
        ALPHA = 0.5
        N_NODES = 12500
        N_EDGES = 200000
        D_IN = 128
        D_OUT = 128

        def _inv_sqrt(deg):
            return jnp.where(deg > 0, jax.lax.rsqrt(jnp.maximum(deg, 1e-30)), 0.0)
        key = jax.random.key(seed)
        k1, k2, k3, k4, k5, k6 = jax.random.split(key, 6)
        x = jax.random.normal(k1, (N_NODES, D_IN), dtype=jnp.float32)
        edge_index = jax.random.randint(k2, (2, N_EDGES), 0, N_NODES, dtype=jnp.int64)
        s = 1.0 / np.sqrt(D_IN)
        W_src = jax.random.uniform(k3, (D_OUT, D_IN), jnp.float32, -s, s)
        b_src = jax.random.uniform(k4, (D_OUT,), jnp.float32, -s, s)
        W_dst = jax.random.uniform(k5, (D_OUT, D_IN), jnp.float32, -s, s)
        b_dst = jax.random.uniform(k6, (D_OUT,), jnp.float32, -s, s)
        return {'x': x, 'edge_index': edge_index, 'W_src': W_src, 'b_src': b_src, 'W_dst': W_dst, 'b_dst': b_dst}
    _L2_gnn_all = _L2_gnn_setup()
    _L2_gnn_in = {k: v for k, v in _L2_gnn_all.items() if k in ('W_src', 'b_src', 'W_dst', 'b_dst')}
    del _L2_gnn_all

    def _L3_gnn_setup():
        import jax, jax.numpy as jnp
        import numpy as np
        N, D, E = (12500, 128, 78125)
        EPS = 1e-05
        key = jax.random.key(seed)
        ks = jax.random.split(key, 8)
        node = jax.random.normal(ks[0], (N, D), dtype=jnp.float32)
        edge_index = jax.random.randint(ks[1], (2, E), 0, N, dtype=jnp.int64)
        edge_attr = jax.random.uniform(ks[2], (E,), dtype=jnp.float32)
        batch_ptr = jnp.sort(jax.random.randint(ks[3], (9,), 0, N, dtype=jnp.int64))
        s = 1.0 / np.sqrt(D)
        W_rel = jax.random.uniform(ks[4], (D, D), dtype=jnp.float32, minval=-s, maxval=s)
        b_rel = jax.random.uniform(ks[5], (D,), dtype=jnp.float32, minval=-s, maxval=s)
        W_root = jax.random.uniform(ks[6], (D, D), dtype=jnp.float32, minval=-s, maxval=s)
        gamma = jnp.ones((D,), dtype=jnp.float32)
        beta = jnp.zeros((D,), dtype=jnp.float32)
        return {'node': node, 'edge_index': edge_index, 'edge_attr': edge_attr, 'batch_ptr': batch_ptr, 'W_rel': W_rel, 'b_rel': b_rel, 'W_root': W_root, 'gamma': gamma, 'beta': beta}
    _L3_gnn_all = _L3_gnn_setup()
    _L3_gnn_in = {k: v for k, v in _L3_gnn_all.items() if k in ('batch_ptr', 'W_rel', 'b_rel', 'W_root', 'gamma', 'beta')}
    del _L3_gnn_all
    return {'x': x, 'src': src, 'dst': dst, 'edge_attr_128': edge_attr_128, 'edge_weight': edge_weight, 'L0_gnn_u': _L0_gnn_in['u'], 'L0_gnn_W1': _L0_gnn_in['W1'], 'L0_gnn_b1': _L0_gnn_in['b1'], 'L0_gnn_W2': _L0_gnn_in['W2'], 'L0_gnn_b2': _L0_gnn_in['b2'], 'L1_gnn_w': _L1_gnn_in['w'], 'L1_gnn_w_r': _L1_gnn_in['w_r'], 'L1_gnn_att_w': _L1_gnn_in['att_w'], 'L1_gnn_loop_w': _L1_gnn_in['loop_w'], 'L2_gnn_W_src': _L2_gnn_in['W_src'], 'L2_gnn_b_src': _L2_gnn_in['b_src'], 'L2_gnn_W_dst': _L2_gnn_in['W_dst'], 'L2_gnn_b_dst': _L2_gnn_in['b_dst'], 'L3_gnn_batch_ptr': _L3_gnn_in['batch_ptr'], 'L3_gnn_W_rel': _L3_gnn_in['W_rel'], 'L3_gnn_b_rel': _L3_gnn_in['b_rel'], 'L3_gnn_W_root': _L3_gnn_in['W_root'], 'L3_gnn_gamma': _L3_gnn_in['gamma'], 'L3_gnn_beta': _L3_gnn_in['beta']}

def reference(x, src, dst, edge_attr_128, edge_weight, L0_gnn_u, L0_gnn_W1, L0_gnn_b1, L0_gnn_W2, L0_gnn_b2, L1_gnn_w, L1_gnn_w_r, L1_gnn_att_w, L1_gnn_loop_w, L2_gnn_W_src, L2_gnn_b_src, L2_gnn_W_dst, L2_gnn_b_dst, L3_gnn_batch_ptr, L3_gnn_W_rel, L3_gnn_b_rel, L3_gnn_W_root, L3_gnn_gamma, L3_gnn_beta):
    import jax
    import jax.numpy as jnp

    def _L0_gnn_ref(x, edge_attr, u, W1, b1, W2, b2, edge_index):
        import jax, jax.numpy as jnp
        import numpy as np
        N_NODES = 6250
        n = x.shape[0]
        recv_idx = edge_index[1]
        recv_agg = jax.ops.segment_sum(edge_attr, recv_idx, num_segments=n)
        u_b = jnp.broadcast_to(u, (n, u.shape[-1]))
        collected = jnp.concatenate([recv_agg, x, u_b], axis=-1)
        h = jax.nn.relu(collected @ W1 + b1)
        updated_nodes = h @ W2 + b2
        return updated_nodes

    def _L1_gnn_ref(x, r_feat, src, dst, w, w_r, att_w, loop_w):
        import jax, jax.numpy as jnp
        import numpy as np
        N_NODES = 6250
        N_EDGES = 80000
        D_IN = 128
        D_OUT = 128
        n = x.shape[0]
        h = x @ w.T
        rh = r_feat @ w_r.T
        d = h.shape[1]
        s_src = h @ att_w[:d]
        s_dst = h @ att_w[d:2 * d]
        s_rel = rh @ att_w[2 * d:]
        e = jax.nn.leaky_relu(s_src[src] + s_dst[dst] + s_rel)
        m = jax.ops.segment_max(e, dst, num_segments=n)
        ex = jnp.exp(e - m[dst])
        denom = jax.ops.segment_sum(ex, dst, num_segments=n)
        alpha = ex / denom[dst]
        msg = alpha[:, None] * (h[src] + rh)
        agg = jax.ops.segment_sum(msg, dst, num_segments=n)
        deg = jax.ops.segment_sum(jnp.ones_like(e), dst, num_segments=n)
        h_out = jnp.where(deg[:, None] > 0, agg + h @ loop_w, h)
        return jax.nn.relu(h_out)

    def _L2_gnn_ref(x, edge_index, W_src, b_src, W_dst, b_dst):
        import jax, jax.numpy as jnp
        import numpy as np
        ALPHA = 0.5
        N_NODES = 12500
        N_EDGES = 200000
        D_IN = 128
        D_OUT = 128

        def _inv_sqrt(deg):
            return jnp.where(deg > 0, jax.lax.rsqrt(jnp.maximum(deg, 1e-30)), 0.0)
        n = x.shape[0]
        row, col = (edge_index[0], edge_index[1])
        ones = jnp.ones(row.shape[0], dtype=x.dtype)
        deg_out = jax.ops.segment_sum(ones, row, num_segments=n)
        deg_in = jax.ops.segment_sum(ones, col, num_segments=n)
        w = _inv_sqrt(deg_out)[row] * _inv_sqrt(deg_in)[col]
        agg_fwd = jax.ops.segment_sum(w[:, None] * x[col], row, num_segments=n)
        agg_bwd = jax.ops.segment_sum(w[:, None] * x[row], col, num_segments=n)
        out = ALPHA * (agg_fwd @ W_src.T + b_src) + (1.0 - ALPHA) * (agg_bwd @ W_dst.T + b_dst)
        return out

    def _L3_gnn_ref(node, edge_index, edge_attr, batch_ptr, W_rel, b_rel, W_root, gamma, beta):
        import jax, jax.numpy as jnp
        import numpy as np
        N, D, E = (12500, 128, 78125)
        EPS = 1e-05
        n = node.shape[0]
        src, dst = (edge_index[0], edge_index[1])
        msg = edge_attr[:, None] * node[src]
        ssum = jax.ops.segment_sum(msg, dst, num_segments=n)
        cnt = jax.ops.segment_sum(jnp.ones_like(edge_attr), dst, num_segments=n)
        agg = ssum / jnp.maximum(cnt, 1.0)[:, None]
        h = agg @ W_rel.T + b_rel + node @ W_root.T
        out = node + h
        mu = jnp.mean(out, axis=-1, keepdims=True)
        var = jnp.var(out, axis=-1, keepdims=True)
        ln = (out - mu) * jax.lax.rsqrt(var + EPS) * gamma + beta
        return jax.nn.relu(ln)
    edge_index = jnp.stack([src, dst])
    h = jnp.maximum(_layernorm(x, axis=-1), 0.0)
    x = x + _L0_gnn_ref(h, edge_attr_128, L0_gnn_u, L0_gnn_W1, L0_gnn_b1, L0_gnn_W2, L0_gnn_b2, edge_index)
    h = jnp.maximum(_layernorm(x, axis=-1), 0.0)
    x = x + _L1_gnn_ref(h, edge_attr_128, src, dst, L1_gnn_w, L1_gnn_w_r, L1_gnn_att_w, L1_gnn_loop_w)
    h = jnp.maximum(_layernorm(x, axis=-1), 0.0)
    x = x + _L2_gnn_ref(h, edge_index, L2_gnn_W_src, L2_gnn_b_src, L2_gnn_W_dst, L2_gnn_b_dst)
    h = jnp.maximum(_layernorm(x, axis=-1), 0.0)
    x = x + _L3_gnn_ref(h, edge_index, edge_weight, L3_gnn_batch_ptr, L3_gnn_W_rel, L3_gnn_b_rel, L3_gnn_W_root, L3_gnn_gamma, L3_gnn_beta)
    return x

_drawn_inputs = setup_inputs


def setup_inputs(seed=0):
    import zlib

    import numpy as np

    out = dict(_drawn_inputs(seed))
    spreads = {'L0_gnn_b1': (0.0, 0.1),
     'L0_gnn_b2': (0.0, 0.1),
     'L3_gnn_gamma': (1.0, 0.2),
     'L3_gnn_beta': (0.0, 0.435)}
    factors = {'edge_weight': 6.352, 'L2_gnn_b_src': 5.639, 'L2_gnn_b_dst': 5.039, 'L3_gnn_b_rel': 3.6}
    for name, (base, spread) in spreads.items():
        noise = np.random.default_rng([zlib.crc32(name.encode()), seed]).standard_normal(out[name].shape)
        drawn = base * np.exp(spread * noise) if base else spread * noise
        out[name] = jnp.asarray(drawn.astype(out[name].dtype))
    for name, factor in factors.items():
        out[name] = (out[name] * factor).astype(out[name].dtype)
    return out
```

```python
import concourse.bass as bass
from concourse import mybir
from contextlib import ExitStack

F32 = mybir.dt.float32
I32 = mybir.dt.int32
U32 = mybir.dt.uint32
BF16 = mybir.dt.bfloat16
ALU = mybir.AluOpType
ACT = mybir.ActivationFunctionType
AX = mybir.AxisListType.X

D = 128
BE = 512
TP = 80
UN = 6
TW = 132
BIG = float(2 ** 100)
M0 = -1.0e20
EPS = 1e-5


def gnn(nc, x, src, dst, ea, ew, u, W1, b1, W2, b2, w, w_r, att, loop_w, Ws, bs, Wd, bd_,
        Wrel, brel, Wroot, gamma, beta, out):
    NN, NE = x.shape[0], src.shape[0]
    NBF = (NE - 4 * TP) // BE
    NR = NBF + 1
    NW = (NN + 127) // 128
    NG = (NN + 511) // 512
    NP = NG * 512
    assert NE == NBF * BE + 4 * TP and NBF % UN == 0 and NN % 4 == 0 and NW <= 98
    grows = [min(512, NN - 512 * g) // 4 for g in range(NG)]
    chunks = [(c, min(128, NR - c)) for c in range(0, NR, 128)]
    NCH = len(chunks)

    def dram(name, shape, dt=F32):
        return nc.dram_tensor(name, shape, dt, kind="Internal").ap()

    x1d, x2d, x3d, h2d = (dram(n, (NP, D)) for n in ("x1d", "x2d", "x3d", "h2d"))
    t1d = dram("t1d", (NP, TW))
    t2d, t3d, t4d = (dram(n, (NP, D)) for n in ("t2d", "t3d", "t4d"))
    sortd = dram("sortd", (NE, 2), I32)
    rngd = dram("rngd", (2, NR, 2), I32)

    top = ExitStack()

    def sb(name, shape, dt=F32):
        return top.enter_context(nc.sbuf_tensor(name, shape, dt))

    NC = max(NN + 132, 12632)
    AB = sb("AB", [128, 2, NC])
    R = sb("R", [128, NC])
    KLD = sb("KLD", [128, NR * 4])
    IDX = sb("IDX", [128, NR * 4], I32)
    SREL = sb("SREL", [128, NR * 4])
    GS = sb("GS", [128, UN, 4, TW])
    XR = sb("XR", [128, max(UN * BE, 2 * NR * 4)])
    RNG = sb("RNG", [64, 2 * NR], I32)
    ID = sb("ID", [128, 128])
    IDB = sb("IDB", [128, 128], BF16)
    ONE = sb("ONE", [128, 128])
    IO = sb("IO", [128, 128])
    IOB = sb("IOB", [128, 64], BF16)
    DIN = sb("DIN", [128, NG * 4])
    DOUT = sb("DOUT", [128, NG * 4])
    EA = XR[:, 0:UN * BE].rearrange("p (s r f) -> p s r f", s=UN, r=4)
    GF = GS[:].rearrange("p s r f -> p (s r f)")
    PS = top.enter_context(nc.psum_tensor("PS", [128, 8, 512], F32))

    nsem = [0]

    def reg(e, name):
        nsem[0] += 1
        return e.alloc_register(f"{name}{nsem[0]}")

    class Phase:

        def __init__(self):
            self.ctx = ExitStack()
            self.q = {k: [] for k in ("sync", "gpsimd", "vector", "scalar", "tensor")}
            self.s = {}
            self.nt = 0

        def sem(self, name):
            if name not in self.s:
                nsem[0] += 1
                self.s[name] = nc.alloc_semaphore(name=f"{name}_{nsem[0]}")
            return self.s[name]

        def on(self, eng):
            def add(f):
                self.q[eng].append(f)
                return f
            return add

        def tile(self, shape, dt=F32, name="w"):
            self.nt += 1
            nsem[0] += 1
            return self.ctx.enter_context(nc.sbuf_tensor(f"{name}{nsem[0]}", shape, dt))

        def run(self):
            with self.ctx:
                with nc.Block() as blk:
                    place = {"sync": blk.sync, "gpsimd": blk.gpsimd, "vector": blk.vector,
                             "scalar": blk.scalar, "tensor": blk.tensor}
                    for eng, fs in self.q.items():
                        def emit(e, fs=fs):
                            for f in fs:
                                f(e)
                        place[eng](emit)
            nc.clear_and_free_semaphores(list(self.s.values()))
            nc.all_engine_barrier()

    def chain(e, sem):
        n = [0]

        def link(ins):
            n[0] += 1
            ins.then_inc(sem, 1)
            e.wait_ge(sem, n[0])
        return link

    def ranges(e, part, col, n):
        return nc.values_load_multi_w_load_instructions(
            RNG[32 * part:32 * part + 1, bass.ds(col, n)], engines=[e.engine], min_val=0, max_val=NN + 1,
            skip_runtime_bounds_check_because="keys are node numbers")[1]

    def p_const():
        p = Phase()
        z, c = p.sem("z"), p.sem("c")

        @p.on("gpsimd")
        def _(e):
            link = chain(e, z)
            e.iota(IO[:], [[1, 128]], base=0, channel_multiplier=0, allow_small_or_imprecise_dtypes=True)
            e.memset(ONE[:], 1.0)
            link(e.memset(ID[:], 0.0))
            link(e.affine_select(out=ID[:], in_=ID[:], compare_op=ALU.not_equal, fill=1.0, base=0,
                                 pattern=[[-1, 128]], channel_multiplier=1))

        @p.on("vector")
        def _(e):
            e.memset(DIN[:], 0.0)
            e.memset(DOUT[:], 0.0)
            e.wait_ge(z, 2)
            e.tensor_copy(IDB[:], ID[:])
            e.tensor_copy(IOB[:], IO[:, 0:64]).then_inc(c, 1)
            e.wait_ge(c, 1)
        p.run()

    def turn_rows(p, ready, pairs):
        tr, cp = p.sem("tr"), p.sem("cp")
        jobs = [(f, t, ci, r) for f, t in pairs for ci in range(NCH) for r in range(4)]

        @p.on("tensor")
        def _(e):
            e.wait_ge(*ready)
            for k, (f, t, ci, r) in enumerate(jobs):
                n = chunks[ci][1]
                if k >= 8:
                    e.wait_ge(cp, k - 7)
                v = f[0:n, ci, :].rearrange("b (p r) -> b r p", r=4)[:, r, :]
                e.transpose(PS[:, k % 8, 0:n], v, ID[0:n, 0:n]).then_inc(tr, 1)

        @p.on("vector")
        def _(e):
            for k, (f, t, ci, r) in enumerate(jobs):
                c0, n = chunks[ci]
                e.wait_ge(tr, k + 1)
                o = t.rearrange("p (b r) -> p b r", r=4)[:, c0:c0 + n, r]
                e.tensor_copy(o, PS[:, k % 8, 0:n]).then_inc(cp, 1)
            e.wait_ge(cp, len(jobs))

    def load_list(p, kind, part, keys, full, raw_f=None):
        B = AB[:, 1, :]
        W = BE * (1 if kind == "in" else 2)
        stg = [B[:, i * NCH * W:(i + 1) * NCH * W].bitcast(I32).rearrange("p (c k) -> p c k", c=NCH)
               for i in range(2 if kind == "in" else 1)]
        o = 2 * NCH * BE
        fl = [B[:, o + i * NCH * BE:o + (i + 1) * NCH * BE].rearrange("p (c k) -> p c k", c=NCH) for i in range(3)]
        mn, mx, rg = p.tile([128, NCH]), p.tile([128, NCH]), p.tile([128, NCH, 2], I32)
        ld, st, dv, rs = (p.sem(n) for n in ("ld", "st", "dv", "rs"))
        nld = [0]

        @p.on("sync")
        def _(e):
            def put(o, i):
                e.dma_start(o, i).then_inc(ld, 16)
                nld[0] += 1
            srcs = [(stg[0], dst, 1), (stg[1], src, 1)] if kind == "in" else [(stg[0], sortd.rearrange("e t -> (e t)"), 2)]
            for t, d, m in srcs:
                for ci, (c0, n) in enumerate(chunks):
                    nf = min(n, NBF - c0)
                    if nf:
                        put(t[0:nf, ci, :], d[c0 * BE * m:(c0 + nf) * BE * m].rearrange("(b k) -> b k", k=BE * m))
                n = (NR - 1) % 128
                put(t[n:n + 1, NCH - 1, 0:4 * TP * m], d[NBF * BE * m:NE * m].rearrange("(b k) -> b k", b=1))
                put(t[n:n + 1, NCH - 1, 4 * TP * m:BE * m],
                    d[NBF * BE * m:NBF * BE * m + (BE - 4 * TP) * m].rearrange("(b k) -> b k", b=1))

        @p.on("vector")
        def _(e):
            e.wait_ge(ld, 16 * nld[0])
            if kind == "in":
                a, b = stg[0], stg[1]
            else:
                v = stg[0].rearrange("p c (k t) -> p c k t", t=2)
                b, a = v[:, :, :, 0], v[:, :, :, 1]
            link = chain(e, dv)
            for ci, (c0, n) in enumerate(chunks):
                e.tensor_copy(fl[0][0:n, ci, :], a[0:n, ci, :])
                last = e.tensor_copy(fl[1][0:n, ci, :], b[0:n, ci, :])
            link(last)
            for ci, (c0, n) in enumerate(chunks):
                e.tensor_reduce(mn[0:n, ci:ci + 1], fl[0][0:n, ci, :], AX, ALU.min)
                last = e.tensor_reduce(mx[0:n, ci:ci + 1], fl[0][0:n, ci, :], AX, ALU.max)
            link(last)
            for ci, (c0, n) in enumerate(chunks):
                e.tensor_copy(rg[0:n, ci, 0:1], mn[0:n, ci:ci + 1])
                e.tensor_scalar(rg[0:n, ci, 1:2], mx[0:n, ci:ci + 1], 1.0, None, ALU.add)
                last = e.tensor_scalar(fl[2][0:n, ci, :], fl[0][0:n, ci, :], mn[0:n, ci:ci + 1], None, ALU.subtract)
            link(last)

        @p.on("scalar")
        def _(e):
            e.wait_ge(dv, 3)
            for ci, (c0, n) in enumerate(chunks):
                e.dma_start(rngd[part, c0:c0 + n, :], rg[0:n, ci, :]).then_inc(st, 16)
            e.wait_ge(st, 16 * NCH)
            e.dma_start(RNG[32 * part:32 * part + 1, :], rngd[part].rearrange("(o r) t -> o (r t)", o=1)).then_inc(rs, 16)
            e.wait_ge(rs, 16)

        turn_rows(p, (dv, 3), [(fl[2], keys)] + [(fl[i], t) for i, t in full])

    B0 = AB[:, 1, :]
    _o = [0]

    def take(n, dt=F32):
        v = B0[:, _o[0]:_o[0] + n]
        _o[0] += n
        return v if dt == F32 else v.bitcast(dt)

    PAY = take(NR * 8, I32).rearrange("p (b t) -> p b t", t=2)
    AW = take(NR * 4)
    POS = take(NR * 4, I32)
    LOW, UPI, ONB = (take(64, BF16) for _ in range(3))
    IOA = take(49, BF16)
    BASE = take(392)
    V3 = take(128)
    OH = [take(196, BF16) for _ in range(2)]
    PR = [take(392) for _ in range(2)]
    LISTEND = _o[0]

    def p_lists():
        p = Phase()
        load_list(p, "in", 0, KLD[:], [(0, AB[:, 0, 0:NR * 4]), (1, AB[:, 0, NR * 4:NR * 8])])
        p.run()

    def p_prep():
        p = Phase()
        dn, oh, mm, g = p.sem("dn"), p.sem("oh"), p.sem("mm"), p.sem("g")
        ff = p.sem("ff")
        DF, SF = AB[:, 0, 0:NR * 4], AB[:, 0, NR * 4:NR * 8]

        @p.on("gpsimd")
        def _(e):
            link = chain(e, g)
            T = AB[:, 0, NR * 8:NR * 8 + 256]
            e.memset(T[:, 128:256], 1.0)
            link(e.memset(T[:, 0:128], 1.0))
            e.affine_select(out=T[:, 0:128], in_=T[:, 0:128], compare_op=ALU.is_gt, fill=0.0, base=0,
                            pattern=[[1, 128]], channel_multiplier=-1)
            link(e.affine_select(out=T[:, 128:256], in_=T[:, 128:256], compare_op=ALU.is_ge, fill=0.0, base=0,
                                 pattern=[[-1, 128]], channel_multiplier=1))

        wr, at3 = p.tile([128, 128]), p.tile([128, 1])
        ld = p.sem("ld")

        @p.on("sync")
        def _(e):
            e.dma_start(wr[:], w_r).then_inc(ld, 16)
            e.dma_start(at3[:], att[2 * D:3 * D].rearrange("(p o) -> p o", o=1)).then_inc(ld, 16)

        TI = AB[:, 0, NR * 8 + 256:NR * 12 + 256].bitcast(I32)

        @p.on("vector")
        def _(e):
            link = chain(e, dn)
            e.tensor_copy(IDX[:], SF)
            e.tensor_copy(PAY[:, :, 0], DF)
            e.tensor_copy(ONB, ONE[:])
            e.tensor_copy(IOA, IO[:, 0:98])
            e.tensor_copy(OH[1], IO[:, 0:1].to_broadcast([128, 392]))
            link(e.tensor_copy(PAY[:, :, 1], SF))
            link(e.tensor_scalar(TI, IDX[:], 7, None, ALU.arith_shift_right))
            e.wait_ge(g, 2)
            e.tensor_copy(LOW, AB[:, 0, NR * 8:NR * 8 + 128])
            e.tensor_copy(UPI, AB[:, 0, NR * 8 + 128:NR * 8 + 256])
            link(e.tensor_copy(AW, TI))
            def ohs(s, c):
                for r in range(4):
                    i = e.tensor_scalar(OH[s][:, 98 * r:98 * r + 98], IOA, AW[:, bass.ds(c + r, 1)], None, ALU.is_equal)
                return i
            k = reg(e, "k")
            e.reg_mov(k, 1)
            with e.Fori(0, NBF // 2) as h:
                for s in range(2):
                    e.wait_ge(mm, e.snap(k))
                    ohs(s, h * 8 + 4 * s).then_inc(oh, 1)
                    e.reg_add(k, k, 1)
            e.wait_ge(mm, NBF + 1)
            ohs(0, 4 * NBF).then_inc(oh, 1)
            e.wait_ge(mm, NBF + 3)
            tot = PR[0].rearrange("p (a r) -> p r a", r=4)
            link(e.tensor_copy(tot, PS[:, 0, 0:392].rearrange("p (r a) -> p r a", r=4)))
            link(e.memset(BASE, 1.0))
            link(e.tensor_tensor_scan(PR[1], BASE, PR[0], 0.0, ALU.mult, ALU.add))
            link(e.tensor_tensor(PR[1], PR[1], PR[0], ALU.subtract))
            e.tensor_copy(V3, PS[:, 1, 0:128])
            link(e.tensor_copy(BASE.rearrange("p (r a) -> p r a", r=4), PR[1].rearrange("p (a r) -> p r a", r=4)))

        @p.on("tensor")
        def _(e):
            e.wait_ge(ld, 32)
            e.matmul(PS[:, 1, 0:128], at3[:, 0:1].to_broadcast([128, 128]), wr[:], start=True, stop=True).then_inc(mm, 1)
            e.wait_ge(dn, 3)
            e.matmul(PS[:, 0, 0:392], ONB, OH[1], start=True, stop=False, skip_group_check=True).then_inc(mm, 1)
            k = reg(e, "kp")
            e.reg_mov(k, 1)
            with e.Fori(0, NBF, 2):
                for s in range(2):
                    e.wait_ge(oh, e.snap(k))
                    e.matmul(PS[:, 0, 0:392], ONB, OH[s], start=False, stop=False, skip_group_check=True).then_inc(mm, 1)
                    e.reg_add(k, k, 1)
            e.wait_ge(oh, NBF + 1)
            e.matmul(PS[:, 0, 0:392], ONB[0:TP, :], OH[0][0:TP, :], start=False, stop=True, skip_group_check=True).then_inc(mm, 1)
        p.run()

    NIT = NBF // UN

    def batches(e, step):
        with e.Fori(0, NIT) as it:
            for s in range(UN):
                step(it * UN + s, s, it, False)
        step(NBF, 0, NIT, True)

    def unit_ranges(e, part):
        held = {}

        def get(b, s, it, last):
            if last:
                return ranges(e, part, 2 * NBF, 2)
            if s == 0:
                held[0] = ranges(e, part, it * (2 * UN), 2 * UN)
            return held[0][2 * s:2 * s + 2]
        return get

    def edge_pass(p, width, part, keys, feats, ready, rstep, ACC, weight=None, count=True, rank=False):
        acc, mmd, oh, bd, dv, kx = (p.sem(n) for n in ("acc", "mmd", "oh", "bd", "dv", "kx"))
        SEL = [p.tile([128, 4, width]) for _ in range(2)]
        KX, TY = p.tile([128, 4]), p.tile([1, 1])
        if rank:
            ohr, low, rd, pos, sr = (p.sem(n) for n in ("ohr", "low", "rd", "pos", "sr"))
            PF = [p.tile([128, 4]) for _ in range(2)]
            SF = [p.tile([128, 4]) for _ in range(2)]
            JK = p.tile([128, 4, 128])

        def sel(e, s, kl, b):
            o = SEL[s % 2]
            if weight is None:
                return e.tensor_tensor(o[:], IO[:, 0:width].unsqueeze(1).to_broadcast([128, 4, width]),
                                       kl.unsqueeze(2).to_broadcast([128, 4, width]), ALU.is_equal)
            for r in range(4):
                i = e.tensor_scalar(o[:, r, :], IO[:, 0:width], kl[:, r:r + 1],
                                    weight[:, bass.ds(b * 4 + r, 1)], ALU.is_equal, ALU.mult)
            return i

        @p.on("vector")
        def _(e):
            link = chain(e, dv)
            e.memset(R[0:1, :], 0.0)
            e.memset(ACC, 0.0)
            if rank:
                e.memset(SF[0][:], 0.0)
            link(e.memset(SEL[1][:], 0.0))
            nu, na, nk, wp = (reg(e, x_) for x_ in ("nu", "na", "nk", "wp"))
            e.reg_mov(nu, 1)
            e.reg_mov(na, 1)
            e.reg_mov(nk, 0)
            e.reg_mov(wp, 0)
            e.nop().then_inc(acc, 1)
            get = unit_ranges(e, part)

            def linked(ins):
                ins.then_inc(kx, 1)
                e.reg_add(nk, nk, 1)

            def accumulate(q, wv, ends=True):
                n_mm, n_acc = e.snap(nu), e.snap(na)
                e.wait_ge(mmd, n_mm)
                e.wait_ge(acc, n_acc)
                if count:
                    i = e.tensor_tensor(R[0:1, bass.ds(wv, width)], R[0:1, bass.ds(wv, width)],
                                        PS[0:1, 2 + q, 0:width], ALU.add)
                elif ends:
                    i = e.memset(TY[:], 0.0)
                if ends:
                    i.then_inc(bd, 1)
                i = e.tensor_tensor(ACC[:, bass.ds(wv, width)], ACC[:, bass.ds(wv, width)],
                                    PS[:, q, 0:width], ALU.add).then_inc(acc, 1)
                e.reg_add(na, na, 1)
                return i

            def step(b, s, it, last):
                lo, hi = get(b, s, it, last)
                kl = keys[:, bass.ds(b * 4, 4)]
                with e.If(lo + width < hi):
                    linked(e.tensor_scalar(KX[:], kl, float(width), None, ALU.subtract))
                    with e.Fori(lo + width, hi, width) as wv:
                        e.wait_ge(kx, e.snap(nk))
                        sel(e, s, KX[:], b).then_inc(oh, 1)
                        e.reg_add(nu, nu, 1)
                        accumulate(s % 2, wv, False)
                        linked(e.tensor_scalar(KX[:], KX[:], float(width), None, ALU.subtract))
                e.end_ifs()
                sel(e, s, kl, b).then_inc(oh, 1)
                if rank:
                    for r in range(4):
                        i = e.tensor_scalar(OH[s % 2][:, 98 * r:98 * r + 98], IOA, AW[:, bass.ds(b * 4 + r, 1)],
                                            None, ALU.is_equal)
                    i.then_inc(ohr, 1)
                accumulate((s + 1) % 2, e.snap(wp, min_val=0, max_val=NN + 1))
                e.reg_add(nu, nu, 1)
                e.reg_mov(wp, lo)
                if rank:
                    e.wait_ge(ready[s], it * rstep + rstep)
                    m = TP if last else 128
                    for r in range(4):
                        i = e.tensor_tensor_reduce(JK[0:m, r, :], feats(s)[0:m, r, 0:D], V3[0:m, :], 1.0, 0.0,
                                                   ALU.mult, ALU.add, SF[s % 2][0:m, r:r + 1])
                    i.then_inc(sr, 1)
                    e.wait_ge(low, b + 1)
                    e.tensor_tensor(PR[s % 2], PS[:, 4, 0:392], OH[s % 2], ALU.mult).then_inc(rd, 1)
                    e.wait_ge(sr, b + 1)
                    e.tensor_copy(SREL[:, bass.ds(b * 4, 4)], SF[s % 2][:])
                    e.wait_ge(rd, b * 3 + 1)
                    e.tensor_reduce(PF[s % 2][:], PR[s % 2].rearrange("p (r a) -> p r a", r=4), AX, ALU.add).then_inc(rd, 1)
                    e.wait_ge(rd, b * 3 + 2)
                    e.tensor_copy(POS[:, bass.ds(b * 4, 4)], PF[s % 2][:]).then_inc(rd, 1)
            batches(e, step)
            accumulate(0, e.snap(wp, min_val=0, max_val=NN + 1))
            n_acc = e.snap(na)
            e.wait_ge(acc, n_acc)
            e.memset(TY[:], 0.0).then_inc(p.sem("edone"), 1)

        @p.on("tensor")
        def _(e):
            e.wait_ge(dv, 1)
            ku = reg(e, "ku")
            e.reg_mov(ku, 1)
            get = unit_ranges(e, part)
            if count:
                e.matmul(PS[0:1, 3, 0:width], ONE[:, 0:1], SEL[1][:, 0, :], start=True, stop=True)
            e.matmul(PS[:, 1, 0:width], ONE[:], SEL[1][:, 0, :], start=True, stop=True).then_inc(mmd, 1)
            if rank:
                e.matmul(PS[:, 4, 0:392], ID[:], BASE, start=True, stop=False, skip_group_check=True)

            def unit(s, m):
                k = e.snap(ku)
                e.wait_ge(oh, k)
                e.wait_ge(acc, k)
                if count:
                    for r in range(4):
                        e.matmul(PS[0:1, 2 + s % 2, 0:width], ONE[0:m, 0:1], SEL[s % 2][0:m, r, :],
                                 start=(r == 0), stop=(r == 3))
                for r in range(4):
                    i = e.matmul(PS[:, s % 2, 0:width], feats(s)[0:m, r, 0:D], SEL[s % 2][0:m, r, :],
                                 start=(r == 0), stop=(r == 3))
                i.then_inc(mmd, 1)
                e.reg_add(ku, ku, 1)

            def step(b, s, it, last):
                m = TP if last else 128
                lo, hi = get(b, s, it, last)
                e.wait_ge(ready[s], it * rstep + rstep)
                with e.If(lo + width < hi):
                    with e.Fori(lo + width, hi, width):
                        unit(s, m)
                e.end_ifs()
                if rank:
                    e.wait_ge(ohr, b + 1)
                    e.matmul(PS[:, 4, 0:392], LOW[0:m, :], OH[s % 2][0:m, :], start=False, stop=False,
                             skip_group_check=True).then_inc(low, 1)
                unit(s, m)
                if rank and not last:
                    e.wait_ge(rd, b * 3 + 1)
                    e.matmul(PS[:, 4, 0:392], UPI, OH[s % 2], start=False, stop=False, skip_group_check=True)
            batches(e, step)
        return bd

    def load_ea(p, bd):
        ready = [p.sem(f"ea{s}") for s in range(UN)]

        @p.on("sync")
        def _(e):
            v = ea[0:NBF * BE, :].rearrange("(b p r) f -> b p (r f)", p=128, r=4)
            t = ea[NBF * BE:NE, :].rearrange("(p r) f -> p (r f)", r=4)

            def one(b, s):
                e.dma_start(XR[:, s * BE:(s + 1) * BE], v[bass.ds(b, 1)].rearrange("b p k -> (b p) k")).then_inc(ready[s], 16)
            for s in range(UN):
                one(s, s)
            if NIT > 1:
                with e.Fori(1, NIT) as it:
                    for s in range(UN):
                        e.wait_ge(bd, (it - 1) * UN + (s + 2))
                        one(it * UN + s, s)
            e.wait_ge(bd, (NIT - 1) * UN + 2)
            e.dma_start(XR[0:TP, 0:BE], t).then_inc(ready[0], 16)
            for s in range(UN):
                e.wait_ge(ready[s], 16 * (NIT + (s == 0)))
        return ready

    def gather(p, bd, table, idx, wide):
        ready = [p.sem(f"g{s}") for s in range(UN)]

        @p.on("gpsimd")
        def _(e):
            for b in range(NR):
                s = b % UN
                m = TP if b == NBF else 128
                if b >= UN:
                    e.wait_ge(bd, b - UN + 2)
                for r in range(4):
                    c = 4 * b + r
                    e.indirect_dma_start(GS[0:m, s, r, 0:wide], None, table,
                                         bass.IndirectOffsetOnAxis(ap=idx[0:m, c:c + 1].bitcast(U32), axis=0)
                                         ).then_inc(ready[s], 16)
            for s in range(UN):
                e.wait_ge(ready[s], 64 * (NIT + (s == 0)))
        return ready

    def p_l0():
        p = Phase()
        ready = load_ea(p, p.sem("bd"))
        edge_pass(p, 64, 0, KLD[:], lambda s: EA[:, s], ready, 16, AB[:, 0, :], rank=True)
        rd = p.sem("rd")
        sc = [p.sem(f"sc{i}") for i in range(4)]

        @p.on("gpsimd")
        def _(e):
            for b in range(NR):
                m = TP if b == NBF else 128
                e.wait_ge(rd, 3 * b + 3)
                for r in range(4):
                    c = 4 * b + r
                    e.indirect_dma_start(sortd, bass.IndirectOffsetOnAxis(ap=POS[0:m, c:c + 1].bitcast(U32), axis=0),
                                         PAY[0:m, c, :], None).then_inc(sc[r], 16)
            for r in range(4):
                e.wait_ge(sc[r], 16 * NR)
        l0_nodes(p)
        p.run()

    def rowsl(ap, g):
        n = grows[g]
        return ap[512 * g:512 * g + 4 * n, :].rearrange("(p j) f -> p (j f)", j=4)

    def jp(ap, g):
        return ap[:, 512 * g:512 * g + 4 * grows[g]].rearrange("f (p j) -> f j p", j=4)

    class Norm:

        def __init__(self, p, tag):
            self.p, self.t = p, tag
            self.st = [p.tile([128, 4, 6]) for _ in range(2)]
            self.mv = [p.tile([128, 4, 2]) for _ in range(2)]
            self.sd = [p.tile([128, 4]) for _ in range(2)]
            self.rs = [p.tile([128, 4]) for _ in range(2)]
            self.nm = [p.tile([128, 4]) for _ in range(2)]
            self.a, self.b, self.c, self.d, self.e_, self.f = (p.sem(f"{tag}{i}") for i in range(6))

        def moments(self, e, xt, g):
            n, s = grows[g], g % 2
            for j in range(4):
                i = e.bn_stats(self.st[s][0:n, j, :], xt[0:n, j, :])
            i.then_inc(self.a, 1)
            e.wait_ge(self.a, g + 1)
            if g >= 2:
                e.wait_ge(self.f, g - 1)
            for j in range(4):
                i = e.bn_aggr(self.mv[s][0:n, j, :], self.st[s][0:n, j, :])
            i.then_inc(self.b, 1)
            e.wait_ge(self.b, g + 1)
            e.tensor_scalar(self.sd[s][0:n, :], self.mv[s][0:n, :, 1], EPS, None, ALU.add).then_inc(self.c, 1)

        def root(self, e, g):
            n, s = grows[g], g % 2
            e.wait_ge(self.c, g + 1)
            e.activation(self.sd[s][0:n, :], self.sd[s][0:n, :], ACT.Sqrt).then_inc(self.d, 1)

        def scale(self, e, g):
            n, s = grows[g], g % 2
            e.wait_ge(self.d, g + 1)
            e.reciprocal(self.rs[s][0:n, :], self.sd[s][0:n, :]).then_inc(self.e_, 1)
            e.wait_ge(self.e_, 2 * g + 1)
            e.scalar_tensor_tensor(out=self.nm[s][0:n, :], in0=self.mv[s][0:n, :, 0], scalar=-1.0,
                                   in1=self.rs[s][0:n, :], op0=ALU.mult, op1=ALU.mult).then_inc(self.e_, 1)

        def apply(self, e, out, xt, g):
            n, s = grows[g], g % 2
            e.wait_ge(self.e_, 2 * g + 2)
            for j in range(4):
                i = e.activation(out[0:n, j, 0:D], xt[0:n, j, :], ACT.Relu, bias=self.nm[s][0:n, j:j + 1],
                                 scale=self.rs[s][0:n, j:j + 1])
            i.then_inc(self.f, 1)

    def l0_nodes(p):
        o = [0]

        def at(region, off, n):
            return region[:, off:off + n]
        XT = [at(XR, 1024 + 512 * i, 512).rearrange("p (j f) -> p j f", j=4) for i in range(2)]
        XT.append(p.tile([128, 4, D]))
        H0 = [at(XR, 2048 + 512 * i, 512).rearrange("p (j f) -> p j f", j=4) for i in range(2)]
        HID = [at(GF, 512 * m, 512) if m < 6 else at(XR, 512 * (m - 6), 512) for m in range(8)]
        W1S = B0[:, LISTEND:LISTEND + 2048].rearrange("p (k h) -> p k h", k=2)
        W2S = B0[:, LISTEND + 2048:LISTEND + 3072].rearrange("p (m f) -> p m f", m=8)
        H0T = [B0[:, LISTEND + 3072 + 512 * i:LISTEND + 3584 + 512 * i] for i in range(2)]
        assert LISTEND + 4096 <= NC and NR * 4 >= 2 * 4 * TW or NBF < 300
        HT = [p.tile([128, 4, TW]) if NBF < 300 else AW[:, 528 * i:528 * i + 528].rearrange("p (j f) -> p j f", j=4)
              for i in range(2)]
        H1T = [B0[:, LISTEND - 784:LISTEND - 272]]
        UT, B1, B1E, AT, V12, B2 = (p.tile([16, 1]), p.tile([128, 8]), p.tile([128, 8]),
                                    p.tile([128, 2]), p.tile([128, 2]), p.tile([1, 128]))
        WW = p.tile([128, 128])
        W1U = XR[0:16, 2048:3072]
        ed, wl = p.sem("edone"), p.sem("wl")
        xl = [p.sem(f"xl{i}") for i in range(3)]
        xs, hs = [p.sem(f"xs{i}") for i in range(3)], [p.sem(f"hs{i}") for i in range(2)]
        n0, n1 = Norm(p, "n"), Norm(p, "m")
        t0, c0, ph, hd, py, pb = (p.sem(k) for k in ("t0", "c0", "ph", "hd", "py", "pb"))
        t1, c1, t2, c2, pre, prd = (p.sem(k) for k in ("t1", "c1", "t2", "c2", "pre", "prd"))

        @p.on("sync")
        def _(e):
            for t, d in ((UT[:], u.rearrange("o k -> k o")),
                         (B1[:], b1.rearrange("(m p) -> p m", p=128)), (WW[:], w),
                         (AT[:], att[0:256].rearrange("(k p) -> p k", p=128)), (B2[:], b2.rearrange("(o f) -> o f", o=1)),
                         (W1S, W1[0:256, :].rearrange("(k p) h -> p k h", p=128)),
                         (W2S, W2.rearrange("(m p) f -> p m f", p=128))):
                e.dma_start(t, d, allow_slow_non_contiguous=True).then_inc(wl, 16)
            e.wait_ge(ed, 1)
            e.dma_start(W1U, W1[256:272, :]).then_inc(wl, 16)
            def load(g):
                n = grows[g]
                e.dma_start(XT[g % 3][0:n].rearrange("p j f -> p (j f)"), rowsl(x, g)).then_inc(xl[g % 3], 16)
            for g in range(min(3, NG)):
                load(g)
            for g in range(NG):
                store(e, g)
                if g + 3 < NG:
                    e.wait_ge(n1.f, g + 1)
                    e.wait_ge(xs[g % 3], 16 * (g // 3 + 1))
                    load(g + 3)
            for i in range(3):
                e.wait_ge(xs[i], 16 * ((NG + 2 - i) // 3))
            for i in range(2):
                e.wait_ge(hs[i], 16 * ((NG + 1 - i) // 2))

        def store(e, g):
            n = grows[g]
            e.wait_ge(pb, g + 1)
            e.dma_start(rowsl(x1d, g), XT[g % 3][0:n].rearrange("p j f -> p (j f)")).then_inc(xs[g % 3], 16)
            e.wait_ge(c2, g + 1)
            e.dma_start(rowsl(t1d, g), HT[g % 2][0:n].rearrange("p j f -> p (j f)")).then_inc(hs[g % 2], 16)

        @p.on("tensor")
        def _(e):
            e.wait_ge(wl, 16 * 8)
            e.wait_ge(ed, 1)
            for m in range(8):
                e.matmul(PS[:, 6, m:m + 1], W1U[:, 128 * m:128 * m + 128], UT[:], start=True, stop=True)
            e.matmul(PS[:, 6, 8:9], WW[:], AT[:, 0:1], start=True, stop=True)
            e.matmul(PS[:, 6, 9:10], WW[:], AT[:, 1:2], start=True, stop=True).then_inc(pre, 1)

            def turn0(g):
                n = grows[g]
                e.wait_ge(n0.f, g + 1)
                if g:
                    e.wait_ge(c0, g)
                for j in range(4):
                    i = e.transpose(PS[:, 3, n * j:n * j + n], H0[g % 2][0:n, j, :], ID[0:n, 0:n])
                i.then_inc(t0, 1)

            def mlp(g):
                n = grows[g]
                e.wait_ge(c0, g + 1)
                if g == 0:
                    e.wait_ge(prd, 1)
                for m in range(8):
                    k = 8 * g + m
                    if k >= 2:
                        e.wait_ge(hd, k - 1)
                    e.matmul(PS[:, m % 2, 0:4 * n].rearrange("h (j p) -> h j p", j=4), W1S[:, 0, 128 * m:128 * m + 128],
                             jp(AB[:, 0, :], g), start=True, stop=False)
                    e.matmul(PS[:, m % 2, 0:4 * n], W1S[:, 1, 128 * m:128 * m + 128], H0T[g % 2][:, 0:4 * n],
                             start=False, stop=True).then_inc(ph, 1)
                if g:
                    e.wait_ge(pb, g)
                for j in range(4):
                    for m in range(8):
                        if j == 0:
                            e.wait_ge(hd, 8 * g + m + 1)
                        e.matmul(PS[0:n, 2, 128 * j:128 * j + 128], HID[m][:, n * j:n * j + n], W2S[:, m, :],
                                 start=(m == 0), stop=False)
                    i = e.matmul(PS[0:n, 2, 128 * j:128 * j + 128], ONE[0:1, 0:n], B2[:], start=False, stop=True)
                i.then_inc(py, 1)

            def turn1(g):
                n = grows[g]
                e.wait_ge(n1.f, g + 1)
                if g:
                    e.wait_ge(c1, g)
                for j in range(4):
                    i = e.transpose(PS[:, 5, n * j:n * j + n], HT[g % 2][0:n, j, 0:D], ID[0:n, 0:n])
                i.then_inc(t1, 1)
                e.wait_ge(c1, g + 1)
                if g:
                    e.wait_ge(c2, g)
                for j in range(4):
                    e.matmul(PS[0:n, 6, j:j + 1], H1T[0][:, n * j:n * j + n], V12[:, 0:1], start=True, stop=True)
                    e.matmul(PS[0:n, 6, 4 + j:5 + j], jp(R[0:1, :], g)[:, j, :], ONE[0:1, 0:1], start=True, stop=True)
                e.matmul(PS[0:1, 7, 0:4 * n], V12[:, 1:2], H1T[0][:, 0:4 * n], start=True, stop=True).then_inc(t2, 1)
            turn0(0)
            for g in range(NG):
                if g + 1 < NG:
                    turn0(g + 1)
                mlp(g)
                if g:
                    turn1(g - 1)
            turn1(NG - 1)

        @p.on("scalar")
        def _(e):
            def root0(g):
                n0.root(e, g)

            def app0(g):
                if g >= 2:
                    e.wait_ge(t0, g - 1)
                n0.apply(e, H0[g % 2], XT[g % 3], g)

            def hid(g):
                n = grows[g]
                if g == 0:
                    e.wait_ge(prd, 1)
                for m in range(8):
                    e.wait_ge(ph, 8 * g + m + 1)
                    e.activation(HID[m][:, 0:4 * n], PS[:, m % 2, 0:4 * n], ACT.Relu, bias=B1E[:, m:m + 1]).then_inc(hd, 1)

            def app1(g):
                if g >= 2:
                    e.wait_ge(hs[g % 2], 16 * (g // 2))
                n1.apply(e, HT[g % 2], XT[g % 3], g)
            root0(0)
            e.wait_ge(pre, 1)
            app0(0)
            for g in range(NG):
                if g:
                    n1.root(e, g - 1)
                if g + 1 < NG:
                    root0(g + 1)
                    app0(g + 1)
                hid(g)
                if g:
                    app1(g - 1)
            n1.root(e, NG - 1)
            app1(NG - 1)

        @p.on("vector")
        def _(e):
            def first(g):
                e.wait_ge(xl[g % 3], 16 * (g // 3 + 1))
                n0.moments(e, XT[g % 3], g)
                n0.scale(e, g)

            def copy0(g):
                n = grows[g]
                e.wait_ge(t0, g + 1)
                e.tensor_copy(H0T[g % 2][:, 0:4 * n], PS[:, 3, 0:4 * n]).then_inc(c0, 1)

            def post(g):
                n = grows[g]
                e.wait_ge(py, g + 1)
                e.wait_ge(n0.f, g + 1)
                e.tensor_tensor(XT[g % 3][0:n], XT[g % 3][0:n], PS[0:n, 2, :].rearrange("p (j f) -> p j f", j=4),
                                ALU.add).then_inc(pb, 1)
                e.wait_ge(pb, g + 1)
                n1.moments(e, XT[g % 3], g)

            def tail(g):
                n = grows[g]
                e.wait_ge(t1, g + 1)
                e.tensor_copy(H1T[0][:, 0:4 * n], PS[:, 5, 0:4 * n]).then_inc(c1, 1)
                e.wait_ge(t2, g + 1)
                e.tensor_copy(HT[g % 2][0:n, :, D], PS[0:n, 6, 0:4])
                e.tensor_copy(DIN[0:n, 4 * g:4 * g + 4], PS[0:n, 6, 4:8])
                e.tensor_copy(jp(R[0:1, :], g), PS[0:1, 7, 0:4 * n].rearrange("o (j p) -> o j p", j=4)).then_inc(c2, 1)
            e.wait_ge(ed, 1)
            e.memset(HT[0][:, :, D:TW], 0.0)
            e.memset(HT[1][:, :, D:TW], 0.0)
            e.wait_ge(pre, 1)
            e.tensor_copy(V12[:], PS[:, 6, 8:10])
            e.tensor_tensor(B1E[:], B1[:], PS[:, 6, 0:8], ALU.add).then_inc(prd, 1)
            first(0)
            copy0(0)
            for g in range(NG):
                if g:
                    n1.scale(e, g - 1)
                if g + 1 < NG:
                    first(g + 1)
                    copy0(g + 1)
                if g:
                    tail(g - 1)
                post(g)
            n1.scale(e, NG - 1)
            tail(NG - 1)
            e.wait_ge(c2, NG)

    FLAG = sb("FLAG", [1, 2], I32)
    FT = AB[0:1, 0, 0:NR]

    def p_flag():
        p = Phase()
        c = p.sem("c")

        @p.on("vector")
        def _(e):
            link = chain(e, c)
            v = RNG[0:1, :].rearrange("o (b t) -> o b t", t=2)
            link(e.tensor_tensor(FT, v[:, :, 1], v[:, :, 0], ALU.subtract))
            e.tensor_copy(FLAG[:, 1:2], FT[:, 0:1])
            link(e.tensor_reduce(FLAG[:, 0:1], FT, AX, ALU.max))
        p.run()

    def p_l1():
        p = Phase()
        bd = p.sem("bd")
        ear = load_ea(p, bd)
        gr = gather(p, bd, t1d[0:NN, :], IDX[:], TW)
        s1, s2, s2a, s3, s4, s4a, s4b, s5, s6a, zz = (p.sem(k) for k in (
            "s1", "s2", "s2a", "s3", "s4", "s4a", "s4b", "s5", "s6a", "zz"))
        pu, pt, pr, pbc, pm = (p.sem(k) for k in ("pu", "pt", "pr", "pbc", "pm"))
        au, ac, acs, aw, kx = (p.sem(k) for k in ("au", "ac", "acs", "aw", "kx"))
        WD = 64
        NQ = [p.tile([128, 4, WD], BF16) for _ in range(2)]
        ZC = [p.tile([128, 4]) for _ in range(2)]
        U1 = [p.tile([128, 4, WD]) for _ in range(2)]
        LL = [p.tile([128, 4, WD]) for _ in range(2)]
        LM = [p.tile([128, 128]) for _ in range(2)]
        ZM = [p.tile([128, 1]) for _ in range(2)]
        MC = [p.tile([33, 2 * WD]) for _ in range(2)]
        DM = [p.tile([33, WD]) for _ in range(2)]
        CS = [p.tile([128, WD]) for _ in range(3)]
        WT = [p.tile([128, 4, WD]) for _ in range(2)]
        T6 = p.tile([128, 2, WD])
        T6R = p.tile([65, WD])
        KX, TY = p.tile([128, 4]), p.tile([1, 1])
        M = R[32:33, :]
        DEN = R[64:65, :]

        def uv(i):
            return PS[:, i, 0:4 * WD].rearrange("p (r n) -> p r n", r=4)

        def d1(e, i, s, kl, b):
            e.tensor_tensor(ZC[i][:], GS[:, s, :, D], SREL[:, bass.ds(b * 4, 4)], ALU.add)
            for r in range(4):
                n = e.tensor_scalar(NQ[i][:, r, :], IOB[:, 0:WD], kl[:, r:r + 1], -BIG, ALU.not_equal, ALU.mult)
            n.then_inc(s1, 1)

        def t1_(e, i, w_):
            u4 = uv(i)
            e.matmul(u4, IDB[:], NQ[i][:], start=True, stop=False)
            e.matmul(u4, ID[:], ZC[i][:].unsqueeze(2).to_broadcast([128, 4, WD]), start=False, stop=False)
            e.matmul(u4, ONE[0:1, :], R[0:1, bass.ds(w_, WD)].unsqueeze(1).to_broadcast([1, 4, WD]),
                     start=False, stop=True).then_inc(pu, 1)

        def a1(e, i):
            e.activation(U1[i][:], uv(i), ACT.Copy, scale=0.01).then_inc(au, 1)

        def d2(e, i, n):
            e.tensor_tensor(LL[i][:], U1[i][:], uv(i), ALU.max).then_inc(s2a, 1)
            e.wait_ge(s2a, n)
            e.tensor_reduce(LM[i][:, 0:WD], LL[i][:].rearrange("p r n -> p n r"), AX, ALU.max).then_inc(s2, 1)

        def t2_(e, i, m):
            e.transpose(PS[:, 2, 0:m], LM[i][0:m, :], ID[0:m, 0:m]).then_inc(pt, 1)

        def d3(e, i, m):
            e.tensor_reduce(ZM[i][:], PS[:, 2, 0:m], AX, ALU.max).then_inc(s3, 1)

        def t3_(e, i):
            e.matmul(PS[0:1, 2, 128:128 + WD], ZM[i][:], ID[:, 0:WD], start=True, stop=True).then_inc(pr, 1)

        def d4(e, i, w_, n):
            mn = MC[i][32:33, 0:WD]
            e.tensor_tensor(mn, M[:, bass.ds(w_, WD)], PS[0:1, 2, 128:128 + WD], ALU.max).then_inc(s4a, 1)
            e.wait_ge(s4a, n)
            e.tensor_tensor(DM[i][32:33, :], M[:, bass.ds(w_, WD)], mn, ALU.subtract).then_inc(s4b, 1)
            e.wait_ge(s4b, n)
            e.tensor_scalar(M[:, bass.ds(w_, WD)], mn, 1.0, None, ALU.mult).then_inc(s4, 1)

        def a2(e, i):
            e.activation(MC[i][32:33, WD:2 * WD], DM[i][32:33, :], ACT.Exp).then_inc(ac, 1)

        def t4_(e, i):
            e.matmul(PS[:, 3, 128 * i:128 * i + 128], ONE[32:33, :], MC[i][32:33, :], start=True, stop=True).then_inc(pbc, 1)

        def a3(e, i, j):
            e.activation(CS[j][:], PS[:, 3, 128 * i + WD:128 * i + 2 * WD], ACT.Copy).then_inc(acs, 1)

        def d5(e, i):
            e.tensor_tensor(LL[i][:], LL[i][:], PS[:, 3, 128 * i:128 * i + WD].unsqueeze(1).to_broadcast([128, 4, WD]),
                            ALU.subtract).then_inc(s5, 1)

        def a4(e, i):
            e.activation(WT[i][:], LL[i][:], ACT.Exp).then_inc(aw, 1)

        def t5_(e, i, s, m):
            for r in range(4):
                e.matmul(PS[:, 4 + i, 0:WD], GS[0:m, s, r, 0:D], WT[i][0:m, r, :], start=(r == 0), stop=(r == 3))
            for r in range(4):
                e.matmul(PS[:, 4 + i, WD:2 * WD], EA[0:m, s, r, :], WT[i][0:m, r, :], start=(r == 0), stop=(r == 3))
            for r in range(4):
                n = e.matmul(PS[0:1, 6 + i, 0:WD], ONE[0:m, 0:1], WT[i][0:m, r, :], start=(r == 0), stop=(r == 3))
            n.then_inc(pm, 1)

        def d6(e, i, j, w_, n, done):
            cur = AB[:, :, bass.ds(w_, WD)]
            dn = DEN[:, bass.ds(w_, WD)]
            e.tensor_tensor(T6R[64:65, :], dn, CS[j][64:65, :], ALU.mult)
            e.tensor_tensor(T6[:], cur, CS[j][:].unsqueeze(1).to_broadcast([128, 2, WD]), ALU.mult).then_inc(s6a, 1)
            e.wait_ge(s6a, n)
            e.tensor_tensor(dn, T6R[64:65, :], PS[0:1, 6 + i, 0:WD], ALU.add)
            e.tensor_tensor(cur, T6[:], PS[:, 4 + i, 0:2 * WD].rearrange("p (a n) -> p a n", a=2), ALU.add
                            ).then_inc(done, 1)

        def fast(e, stage):
            lo = [None]
            for s in range(UN):
                if s == 0:
                    v = ranges(e, 0, 0, 2 * UN)
                stage(s, s, 0, v[2 * s])
            if NIT > 1:
                with e.Fori(1, NIT) as it:
                    v = ranges(e, 0, it * (2 * UN), 2 * UN)
                    for s in range(UN):
                        stage(it * UN + s, s, it, v[2 * s])
            v = ranges(e, 0, 2 * NBF, 2)
            stage(NBF, 0, NIT, v[0])
            stage(NBF + 1, 1, NIT, None)
            stage(NBF + 2, 2, NIT, None)

        def past(k, n):
            return not isinstance(k, int) or k >= n

        def live(k, s=None):
            return not isinstance(k, int) or k <= NBF

        def rows(k):
            return TP if isinstance(k, int) and k == NBF else 128

        def general(e, unit, first=None, after=None):
            n = reg(e, "units")
            e.reg_mov(n, 1)
            get = unit_ranges(e, 0)

            def step(b, s, it, last):
                lo, hi = get(b, s, it, last)
                if first:
                    first(b, s, it)
                with e.Fori(lo, hi, WD) as w_:
                    unit(s, w_, e.snap(n), TP if last else 128, b, it)
                    e.reg_add(n, n, 1)
                if after:
                    after()
            batches(e, step)

        def flag(e):
            return nc.values_load_multi_w_load_instructions(
                FLAG[0:1, 0:1], engines=[e.engine], min_val=0, max_val=NN + 1,
                skip_runtime_bounds_check_because="a difference of node numbers")[1][0]

        @p.on("vector")
        def _(e):
            e.memset(AB[:], 0.0)
            e.memset(DEN, 0.0)
            for t in LM:
                e.memset(t[:], 0.0)
            e.memset(R[32:33, :], M0)
            e.memset(TY[:], 0.0).then_inc(zz, 1)
            e.wait_ge(zz, 1)
            e.nop().then_inc(bd, 1)
            fl = flag(e)
            w1, w2 = reg(e, "w1"), reg(e, "w2")
            nk = reg(e, "nkx")
            with e.If(fl <= WD):
                e.reg_mov(w1, 0)
                e.reg_mov(w2, 0)

                def first(b, s, it):
                    e.wait_ge(gr[s], it * 64 + 64)
                    if past(b, 2):
                        e.wait_ge(pu, b - 1)
                    d1(e, s % 2, s, KLD[:, bass.ds(b * 4, 4)], b)

                def stage(k, s, it, lo):
                    if not live(k):
                        if k == NBF + 1:
                            e.wait_ge(acs, k)
                            d5(e, (k - 1) % 2)
                        w_ = e.snap(w2, min_val=0, max_val=NN + 1)
                        e.wait_ge(pm, k - 1)
                        e.wait_ge(bd, k - 1)
                        d6(e, k % 2, (k - 2) % 3, w_, k - 1, bd)
                        e.reg_mov(w2, w1)
                        return
                    if not (isinstance(k, int) and k == NBF):
                        first(k + 1, (s + 1) % UN, it + (s == UN - 1))
                    e.wait_ge(au, k + 1)
                    if past(k, 2):
                        e.wait_ge(aw, k - 1)
                    d2(e, s % 2, k + 1)
                    if past(k, 1):
                        e.wait_ge(acs, k)
                        d5(e, (s + 1) % 2)
                    e.wait_ge(pt, k + 1)
                    d3(e, s % 2, rows(k))
                    if past(k, 2):
                        w_ = e.snap(w2, min_val=0, max_val=NN + 1)
                        e.wait_ge(pm, k - 1)
                        e.wait_ge(acs, k - 1)
                        e.wait_ge(bd, k - 1)
                        d6(e, s % 2, (s + 1) % 3, w_, k - 1, bd)
                    e.reg_mov(w2, w1)
                    e.reg_mov(w1, lo)
                    e.wait_ge(pr, k + 1)
                    if past(k, 1):
                        e.wait_ge(s4, k)
                    d4(e, s % 2, lo, k + 1)
                first(0, 0, 0)
                fast(e, stage)
                e.wait_ge(bd, NR + 1)
            with e.Else():
                e.reg_mov(nk, 0)

                def before(b, s, it):
                    e.wait_ge(gr[s], it * 64 + 64)
                    e.tensor_copy(KX[:], KLD[:, bass.ds(b * 4, 4)]).then_inc(kx, 1)
                    e.reg_add(nk, nk, 1)

                def unit(s, w_, n, m, b, it):
                    e.wait_ge(kx, e.snap(nk))
                    d1(e, 0, s, KX[:], b)
                    e.wait_ge(s1, n)
                    e.tensor_scalar(KX[:], KX[:], float(WD), None, ALU.subtract).then_inc(kx, 1)
                    e.reg_add(nk, nk, 1)
                    e.wait_ge(au, n)
                    d2(e, 0, n)
                    e.wait_ge(pt, n)
                    d3(e, 0, m)
                    e.wait_ge(pr, n)
                    d4(e, 0, w_, n)
                    e.wait_ge(acs, n)
                    d5(e, 0)
                    e.wait_ge(pm, n)
                    d6(e, 0, 0, w_, n, zz)
                    e.wait_ge(zz, n + 1)

                def after():
                    e.memset(TY[:], 0.0).then_inc(bd, 1)
                general(e, unit, before, after)

        @p.on("tensor")
        def _(e):
            fl = flag(e)
            e.wait_ge(zz, 1)
            with e.If(fl <= WD):
                def first(b, s, lo):
                    e.wait_ge(s1, b + 1)
                    if past(b, 2):
                        e.wait_ge(s2, b - 1)
                    t1_(e, s % 2, lo)
                v = ranges(e, 0, 0, 2)
                first(0, 0, v[0])
                nx = [None]

                def stage(k, s, it, lo):
                    if not live(k):
                        if k == NBF + 1:
                            e.wait_ge(aw, k)
                            t5_(e, (k - 1) % 2, 0, TP)
                        return
                    if not (isinstance(k, int) and k == NBF):
                        if s < UN - 1:
                            nxt = nx[0][2 * s + 2]
                        else:
                            nxt = ranges(e, 0, k * 2 + 2, 2)[0]
                        first(k + 1, (s + 1) % UN, nxt)
                    e.wait_ge(s2, k + 1)
                    if past(k, 1):
                        e.wait_ge(s3, k)
                    t2_(e, s % 2, rows(k))
                    e.wait_ge(s3, k + 1)
                    if past(k, 1):
                        e.wait_ge(s4, k)
                    t3_(e, s % 2)
                    if past(k, 1):
                        e.wait_ge(aw, k)
                        e.wait_ge(ear[(s - 1) % UN], it * 16 + (16 if s else 0))
                        if past(k, 3):
                            e.wait_ge(bd, k - 1)
                        t5_(e, (s + 1) % 2, (s - 1) % UN, 128)
                    e.wait_ge(ac, k + 1)
                    if past(k, 2):
                        e.wait_ge(s5, k - 1)
                        e.wait_ge(acs, k - 1)
                    t4_(e, s % 2)

                def outer(k, s, it, lo):
                    stage(k, s, it, lo)
                nx[0] = ranges(e, 0, 0, 2 * UN)
                for s in range(UN):
                    stage(s, s, 0, None)
                if NIT > 1:
                    with e.Fori(1, NIT) as it:
                        nx[0] = ranges(e, 0, it * (2 * UN), 2 * UN)
                        for s in range(UN):
                            stage(it * UN + s, s, it, None)
                stage(NBF, 0, NIT, None)
                e.wait_ge(ear[0], 16 * NIT + 16)
                stage(NBF + 1, 1, NIT, None)
            with e.Else():
                def unit(s, w_, n, m, b, it):
                    e.wait_ge(s1, n)
                    t1_(e, 0, w_)
                    e.wait_ge(s2, n)
                    t2_(e, 0, m)
                    e.wait_ge(s3, n)
                    t3_(e, 0)
                    e.wait_ge(ac, n)
                    t4_(e, 0)
                    e.wait_ge(aw, n)
                    e.wait_ge(ear[s], it * 16 + 16)
                    t5_(e, 0, s, m)
                general(e, unit)

        @p.on("scalar")
        def _(e):
            fl = flag(e)
            e.wait_ge(zz, 1)
            with e.If(fl <= WD):
                def first(b, s):
                    e.wait_ge(pu, b + 1)
                    a1(e, s % 2)
                first(0, 0)

                def stage(k, s, it, lo):
                    if not live(k):
                        if k == NBF + 1:
                            e.wait_ge(s5, k)
                            e.wait_ge(pm, k - 2)
                            a4(e, (k - 1) % 2)
                        return
                    if not (isinstance(k, int) and k == NBF):
                        first(k + 1, (s + 1) % UN)
                    if past(k, 1):
                        e.wait_ge(s5, k)
                        if past(k, 3):
                            e.wait_ge(pm, k - 2)
                        a4(e, (s + 1) % 2)
                    e.wait_ge(s4, k + 1)
                    a2(e, s % 2)
                    e.wait_ge(pbc, k + 1)
                    if past(k, 3):
                        e.wait_ge(bd, k - 1)
                    a3(e, s % 2, s % 3)
                for s in range(UN):
                    stage(s, s, 0, None)
                if NIT > 1:
                    with e.Fori(1, NIT) as it:
                        for s in range(UN):
                            stage(it * UN + s, s, it, None)
                stage(NBF, 0, NIT, None)
                stage(NBF + 1, 1, NIT, None)
            with e.Else():
                def unit(s, w_, n, m, b, it):
                    e.wait_ge(pu, n)
                    a1(e, 0)
                    e.wait_ge(s4, n)
                    a2(e, 0)
                    e.wait_ge(pbc, n)
                    a3(e, 0, 0)
                    e.wait_ge(s5, n)
                    a4(e, 0)
                general(e, unit)
        p.run()

    XT3 = [GF[:, 512 * i:512 * i + 512].rearrange("p (j f) -> p j f", j=4) for i in range(3)]
    GI3 = [GF[:, 1536 + 528 * i:1536 + 528 * i + 512].rearrange("p (j f) -> p j f", j=4) for i in range(3)]
    HTT = [XR[:, 512 * i:512 * i + 512] for i in range(2)]
    HO = [XR[:, 1024 + 512 * i:1536 + 512 * i].rearrange("p (j f) -> p j f", j=4) for i in range(2)]
    TO = [XR[:, 2048 + 512 * i:2560 + 512 * i].rearrange("p (j f) -> p j f", j=4) for i in range(2)]

    def flat(t, n):
        return t[0:n].rearrange("p j f -> p (j f)")

    def bank(i, n):
        return PS[0:n, i, :].rearrange("p (j f) -> p j f", j=4)

    def weights(p, specs, rows=()):
        wl, wt, wc = p.sem("wl"), p.sem("wt"), p.sem("wc")
        raw = [p.tile([128, 128]) for _ in specs]
        done = [p.tile([128, 128]) for _ in specs]
        rw = [p.tile([1, 128]) for _ in rows]
        rep = [p.tile([128, 128]) for _ in rows]

        @p.on("sync")
        def _(e):
            for t, d in zip(raw, specs):
                e.dma_start(t[:], d).then_inc(wl, 16)
            for t, d in zip(rw, rows):
                e.dma_start(t[:], d.rearrange("(o f) -> o f", o=1)).then_inc(wl, 16)
        n = len(specs) + len(rows)

        @p.on("tensor")
        def _(e):
            e.wait_ge(wl, 16 * n)
            for k, t in enumerate(raw):
                if k:
                    e.wait_ge(wc, k)
                e.transpose(PS[:, 7, 0:128], t[:], ID[:]).then_inc(wt, 1)
            for k, t in enumerate(rw):
                e.wait_ge(wc, len(raw) + k)
                e.matmul(PS[:, 7, 0:128], ONE[0:1, :], t[:], start=True, stop=True).then_inc(wt, 1)

        @p.on("vector")
        def _(e):
            for k, t in enumerate(done + rep):
                e.wait_ge(wt, k + 1)
                e.tensor_copy(t[:], PS[:, 7, 0:128]).then_inc(wc, 1)
        return raw, done, rw, rep, wc, n

    def nodes(p, xin, hin, hw, xout, turned, mm, evac, combine, finish, souts, ready, norm="act", pre=None):
        xl, gl = [p.sem(f"xl{i}") for i in range(3)], [p.sem(f"gl{i}") for i in range(3)]
        tp_, tc, pmm, ev, cb, fi = (p.sem(k) for k in ("tp", "tc", "pmm", "ev", "cb", "fi"))
        nr = Norm(p, "q")
        st = [[p.sem(f"st{a}_{i}") for i in range(3)] for a in range(len(souts) + 1)]
        rings = [3] + [len(r) for _, r, _ in souts]
        outs = ([(xout, XT3, cb)] if xout is not None else []) + souts
        rings = [len(r) for _, r, _ in outs]

        @p.on("sync")
        def _(e):
            def load(g):
                e.dma_start(flat(XT3[g % 3], grows[g]), rowsl(xin, g)).then_inc(xl[g % 3], 16)
                if hin is not None:
                    n = grows[g]
                    h = hin[512 * g:512 * g + 4 * n, :].rearrange("(p j) f -> p j f", j=4)[:, :, 0:D]
                    e.dma_start(GI3[g % 3][0:n], h).then_inc(gl[g % 3], 16)
            for g in range(min(3, NG)):
                load(g)
            for g in range(NG):
                n = grows[g]
                for a, (d, ring, sem) in enumerate(outs):
                    e.wait_ge(fi if sem is None else sem, g + 1)
                    e.dma_start(rowsl(d, g), flat(ring[g % len(ring)], n)).then_inc(st[a][g % len(ring)], 16)
                if g + 3 < NG:
                    if xout is not None:
                        e.wait_ge(st[0][g % 3], 16 * (g // 3 + 1))
                    e.wait_ge(fi, g + 1)
                    load(g + 3)
            for a, (d, ring, sem) in enumerate(outs):
                k = len(ring)
                for i in range(min(k, NG)):
                    e.wait_ge(st[a][i], 16 * ((NG - 1 - i) // k + 1))

        def stored(e, ring, g):
            for a, (d, r, sem) in enumerate(outs):
                if r is ring and g >= len(r):
                    e.wait_ge(st[a][g % len(r)], 16 * (g // len(r)))

        @p.on("tensor")
        def _(e):
            e.wait_ge(*ready)

            def turn(g):
                n = grows[g]
                e.wait_ge(gl[g % 3], 16 * (g // 3 + 1))
                if g:
                    e.wait_ge(tc, g)
                for j in range(4):
                    i = e.transpose(PS[:, 3, n * j:n * j + n], GI3[g % 3][0:n, j, :], ID[0:n, 0:n])
                i.then_inc(tp_, 1)
            if turned:
                turn(0)
            for g in range(NG):
                if turned and g + 1 < NG:
                    turn(g + 1)
                if turned:
                    e.wait_ge(tc, g + 1)
                if g:
                    e.wait_ge(cb, g)
                mm(e, g, grows[g]).then_inc(pmm, 1)

        @p.on("scalar")
        def _(e):
            for g in range(NG):
                if g:
                    nr.root(e, g - 1)
                e.wait_ge(pmm, g + 1)
                if g:
                    e.wait_ge(cb, g)
                evac(e, g, grows[g]).then_inc(ev, 1)
                if g and norm == "act":
                    if g >= 3:
                        e.wait_ge(fi, g - 2)
                    stored(e, HO, g - 1)
                    nr.apply(e, HO[(g - 1) % 2], XT3[(g - 1) % 3], g - 1)
            nr.root(e, NG - 1)
            if norm == "act":
                if NG >= 3:
                    e.wait_ge(fi, NG - 2)
                stored(e, HO, NG - 1)
                nr.apply(e, HO[(NG - 1) % 2], XT3[(NG - 1) % 3], NG - 1)

        @p.on("vector")
        def _(e):
            def copyt(g):
                e.wait_ge(tp_, g + 1)
                if g >= 2:
                    e.wait_ge(pmm, g - 1)
                e.tensor_copy(HTT[g % 2][:, 0:4 * grows[g]], PS[:, 3, 0:4 * grows[g]]).then_inc(tc, 1)
            if turned:
                copyt(0)

            def fin(g):
                if norm == "act":
                    e.wait_ge(nr.f, g + 1)
                else:
                    e.wait_ge(nr.e_, 2 * g + 2)
                for ring in (TO, HO):
                    if norm != "act" or ring is TO:
                        stored(e, ring, g)
                finish(e, g, grows[g], nr).then_inc(fi, 1)
            for g in range(NG):
                if g:
                    nr.scale(e, g - 1)
                if turned and g + 1 < NG:
                    copyt(g + 1)
                if pre:
                    pre(e, g, grows[g])
                e.wait_ge(ev, g + 1)
                e.wait_ge(xl[g % 3], 16 * (g // 3 + 1))
                if hin is not None:
                    e.wait_ge(gl[g % 3], 16 * (g // 3 + 1))
                if norm != "act" and g >= 3:
                    e.wait_ge(fi, g - 2)
                combine(e, g, grows[g]).then_inc(cb, 1)
                e.wait_ge(cb, g + 1)
                nr_src = XT3[g % 3] if norm == "act" else SC[g % 2]
                nr.moments(e, nr_src, g)
                if g:
                    fin(g - 1)
            nr.scale(e, NG - 1)
            fin(NG - 1)
            e.wait_ge(fi, NG)
        SC = [p.tile([128, 4, D]) for _ in range(2)] if norm != "act" else None
        return SC

    RIN = sb("RIN", [128, NG * 4])
    ROUT = sb("ROUT", [128, NG * 4])

    def p_l1_nodes():
        p = Phase()
        raw, wt_, _, _, wc, nw = weights(p, [w, w_r])
        WT_, WRT = wt_
        LW, WL = p.tile([128, 128]), p.tile([128, 128])
        P2S, T3 = p.tile([128, 4, D]), p.tile([128, 4, D])
        DC = [p.tile([128, 4]) for _ in range(2)]
        MK = [p.tile([128, 4]) for _ in range(2)]
        NM = [p.tile([128, 4]) for _ in range(2)]
        RD = [p.tile([128, 4]) for _ in range(2)]
        Q = p.tile([128, 4, D])
        TMP = p.tile([128, NG * 4])
        ll, wp, wq, dv, rin, rdn = (p.sem(k) for k in ("ll", "wp", "wq", "dv", "rin", "rdn"))
        cc, mkd = p.sem("cc"), p.sem("mkd")
        cn = [0]

        @p.on("sync")
        def _(e):
            e.dma_start(LW[:], loop_w).then_inc(ll, 16)

        @p.on("tensor")
        def _(e):
            e.wait_ge(ll, 16)
            e.wait_ge(wc, nw)
            e.matmul(PS[:, 7, 0:128], raw[0][:], LW[:], start=True, stop=True).then_inc(wp, 1)

        @p.on("scalar")
        def _(e):
            e.wait_ge(rin, 1)
            e.activation(TMP[:], TMP[:], ACT.Sqrt).then_inc(rdn, 1)

        @p.on("vector")
        def _(e):
            e.wait_ge(wp, 1)
            e.tensor_copy(WL[:], PS[:, 7, 0:128]).then_inc(wq, 1)
            e.tensor_scalar(TMP[:], DIN[:], 1.0, None, ALU.max).then_inc(rin, 1)
            e.wait_ge(rdn, 1)
            link = chain(e, dv)
            link(e.reciprocal(RIN[:], TMP[:]))
            link(e.tensor_scalar(TMP[:], DIN[:], 1.0, None, ALU.min))
            link(e.tensor_tensor(RIN[:], RIN[:], TMP[:], ALU.mult))

        def mm(e, g, n):
            ag, ae = jp(AB[:, 0, :], g), jp(AB[:, 1, :], g)
            for j in range(4):
                c = slice(128 * j, 128 * j + 128)
                e.matmul(PS[0:n, 0, c], ag[:, j, :], WT_[:], start=True, stop=False)
                e.matmul(PS[0:n, 0, c], ae[:, j, :], WRT[:], start=False, stop=True)
                h = HTT[g % 2][:, n * j:n * j + n]
                e.matmul(PS[0:n, 1, c], h, WL[:], start=True, stop=True)
                e.matmul(PS[0:n, 2, c], h, WT_[:], start=True, stop=True)
                i = e.matmul(PS[0:n, 6, j:j + 1], jp(R[64:65, :], g)[:, j, :], ONE[64:65, 0:1], start=True, stop=True)
            return i

        def evac(e, g, n):
            e.activation(P2S[0:n], bank(1, n), ACT.Copy)
            e.wait_ge(mkd, g + 1)
            for j in range(4):
                i = e.activation(T3[0:n, j, :], bank(2, n)[:, j, :], ACT.Copy, scale=NM[g % 2][0:n, j:j + 1])
            return i

        def combine(e, g, n):
            s = g % 2
            for j in range(4):
                i = e.scalar_tensor_tensor(out=Q[0:n, j, :], in0=bank(0, n)[:, j, :], scalar=RD[s][0:n, j:j + 1],
                                           in1=P2S[0:n, j, :], op0=ALU.mult, op1=ALU.add)
            i.then_inc(cc, 1)
            e.wait_ge(cc, 2 * g + 1)
            for j in range(4):
                i = e.scalar_tensor_tensor(out=Q[0:n, j, :], in0=Q[0:n, j, :], scalar=MK[s][0:n, j:j + 1],
                                           in1=T3[0:n, j, :], op0=ALU.mult, op1=ALU.add)
            i.then_inc(cc, 1)
            e.wait_ge(cc, 2 * g + 2)
            return e.scalar_tensor_tensor(out=XT3[g % 3][0:n], in0=Q[0:n], scalar=0.0, in1=XT3[g % 3][0:n],
                                          op0=ALU.max, op1=ALU.add)

        def finish(e, g, n, nr):
            for j in range(4):
                i = e.tensor_scalar(TO[g % 2][0:n, j, :], HO[g % 2][0:n, j, :], RIN[0:n, 4 * g + j:4 * g + j + 1],
                                    None, ALU.mult)
            return i

        def pre(e, g, n):
            s = g % 2
            e.wait_ge(p.sem("pmm"), g + 1)
            e.tensor_copy(DC[s][0:n], PS[0:n, 6, 0:4]).then_inc(p.sem("pa"), 1)
            e.wait_ge(p.sem("pa"), g + 1)
            e.tensor_scalar(MK[s][0:n], DC[s][0:n], 0.0, None, ALU.is_gt).then_inc(p.sem("pb"), 1)
            e.wait_ge(p.sem("pb"), g + 1)
            e.tensor_scalar(NM[s][0:n], MK[s][0:n], -1.0, 1.0, ALU.mult, ALU.add).then_inc(mkd, 1)
            e.wait_ge(mkd, g + 1)
            e.tensor_tensor(DC[s][0:n], DC[s][0:n], NM[s][0:n], ALU.add).then_inc(p.sem("pc"), 1)
            e.wait_ge(p.sem("pc"), g + 1)
            e.reciprocal(RD[s][0:n], DC[s][0:n]).then_inc(p.sem("pd"), 1)
            e.wait_ge(p.sem("pd"), g + 1)
        nodes(p, x1d, t1d, TW, x2d, True, mm, evac, combine, finish, [(h2d, HO, p.sem("q5")), (t2d, TO, None)], (wq, 1), pre=pre)
        p.run()

    KLS = XR[:, 0:NR * 4]
    IDXS = XR[:, NR * 4:NR * 8].bitcast(I32)

    def p_sorted():
        p = Phase()
        T = AB[:, 0, 0:NR * 4]
        load_list(p, "sorted", 1, KLS, [(1, T)])

        @p.on("vector")
        def _(e):
            e.tensor_copy(IDXS, T).then_inc(p.sem("ix"), 1)
            e.wait_ge(p.sem("ix"), 1)
        p.run()

    def gathered(s):
        return GS[:, s, :, :]

    def aggregate(table, idx, width, part, keys, ACC, weight=None, count=False):
        p = Phase()
        ready = gather(p, p.sem("bd"), table[0:NN, :], idx, D)
        edge_pass(p, width, part, keys, gathered, ready, 64, ACC, weight=weight, count=count)

        for k in ("vector", "tensor"):
            @p.on(k)
            def _(e):
                e.wait_ge(p.sem("edone"), 1)
        p.run()

    def p_l2f():
        aggregate(t2d, IDXS, 128, 1, KLS, AB[:, 0, :], count=True)

    def p_l2b():
        aggregate(t3d, IDX[:], 64, 0, KLD[:], AB[:, 1, :])

    def p_out_degrees():
        p = Phase()
        TMP = p.tile([128, NG * 4])
        mm, dg, rt, dv, sc = (p.sem(k) for k in ("mm", "dg", "rt", "dv", "sc"))
        NB = 6
        ld, st = [p.sem(f"ld{i}") for i in range(NB)], [p.sem(f"st{i}") for i in range(NB)]
        HB = [GF[:, 512 * i:512 * i + 512].rearrange("p (j f) -> p j f", j=4) for i in range(NB)]

        @p.on("tensor")
        def _(e):
            for g in range(NG):
                n = grows[g]
                for j in range(4):
                    i = e.matmul(PS[0:n, 6, 4 * g + j:4 * g + j + 1], jp(R[0:1, :], g)[:, j, :], ONE[0:1, 0:1],
                                 start=True, stop=True)
            i.then_inc(mm, 1)

        @p.on("scalar")
        def _(e):
            e.wait_ge(dg, 1)
            e.activation(TMP[:], TMP[:], ACT.Sqrt).then_inc(rt, 1)
            for g in range(NG):
                e.wait_ge(sc, g + 1)
                e.dma_start(rowsl(t3d, g), flat(HB[g % NB], grows[g])).then_inc(st[g % NB], 16)
            for i in range(NB):
                if i < NG:
                    e.wait_ge(st[i], 16 * ((NG - 1 - i) // NB + 1))

        @p.on("sync")
        def _(e):
            for g in range(NG):
                if g >= NB:
                    e.wait_ge(st[g % NB], 16 * (g // NB))
                e.dma_start(flat(HB[g % NB], grows[g]), rowsl(h2d, g)).then_inc(ld[g % NB], 16)

        @p.on("vector")
        def _(e):
            link = chain(e, dv)
            n, c = grows[NG - 1], 4 * (NG - 1)
            e.wait_ge(mm, 1)
            if NG > 1:
                e.tensor_copy(DOUT[:, 0:c], PS[:, 6, 0:c])
            link(e.tensor_copy(DOUT[0:n, c:c + 4], PS[0:n, 6, c:c + 4]))
            e.tensor_scalar(TMP[:], DOUT[:], 1.0, None, ALU.max).then_inc(dg, 1)
            e.wait_ge(rt, 1)
            link(e.reciprocal(ROUT[:], TMP[:]))
            link(e.tensor_scalar(TMP[:], DOUT[:], 1.0, None, ALU.min))
            link(e.tensor_tensor(ROUT[:], ROUT[:], TMP[:], ALU.mult))
            for g in range(NG):
                n = grows[g]
                e.wait_ge(ld[g % NB], 16 * (g // NB + 1))
                for j in range(4):
                    i = e.tensor_scalar(HB[g % NB][0:n, j, :], HB[g % NB][0:n, j, :],
                                        ROUT[0:n, 4 * g + j:4 * g + j + 1], None, ALU.mult)
                i.then_inc(sc, 1)
        p.run()

    def p_l2_nodes():
        p = Phase()
        raw, mats, _, rep, wc, nw = weights(p, [Ws, Wd], [bs, bd_])
        Q, P2S, TY = p.tile([128, 4, D]), p.tile([128, 4, D]), p.tile([1, 1])
        dv, cc = p.sem("dv"), p.sem("cc")

        @p.on("vector")
        def _(e):
            link = chain(e, dv)
            e.wait_ge(wc, nw)
            e.tensor_scalar(mats[0][:], mats[0][:], 0.5, None, ALU.mult)
            e.tensor_scalar(mats[1][:], mats[1][:], 0.5, None, ALU.mult)
            link(e.tensor_tensor(rep[0][:], rep[0][:], rep[1][:], ALU.add))
            link(e.tensor_scalar(rep[0][:], rep[0][:], 0.5, None, ALU.mult))

        def mm(e, g, n):
            for a in range(2):
                for j in range(4):
                    i = e.matmul(PS[0:n, a, 128 * j:128 * j + 128], jp(AB[:, a, :], g)[:, j, :], mats[a][:],
                                 start=True, stop=True)
            return i

        def evac(e, g, n):
            for j in range(4):
                i = e.activation(P2S[0:n, j, :], bank(1, n)[:, j, :], ACT.Copy, scale=RIN[0:n, 4 * g + j:4 * g + j + 1])
            return i

        def combine(e, g, n):
            for j in range(4):
                i = e.scalar_tensor_tensor(out=Q[0:n, j, :], in0=bank(0, n)[:, j, :],
                                           scalar=ROUT[0:n, 4 * g + j:4 * g + j + 1],
                                           in1=P2S[0:n, j, :], op0=ALU.mult, op1=ALU.add)
            i.then_inc(cc, 1)
            e.wait_ge(cc, 2 * g + 1)
            e.tensor_tensor(Q[0:n], Q[0:n], rep[0][0:n].unsqueeze(1).to_broadcast([n, 4, D]), ALU.add).then_inc(cc, 1)
            e.wait_ge(cc, 2 * g + 2)
            return e.tensor_tensor(XT3[g % 3][0:n], Q[0:n], XT3[g % 3][0:n], ALU.add)

        def finish(e, g, n, nr):
            return e.memset(TY[:], 0.0)
        nodes(p, x2d, None, D, x3d, False, mm, evac, combine, finish, [(t4d, HO, p.sem("q5"))], (dv, 2))
        p.run()

    EW = XR[:, 0:NR * 4]

    def p_weights():
        p = Phase()
        ld = p.sem("ld")
        T = AB[:, 1, 0:NCH * BE].rearrange("p (c k) -> p c k", c=NCH)
        nld = [0]

        @p.on("sync")
        def _(e):
            def put(o, i):
                e.dma_start(o, i).then_inc(ld, 16)
                nld[0] += 1
            for ci, (c0, n) in enumerate(chunks):
                nf = min(n, NBF - c0)
                if nf:
                    put(T[0:nf, ci, :], ew[c0 * BE:(c0 + nf) * BE].rearrange("(b k) -> b k", k=BE))
            n = (NR - 1) % 128
            put(T[n:n + 1, NCH - 1, 0:4 * TP], ew[NBF * BE:NE].rearrange("(b k) -> b k", b=1))
            put(T[n:n + 1, NCH - 1, 4 * TP:BE], ew[NBF * BE:NBF * BE + BE - 4 * TP].rearrange("(b k) -> b k", b=1))
        nput = sum(1 for c0, n in chunks if min(n, NBF - c0)) + 2
        turn_rows(p, (ld, 16 * nput), [(T, EW)])
        p.run()

    def p_l3():
        aggregate(t4d, IDX[:], 64, 0, KLD[:], AB[:, 0, :], weight=EW)

    def p_l3_nodes():
        p = Phase()
        raw, mats, _, rep, wc, nw = weights(p, [Wrel, Wroot], [brel, gamma, beta])
        Q, P1S, RC = p.tile([128, 4, D]), p.tile([128, 4, D]), p.tile([128, NG * 4])
        dv, cc, ff = p.sem("dv"), p.sem("cc"), p.sem("ff")

        @p.on("vector")
        def _(e):
            link = chain(e, dv)
            e.wait_ge(wc, nw)
            link(e.tensor_scalar(RC[:], DIN[:], 1.0, None, ALU.max))
            link(e.reciprocal(RC[:], RC[:]))

        def mm(e, g, n):
            for j in range(4):
                e.matmul(PS[0:n, 0, 128 * j:128 * j + 128], jp(AB[:, 0, :], g)[:, j, :], mats[0][:], start=True, stop=True)
            for j in range(4):
                i = e.matmul(PS[0:n, 1, 128 * j:128 * j + 128], HTT[g % 2][:, n * j:n * j + n], mats[1][:],
                             start=True, stop=True)
            return i

        def evac(e, g, n):
            return e.activation(P1S[0:n], bank(1, n), ACT.Copy)

        def combine(e, g, n):
            for j in range(4):
                i = e.scalar_tensor_tensor(out=Q[0:n, j, :], in0=bank(0, n)[:, j, :],
                                           scalar=RC[0:n, 4 * g + j:4 * g + j + 1],
                                           in1=P1S[0:n, j, :], op0=ALU.mult, op1=ALU.add)
            i.then_inc(cc, 1)
            e.wait_ge(cc, 2 * g + 1)
            e.tensor_tensor(Q[0:n], Q[0:n], rep[0][0:n].unsqueeze(1).to_broadcast([n, 4, D]), ALU.add).then_inc(cc, 1)
            e.wait_ge(cc, 2 * g + 2)
            return e.tensor_tensor(SC[g % 2][0:n], Q[0:n], GI3[g % 3][0:n], ALU.add)

        def finish(e, g, n, nr):
            s = g % 2
            Y = SC[s][0:n]
            for j in range(4):
                i = e.tensor_scalar(Y[:, j, :], Y[:, j, :], nr.rs[s][0:n, j:j + 1], nr.nm[s][0:n, j:j + 1],
                                    ALU.mult, ALU.add)
            i.then_inc(nr.f, 1)
            e.wait_ge(nr.f, g + 1)
            e.tensor_tensor(Y, Y, rep[1][0:n].unsqueeze(1).to_broadcast([n, 4, D]), ALU.mult).then_inc(ff, 1)
            e.wait_ge(ff, 2 * g + 1)
            e.tensor_tensor(Y, Y, rep[2][0:n].unsqueeze(1).to_broadcast([n, 4, D]), ALU.add).then_inc(ff, 1)
            e.wait_ge(ff, 2 * g + 2)
            return e.scalar_tensor_tensor(out=TO[s][0:n], in0=Y, scalar=0.0, in1=XT3[g % 3][0:n],
                                          op0=ALU.max, op1=ALU.add)
        SC = nodes(p, x3d, t4d, D, None, True, mm, evac, combine, finish, [(out, TO, None)], (dv, 2), norm="dve")
        p.run()

    for phase in (p_const, p_lists, p_prep, p_l0, p_flag, p_l1, p_l1_nodes, p_sorted, p_l2f, p_out_degrees,
                  p_l2b, p_l2_nodes, p_weights, p_l3, p_l3_nodes):
        phase()


_INS = ["x", "src", "dst", "edge_attr_128", "edge_weight", "L0_gnn_u", "L0_gnn_W1", "L0_gnn_b1", "L0_gnn_W2",
        "L0_gnn_b2", "L1_gnn_w", "L1_gnn_w_r", "L1_gnn_att_w", "L1_gnn_loop_w", "L2_gnn_W_src", "L2_gnn_b_src",
        "L2_gnn_W_dst", "L2_gnn_b_dst", "L3_gnn_W_rel", "L3_gnn_b_rel", "L3_gnn_W_root", "L3_gnn_gamma",
        "L3_gnn_beta"]


def kernel(**inputs):
    import numpy as _np
    import concourse.bacc as _bacc
    from concourse import mybir as _mybir
    from concourse.bass_utils import run_bass_kernel_spmd as _run

    nc = _bacc.Bacc("TRN2", target_bir_lowering=False, num_devices=1, dynamic_dma_scratch_size=8192)
    arrays, args = {}, []
    for name in _INS:
        a = _np.ascontiguousarray(inputs[name])
        arrays[f"in_{name}"] = a
        args.append(nc.dram_tensor(f"in_{name}", a.shape, _mybir.dt.from_np(a.dtype), kind="ExternalInput").ap())
    shape = inputs["x"].shape
    out = nc.dram_tensor("out_0", shape, _mybir.dt.float32, kind="ExternalOutput").ap()
    gnn(nc, *args, out)
    r = _run(nc, [arrays], core_ids=[0])
    return r.results[0]["out_0"]
```

```python
import concourse.bass as bass
from concourse import mybir
from contextlib import ExitStack

F32 = mybir.dt.float32
I32 = mybir.dt.int32
U32 = mybir.dt.uint32
BF16 = mybir.dt.bfloat16
ALU = mybir.AluOpType
ACT = mybir.ActivationFunctionType
AX = mybir.AxisListType.X

D = 128
BE = 512
TP = 80
UN = 6
TW = 132
BIG = float(2 ** 100)
M0 = -1.0e20
EPS = 1e-5


def gnn(nc, x, src, dst, ea, ew, u, W1, b1, W2, b2, w, w_r, att, loop_w, Ws, bs, Wd, bd_,
        Wrel, brel, Wroot, gamma, beta, out):
    NN, NE = x.shape[0], src.shape[0]
    NBF = (NE - 4 * TP) // BE
    NR = NBF + 1
    NW = (NN + 127) // 128
    NG = (NN + 511) // 512
    NP = NG * 512
    assert NE == NBF * BE + 4 * TP and NBF % UN == 0 and NN % 4 == 0 and NW <= 98
    grows = [min(512, NN - 512 * g) // 4 for g in range(NG)]
    chunks = [(c, min(128, NR - c)) for c in range(0, NR, 128)]
    NCH = len(chunks)

    def dram(name, shape, dt=F32):
        return nc.dram_tensor(name, shape, dt, kind="Internal").ap()

    x1d, x2d, x3d, h2d = (dram(n, (NP, D)) for n in ("x1d", "x2d", "x3d", "h2d"))
    t1d = dram("t1d", (NP, TW))
    t2d, t3d, t4d = (dram(n, (NP, D)) for n in ("t2d", "t3d", "t4d"))
    sortd = dram("sortd", (NE, 2), I32)
    rngd = dram("rngd", (2, NR, 2), I32)

    top = ExitStack()

    def sb(name, shape, dt=F32):
        return top.enter_context(nc.sbuf_tensor(name, shape, dt))

    NC = max(NN + 132, 12632)
    AB = sb("AB", [128, 2, NC])
    R = sb("R", [128, NC])
    KLD = sb("KLD", [128, NR * 4])
    IDX = sb("IDX", [128, NR * 4], I32)
    SREL = sb("SREL", [128, NR * 4])
    GS = sb("GS", [128, UN, 4, TW])
    XR = sb("XR", [128, max(UN * BE, 2 * NR * 4)])
    RNG = sb("RNG", [64, 2 * NR + 2], I32)
    ID = sb("ID", [128, 128])
    IDB = sb("IDB", [128, 128], BF16)
    ONE = sb("ONE", [128, 128])
    IO = sb("IO", [128, 128])
    IOB = sb("IOB", [128, 64], BF16)
    DIN = sb("DIN", [128, NG * 4])
    DOUT = sb("DOUT", [128, NG * 4])
    EA = XR[:, 0:UN * BE].rearrange("p (s r f) -> p s r f", s=UN, r=4)
    GF = GS[:].rearrange("p s r f -> p (s r f)")
    PS = top.enter_context(nc.psum_tensor("PS", [128, 8, 512], F32))

    nsem = [0]

    def reg(e, name):
        nsem[0] += 1
        return e.alloc_register(f"{name}{nsem[0]}")

    class Phase:

        def __init__(self):
            self.ctx = ExitStack()
            self.q = {k: [] for k in ("sync", "gpsimd", "vector", "scalar", "tensor")}
            self.s = {}
            self.nt = 0

        def sem(self, name):
            if name not in self.s:
                nsem[0] += 1
                self.s[name] = nc.alloc_semaphore(name=f"{name}_{nsem[0]}")
            return self.s[name]

        def on(self, eng):
            def add(f):
                self.q[eng].append(f)
                return f
            return add

        def tile(self, shape, dt=F32, name="w"):
            self.nt += 1
            nsem[0] += 1
            return self.ctx.enter_context(nc.sbuf_tensor(f"{name}{nsem[0]}", shape, dt))

        def run(self):
            with self.ctx:
                with nc.Block() as blk:
                    place = {"sync": blk.sync, "gpsimd": blk.gpsimd, "vector": blk.vector,
                             "scalar": blk.scalar, "tensor": blk.tensor}
                    for eng, fs in self.q.items():
                        def emit(e, fs=fs):
                            for f in fs:
                                f(e)
                        place[eng](emit)
            nc.clear_and_free_semaphores(list(self.s.values()))
            nc.all_engine_barrier()

    def chain(e, sem):
        n = [0]

        def link(ins):
            n[0] += 1
            ins.then_inc(sem, 1)
            e.wait_ge(sem, n[0])
        return link

    def ranges(e, part, col, n):
        return nc.values_load_multi_w_load_instructions(
            RNG[32 * part:32 * part + 1, bass.ds(col, n)], engines=[e.engine], min_val=0, max_val=NN + 1,
            skip_runtime_bounds_check_because="keys are node numbers")[1]

    def p_const():
        p = Phase()
        z, c = p.sem("z"), p.sem("c")

        @p.on("gpsimd")
        def _(e):
            link = chain(e, z)
            e.iota(IO[:], [[1, 128]], base=0, channel_multiplier=0, allow_small_or_imprecise_dtypes=True)
            e.memset(ONE[:], 1.0)
            link(e.memset(ID[:], 0.0))
            link(e.affine_select(out=ID[:], in_=ID[:], compare_op=ALU.not_equal, fill=1.0, base=0,
                                 pattern=[[-1, 128]], channel_multiplier=1))

        @p.on("vector")
        def _(e):
            e.memset(DIN[:], 0.0)
            e.memset(DOUT[:], 0.0)
            e.memset(RNG[:], 0)
            e.wait_ge(z, 2)
            e.tensor_copy(IDB[:], ID[:])
            e.tensor_copy(IOB[:], IO[:, 0:64]).then_inc(c, 1)
            e.wait_ge(c, 1)
        p.run()

    def turn_rows(p, ready, pairs):
        tr, cp = p.sem("tr"), p.sem("cp")
        jobs = [(f, t, ci, r) for f, t in pairs for ci in range(NCH) for r in range(4)]

        @p.on("tensor")
        def _(e):
            e.wait_ge(*ready)
            for k, (f, t, ci, r) in enumerate(jobs):
                n = chunks[ci][1]
                if k >= 8:
                    e.wait_ge(cp, k - 7)
                v = f[0:n, ci, :].rearrange("b (p r) -> b r p", r=4)[:, r, :]
                e.transpose(PS[:, k % 8, 0:n], v, ID[0:n, 0:n]).then_inc(tr, 1)

        @p.on("vector")
        def _(e):
            for k, (f, t, ci, r) in enumerate(jobs):
                c0, n = chunks[ci]
                e.wait_ge(tr, k + 1)
                o = t.rearrange("p (b r) -> p b r", r=4)[:, c0:c0 + n, r]
                e.tensor_copy(o, PS[:, k % 8, 0:n]).then_inc(cp, 1)
            e.wait_ge(cp, len(jobs))

    def load_list(p, kind, part, keys, full, raw_f=None):
        B = AB[:, 1, :]
        W = BE * (1 if kind == "in" else 2)
        stg = [B[:, i * NCH * W:(i + 1) * NCH * W].bitcast(I32).rearrange("p (c k) -> p c k", c=NCH)
               for i in range(2 if kind == "in" else 1)]
        o = 2 * NCH * BE
        fl = [B[:, o + i * NCH * BE:o + (i + 1) * NCH * BE].rearrange("p (c k) -> p c k", c=NCH) for i in range(3)]
        mn, mx, rg = p.tile([128, NCH]), p.tile([128, NCH]), p.tile([128, NCH, 2], I32)
        ld, st, dv, rs = (p.sem(n) for n in ("ld", "st", "dv", "rs"))
        nld = [0]

        @p.on("sync")
        def _(e):
            def put(o, i):
                e.dma_start(o, i).then_inc(ld, 16)
                nld[0] += 1
            srcs = [(stg[0], dst, 1), (stg[1], src, 1)] if kind == "in" else [(stg[0], sortd.rearrange("e t -> (e t)"), 2)]
            for t, d, m in srcs:
                for ci, (c0, n) in enumerate(chunks):
                    nf = min(n, NBF - c0)
                    if nf:
                        put(t[0:nf, ci, :], d[c0 * BE * m:(c0 + nf) * BE * m].rearrange("(b k) -> b k", k=BE * m))
                n = (NR - 1) % 128
                put(t[n:n + 1, NCH - 1, 0:4 * TP * m], d[NBF * BE * m:NE * m].rearrange("(b k) -> b k", b=1))
                put(t[n:n + 1, NCH - 1, 4 * TP * m:BE * m],
                    d[NBF * BE * m:NBF * BE * m + (BE - 4 * TP) * m].rearrange("(b k) -> b k", b=1))

        @p.on("vector")
        def _(e):
            e.wait_ge(ld, 16 * nld[0])
            if kind == "in":
                a, b = stg[0], stg[1]
            else:
                v = stg[0].rearrange("p c (k t) -> p c k t", t=2)
                b, a = v[:, :, :, 0], v[:, :, :, 1]
            link = chain(e, dv)
            for ci, (c0, n) in enumerate(chunks):
                e.tensor_copy(fl[0][0:n, ci, :], a[0:n, ci, :])
                last = e.tensor_copy(fl[1][0:n, ci, :], b[0:n, ci, :])
            link(last)
            for ci, (c0, n) in enumerate(chunks):
                e.tensor_reduce(mn[0:n, ci:ci + 1], fl[0][0:n, ci, :], AX, ALU.min)
                last = e.tensor_reduce(mx[0:n, ci:ci + 1], fl[0][0:n, ci, :], AX, ALU.max)
            link(last)
            for ci, (c0, n) in enumerate(chunks):
                e.tensor_copy(rg[0:n, ci, 0:1], mn[0:n, ci:ci + 1])
                e.tensor_scalar(rg[0:n, ci, 1:2], mx[0:n, ci:ci + 1], 1.0, None, ALU.add)
                last = e.tensor_scalar(fl[2][0:n, ci, :], fl[0][0:n, ci, :], mn[0:n, ci:ci + 1], None, ALU.subtract)
            link(last)

        @p.on("scalar")
        def _(e):
            e.wait_ge(dv, 3)
            for ci, (c0, n) in enumerate(chunks):
                e.dma_start(rngd[part, c0:c0 + n, :], rg[0:n, ci, :]).then_inc(st, 16)
            e.wait_ge(st, 16 * NCH)
            e.dma_start(RNG[32 * part:32 * part + 1, 0:2 * NR], rngd[part].rearrange("(o r) t -> o (r t)", o=1)).then_inc(rs, 16)
            e.wait_ge(rs, 16)

        turn_rows(p, (dv, 3), [(fl[2], keys)] + [(fl[i], t) for i, t in full])

    B0 = AB[:, 1, :]
    _o = [0]

    def take(n, dt=F32):
        v = B0[:, _o[0]:_o[0] + n]
        _o[0] += n
        return v if dt == F32 else v.bitcast(dt)

    PAY = take(NR * 8, I32).rearrange("p (b t) -> p b t", t=2)
    AW = take(NR * 4)
    POS = take(NR * 4, I32)
    LOW, UPI, ONB = (take(64, BF16) for _ in range(3))
    IOA = take(49, BF16)
    BASE = take(392)
    V3 = take(128)
    OH = [take(196, BF16) for _ in range(2)]
    PR = [take(392) for _ in range(2)]
    LISTEND = _o[0]

    def p_lists():
        p = Phase()
        load_list(p, "in", 0, KLD[:], [(0, AB[:, 0, 0:NR * 4]), (1, AB[:, 0, NR * 4:NR * 8])])
        p.run()

    def p_prep():
        p = Phase()
        dn, oh, mm, g = p.sem("dn"), p.sem("oh"), p.sem("mm"), p.sem("g")
        ff = p.sem("ff")
        DF, SF = AB[:, 0, 0:NR * 4], AB[:, 0, NR * 4:NR * 8]

        @p.on("gpsimd")
        def _(e):
            link = chain(e, g)
            T = AB[:, 0, NR * 8:NR * 8 + 256]
            e.memset(T[:, 128:256], 1.0)
            link(e.memset(T[:, 0:128], 1.0))
            e.affine_select(out=T[:, 0:128], in_=T[:, 0:128], compare_op=ALU.is_gt, fill=0.0, base=0,
                            pattern=[[1, 128]], channel_multiplier=-1)
            link(e.affine_select(out=T[:, 128:256], in_=T[:, 128:256], compare_op=ALU.is_ge, fill=0.0, base=0,
                                 pattern=[[-1, 128]], channel_multiplier=1))

        wr, at3 = p.tile([128, 128]), p.tile([128, 1])
        ld = p.sem("ld")

        @p.on("sync")
        def _(e):
            e.dma_start(wr[:], w_r).then_inc(ld, 16)
            e.dma_start(at3[:], att[2 * D:3 * D].rearrange("(p o) -> p o", o=1)).then_inc(ld, 16)

        TI = AB[:, 0, NR * 8 + 256:NR * 12 + 256].bitcast(I32)

        @p.on("vector")
        def _(e):
            link = chain(e, dn)
            e.tensor_copy(IDX[:], SF)
            e.tensor_copy(PAY[:, :, 0], DF)
            e.tensor_copy(ONB, ONE[:])
            e.tensor_copy(IOA, IO[:, 0:98])
            e.tensor_copy(OH[1], IO[:, 0:1].to_broadcast([128, 392]))
            link(e.tensor_copy(PAY[:, :, 1], SF))
            link(e.tensor_scalar(TI, IDX[:], 7, None, ALU.arith_shift_right))
            e.wait_ge(g, 2)
            e.tensor_copy(LOW, AB[:, 0, NR * 8:NR * 8 + 128])
            e.tensor_copy(UPI, AB[:, 0, NR * 8 + 128:NR * 8 + 256])
            link(e.tensor_copy(AW, TI))
            def ohs(s, c):
                for r in range(4):
                    i = e.tensor_scalar(OH[s][:, 98 * r:98 * r + 98], IOA, AW[:, bass.ds(c + r, 1)], None, ALU.is_equal)
                return i
            k = reg(e, "k")
            e.reg_mov(k, 1)
            with e.Fori(0, NBF // 2) as h:
                for s in range(2):
                    e.wait_ge(mm, e.snap(k))
                    ohs(s, h * 8 + 4 * s).then_inc(oh, 1)
                    e.reg_add(k, k, 1)
            e.wait_ge(mm, NBF + 1)
            ohs(0, 4 * NBF).then_inc(oh, 1)
            e.wait_ge(mm, NBF + 3)
            tot = PR[0].rearrange("p (a r) -> p r a", r=4)
            link(e.tensor_copy(tot, PS[:, 0, 0:392].rearrange("p (r a) -> p r a", r=4)))
            link(e.memset(BASE, 1.0))
            link(e.tensor_tensor_scan(PR[1], BASE, PR[0], 0.0, ALU.mult, ALU.add))
            link(e.tensor_tensor(PR[1], PR[1], PR[0], ALU.subtract))
            e.tensor_copy(V3, PS[:, 1, 0:128])
            link(e.tensor_copy(BASE.rearrange("p (r a) -> p r a", r=4), PR[1].rearrange("p (a r) -> p r a", r=4)))

        @p.on("tensor")
        def _(e):
            e.wait_ge(ld, 32)
            e.matmul(PS[:, 1, 0:128], at3[:, 0:1].to_broadcast([128, 128]), wr[:], start=True, stop=True).then_inc(mm, 1)
            e.wait_ge(dn, 3)
            e.matmul(PS[:, 0, 0:392], ONB, OH[1], start=True, stop=False, skip_group_check=True).then_inc(mm, 1)
            k = reg(e, "kp")
            e.reg_mov(k, 1)
            with e.Fori(0, NBF, 2):
                for s in range(2):
                    e.wait_ge(oh, e.snap(k))
                    e.matmul(PS[:, 0, 0:392], ONB, OH[s], start=False, stop=False, skip_group_check=True).then_inc(mm, 1)
                    e.reg_add(k, k, 1)
            e.wait_ge(oh, NBF + 1)
            e.matmul(PS[:, 0, 0:392], ONB[0:TP, :], OH[0][0:TP, :], start=False, stop=True, skip_group_check=True).then_inc(mm, 1)
        p.run()

    NIT = NBF // UN

    def batches(e, step):
        with e.Fori(0, NIT) as it:
            for s in range(UN):
                step(it * UN + s, s, it, False)
        step(NBF, 0, NIT, True)

    def unit_ranges(e, part):
        held = {}

        def get(b, s, it, last):
            if last:
                return ranges(e, part, 2 * NBF, 2)
            if s == 0:
                held[0] = ranges(e, part, it * (2 * UN), 2 * UN)
            return held[0][2 * s:2 * s + 2]
        return get

    def edge_pass(p, width, part, keys, feats, ready, rstep, ACC, weight=None, count=True, rank=False):
        acc, mmd, oh, bd, dv, kx = (p.sem(n) for n in ("acc", "mmd", "oh", "bd", "dv", "kx"))
        SEL = [p.tile([128, 4, width]) for _ in range(2)]
        KX, TY = p.tile([128, 4]), p.tile([1, 1])
        if rank:
            ohr, low, rd, pos, sr = (p.sem(n) for n in ("ohr", "low", "rd", "pos", "sr"))
            PF = [p.tile([128, 4]) for _ in range(2)]
            SF = [p.tile([128, 4]) for _ in range(2)]
            JK = p.tile([128, 4, 128])

        def sel(e, s, kl, b):
            o = SEL[s % 2]
            if weight is None:
                return e.tensor_tensor(o[:], IO[:, 0:width].unsqueeze(1).to_broadcast([128, 4, width]),
                                       kl.unsqueeze(2).to_broadcast([128, 4, width]), ALU.is_equal)
            for r in range(4):
                i = e.tensor_scalar(o[:, r, :], IO[:, 0:width], kl[:, r:r + 1],
                                    weight[:, bass.ds(b * 4 + r, 1)], ALU.is_equal, ALU.mult)
            return i

        @p.on("vector")
        def _(e):
            link = chain(e, dv)
            e.memset(R[0:1, :], 0.0)
            e.memset(ACC, 0.0)
            if rank:
                e.memset(SF[0][:], 0.0)
            link(e.memset(SEL[1][:], 0.0))
            nu, na, nk, wp = (reg(e, x_) for x_ in ("nu", "na", "nk", "wp"))
            e.reg_mov(nu, 1)
            e.reg_mov(na, 1)
            e.reg_mov(nk, 1)
            e.nop().then_inc(kx, 1)
            e.reg_mov(wp, 0)
            e.nop().then_inc(acc, 1)
            get = unit_ranges(e, part)

            def linked(ins):
                ins.then_inc(kx, 1)
                e.reg_add(nk, nk, 1)

            def accumulate(q, wv, ends=True):
                n_mm, n_acc = e.snap(nu), e.snap(na)
                e.wait_ge(mmd, n_mm)
                e.wait_ge(acc, n_acc)
                if count:
                    i = e.tensor_tensor(R[0:1, bass.ds(wv, width)], R[0:1, bass.ds(wv, width)],
                                        PS[0:1, 2 + q, 0:width], ALU.add)
                elif ends:
                    i = e.memset(TY[:], 0.0)
                if ends:
                    i.then_inc(bd, 1)
                i = e.tensor_tensor(ACC[:, bass.ds(wv, width)], ACC[:, bass.ds(wv, width)],
                                    PS[:, q, 0:width], ALU.add).then_inc(acc, 1)
                e.reg_add(na, na, 1)
                return i

            def step(b, s, it, last):
                lo, hi = get(b, s, it, last)
                kl = keys[:, bass.ds(b * 4, 4)]
                with e.If(lo + width < hi):
                    e.wait_ge(kx, e.snap(nk))
                    linked(e.tensor_scalar(KX[:], kl, float(width), None, ALU.subtract))
                    with e.Fori(lo + width, hi, width) as wv:
                        e.wait_ge(kx, e.snap(nk))
                        sel(e, s, KX[:], b).then_inc(oh, 1)
                        e.reg_add(nu, nu, 1)
                        accumulate(s % 2, wv, False)
                        linked(e.tensor_scalar(KX[:], KX[:], float(width), None, ALU.subtract))
                e.end_ifs()
                sel(e, s, kl, b).then_inc(oh, 1)
                if rank:
                    for r in range(4):
                        i = e.tensor_scalar(OH[s % 2][:, 98 * r:98 * r + 98], IOA, AW[:, bass.ds(b * 4 + r, 1)],
                                            None, ALU.is_equal)
                    i.then_inc(ohr, 1)
                accumulate((s + 1) % 2, e.snap(wp, min_val=0, max_val=NN + 1))
                e.reg_add(nu, nu, 1)
                e.reg_mov(wp, lo)
                if rank:
                    e.wait_ge(ready[s], it * rstep + rstep)
                    m = TP if last else 128
                    for r in range(4):
                        i = e.tensor_tensor_reduce(JK[0:m, r, :], feats(s)[0:m, r, 0:D], V3[0:m, :], 1.0, 0.0,
                                                   ALU.mult, ALU.add, SF[s % 2][0:m, r:r + 1])
                    i.then_inc(sr, 1)
                    e.wait_ge(low, b + 1)
                    e.tensor_tensor(PR[s % 2], PS[:, 4, 0:392], OH[s % 2], ALU.mult).then_inc(rd, 1)
                    e.wait_ge(sr, b + 1)
                    e.tensor_copy(SREL[:, bass.ds(b * 4, 4)], SF[s % 2][:])
                    e.wait_ge(rd, b * 3 + 1)
                    e.tensor_reduce(PF[s % 2][:], PR[s % 2].rearrange("p (r a) -> p r a", r=4), AX, ALU.add).then_inc(rd, 1)
                    e.wait_ge(rd, b * 3 + 2)
                    e.tensor_copy(POS[:, bass.ds(b * 4, 4)], PF[s % 2][:]).then_inc(rd, 1)
            batches(e, step)
            accumulate(0, e.snap(wp, min_val=0, max_val=NN + 1))
            n_acc = e.snap(na)
            e.wait_ge(acc, n_acc)
            e.memset(TY[:], 0.0).then_inc(p.sem("edone"), 1)

        @p.on("tensor")
        def _(e):
            e.wait_ge(dv, 1)
            ku = reg(e, "ku")
            e.reg_mov(ku, 1)
            get = unit_ranges(e, part)
            if count:
                e.matmul(PS[0:1, 3, 0:width], ONE[:, 0:1], SEL[1][:, 0, :], start=True, stop=True)
            e.matmul(PS[:, 1, 0:width], ONE[:], SEL[1][:, 0, :], start=True, stop=True).then_inc(mmd, 1)
            if rank:
                e.matmul(PS[:, 4, 0:392], ID[:], BASE, start=True, stop=False, skip_group_check=True)

            def unit(s, m):
                k = e.snap(ku)
                e.wait_ge(oh, k)
                e.wait_ge(acc, k)
                if count:
                    for r in range(4):
                        e.matmul(PS[0:1, 2 + s % 2, 0:width], ONE[0:m, 0:1], SEL[s % 2][0:m, r, :],
                                 start=(r == 0), stop=(r == 3))
                for r in range(4):
                    i = e.matmul(PS[:, s % 2, 0:width], feats(s)[0:m, r, 0:D], SEL[s % 2][0:m, r, :],
                                 start=(r == 0), stop=(r == 3))
                i.then_inc(mmd, 1)
                e.reg_add(ku, ku, 1)

            def step(b, s, it, last):
                m = TP if last else 128
                lo, hi = get(b, s, it, last)
                e.wait_ge(ready[s], it * rstep + rstep)
                with e.If(lo + width < hi):
                    with e.Fori(lo + width, hi, width):
                        unit(s, m)
                e.end_ifs()
                if rank:
                    e.wait_ge(ohr, b + 1)
                    e.matmul(PS[:, 4, 0:392], LOW[0:m, :], OH[s % 2][0:m, :], start=False, stop=False,
                             skip_group_check=True).then_inc(low, 1)
                unit(s, m)
                if rank and not last:
                    e.wait_ge(rd, b * 3 + 1)
                    e.matmul(PS[:, 4, 0:392], UPI, OH[s % 2], start=False, stop=False, skip_group_check=True)
            batches(e, step)
        return bd

    def load_ea(p, bd):
        ready = [p.sem(f"ea{s}") for s in range(UN)]

        @p.on("sync")
        def _(e):
            v = ea[0:NBF * BE, :].rearrange("(b p r) f -> b p (r f)", p=128, r=4)
            t = ea[NBF * BE:NE, :].rearrange("(p r) f -> p (r f)", r=4)

            def one(b, s):
                e.dma_start(XR[:, s * BE:(s + 1) * BE], v[bass.ds(b, 1)].rearrange("b p k -> (b p) k")).then_inc(ready[s], 16)
            for s in range(UN):
                one(s, s)
            if NIT > 1:
                with e.Fori(1, NIT) as it:
                    for s in range(UN):
                        e.wait_ge(bd, (it - 1) * UN + (s + 2))
                        one(it * UN + s, s)
            e.wait_ge(bd, (NIT - 1) * UN + 2)
            e.dma_start(XR[0:TP, 0:BE], t).then_inc(ready[0], 16)
            for s in range(UN):
                e.wait_ge(ready[s], 16 * (NIT + (s == 0)))
        return ready

    def gather(p, bd, table, idx, wide):
        ready = [p.sem(f"g{s}") for s in range(UN)]

        @p.on("gpsimd")
        def _(e):
            for b in range(NR):
                s = b % UN
                m = TP if b == NBF else 128
                if b >= UN:
                    e.wait_ge(bd, b - UN + 2)
                for r in range(4):
                    c = 4 * b + r
                    e.indirect_dma_start(GS[0:m, s, r, 0:wide], None, table,
                                         bass.IndirectOffsetOnAxis(ap=idx[0:m, c:c + 1].bitcast(U32), axis=0)
                                         ).then_inc(ready[s], 16)
            for s in range(UN):
                e.wait_ge(ready[s], 64 * (NIT + (s == 0)))
        return ready

    def p_l0():
        p = Phase()
        ready = load_ea(p, p.sem("bd"))
        edge_pass(p, 64, 0, KLD[:], lambda s: EA[:, s], ready, 16, AB[:, 0, :], rank=True)
        rd = p.sem("rd")
        sc = [p.sem(f"sc{i}") for i in range(4)]

        @p.on("gpsimd")
        def _(e):
            for b in range(NR):
                m = TP if b == NBF else 128
                e.wait_ge(rd, 3 * b + 3)
                for r in range(4):
                    c = 4 * b + r
                    e.indirect_dma_start(sortd, bass.IndirectOffsetOnAxis(ap=POS[0:m, c:c + 1].bitcast(U32), axis=0),
                                         PAY[0:m, c, :], None).then_inc(sc[r], 16)
            for r in range(4):
                e.wait_ge(sc[r], 16 * NR)
        l0_nodes(p)
        p.run()

    def rowsl(ap, g):
        n = grows[g]
        return ap[512 * g:512 * g + 4 * n, :].rearrange("(p j) f -> p (j f)", j=4)

    def jp(ap, g):
        return ap[:, 512 * g:512 * g + 4 * grows[g]].rearrange("f (p j) -> f j p", j=4)

    class Norm:

        def __init__(self, p, tag):
            self.p, self.t = p, tag
            self.st = [p.tile([128, 4, 6]) for _ in range(2)]
            self.mv = [p.tile([128, 4, 2]) for _ in range(2)]
            self.sd = [p.tile([128, 4]) for _ in range(2)]
            self.rs = [p.tile([128, 4]) for _ in range(2)]
            self.nm = [p.tile([128, 4]) for _ in range(2)]
            self.a, self.b, self.c, self.d, self.e_, self.f = (p.sem(f"{tag}{i}") for i in range(6))

        def moments(self, e, xt, g):
            n, s = grows[g], g % 2
            for j in range(4):
                i = e.bn_stats(self.st[s][0:n, j, :], xt[0:n, j, :])
            i.then_inc(self.a, 1)
            e.wait_ge(self.a, g + 1)
            if g >= 2:
                e.wait_ge(self.f, g - 1)
            for j in range(4):
                i = e.bn_aggr(self.mv[s][0:n, j, :], self.st[s][0:n, j, :])
            i.then_inc(self.b, 1)
            e.wait_ge(self.b, g + 1)
            e.tensor_scalar(self.sd[s][0:n, :], self.mv[s][0:n, :, 1], EPS, None, ALU.add).then_inc(self.c, 1)

        def root(self, e, g):
            n, s = grows[g], g % 2
            e.wait_ge(self.c, g + 1)
            e.activation(self.sd[s][0:n, :], self.sd[s][0:n, :], ACT.Sqrt).then_inc(self.d, 1)

        def scale(self, e, g):
            n, s = grows[g], g % 2
            e.wait_ge(self.d, g + 1)
            e.reciprocal(self.rs[s][0:n, :], self.sd[s][0:n, :]).then_inc(self.e_, 1)
            e.wait_ge(self.e_, 2 * g + 1)
            e.scalar_tensor_tensor(out=self.nm[s][0:n, :], in0=self.mv[s][0:n, :, 0], scalar=-1.0,
                                   in1=self.rs[s][0:n, :], op0=ALU.mult, op1=ALU.mult).then_inc(self.e_, 1)

        def apply(self, e, out, xt, g):
            n, s = grows[g], g % 2
            e.wait_ge(self.e_, 2 * g + 2)
            for j in range(4):
                i = e.activation(out[0:n, j, 0:D], xt[0:n, j, :], ACT.Relu, bias=self.nm[s][0:n, j:j + 1],
                                 scale=self.rs[s][0:n, j:j + 1])
            i.then_inc(self.f, 1)

    def l0_nodes(p):
        o = [0]

        def at(region, off, n):
            return region[:, off:off + n]
        XT = [at(XR, 1024 + 512 * i, 512).rearrange("p (j f) -> p j f", j=4) for i in range(2)]
        XT.append(p.tile([128, 4, D]))
        H0 = [at(XR, 2048 + 512 * i, 512).rearrange("p (j f) -> p j f", j=4) for i in range(2)]
        HID = [at(GF, 512 * m, 512) if m < 6 else at(XR, 512 * (m - 6), 512) for m in range(8)]
        W1S = B0[:, LISTEND:LISTEND + 2048].rearrange("p (k h) -> p k h", k=2)
        W2S = B0[:, LISTEND + 2048:LISTEND + 3072].rearrange("p (m f) -> p m f", m=8)
        H0T = [B0[:, LISTEND + 3072 + 512 * i:LISTEND + 3584 + 512 * i] for i in range(2)]
        assert LISTEND + 4096 <= NC and NR * 4 >= 2 * 4 * TW or NBF < 300
        HT = [p.tile([128, 4, TW]) if NBF < 300 else AW[:, 528 * i:528 * i + 528].rearrange("p (j f) -> p j f", j=4)
              for i in range(2)]
        H1T = [B0[:, LISTEND - 784:LISTEND - 272]]
        UT, B1, B1E, AT, V12, B2 = (p.tile([16, 1]), p.tile([128, 8]), p.tile([128, 8]),
                                    p.tile([128, 2]), p.tile([128, 2]), p.tile([1, 128]))
        WW = p.tile([128, 128])
        W1U = XR[0:16, 2048:3072]
        ed, wl = p.sem("edone"), p.sem("wl")
        xl = [p.sem(f"xl{i}") for i in range(3)]
        xs, hs = [p.sem(f"xs{i}") for i in range(3)], [p.sem(f"hs{i}") for i in range(2)]
        n0, n1 = Norm(p, "n"), Norm(p, "m")
        t0, c0, ph, hd, py, pb = (p.sem(k) for k in ("t0", "c0", "ph", "hd", "py", "pb"))
        t1, c1, t2, c2, pre, prd = (p.sem(k) for k in ("t1", "c1", "t2", "c2", "pre", "prd"))

        @p.on("sync")
        def _(e):
            for t, d in ((UT[:], u.rearrange("o k -> k o")),
                         (B1[:], b1.rearrange("(m p) -> p m", p=128)), (WW[:], w),
                         (AT[:], att[0:256].rearrange("(k p) -> p k", p=128)), (B2[:], b2.rearrange("(o f) -> o f", o=1)),
                         (W1S, W1[0:256, :].rearrange("(k p) h -> p k h", p=128)),
                         (W2S, W2.rearrange("(m p) f -> p m f", p=128))):
                e.dma_start(t, d, allow_slow_non_contiguous=True).then_inc(wl, 16)
            e.wait_ge(ed, 1)
            e.dma_start(W1U, W1[256:272, :]).then_inc(wl, 16)
            def load(g):
                n = grows[g]
                e.dma_start(XT[g % 3][0:n].rearrange("p j f -> p (j f)"), rowsl(x, g)).then_inc(xl[g % 3], 16)
            for g in range(min(3, NG)):
                load(g)
            for g in range(NG):
                store(e, g)
                if g + 3 < NG:
                    e.wait_ge(n1.f, g + 1)
                    e.wait_ge(xs[g % 3], 16 * (g // 3 + 1))
                    load(g + 3)
            for i in range(3):
                e.wait_ge(xs[i], 16 * ((NG + 2 - i) // 3))
            for i in range(2):
                e.wait_ge(hs[i], 16 * ((NG + 1 - i) // 2))

        def store(e, g):
            n = grows[g]
            e.wait_ge(pb, g + 1)
            e.dma_start(rowsl(x1d, g), XT[g % 3][0:n].rearrange("p j f -> p (j f)")).then_inc(xs[g % 3], 16)
            e.wait_ge(c2, g + 1)
            e.dma_start(rowsl(t1d, g), HT[g % 2][0:n].rearrange("p j f -> p (j f)")).then_inc(hs[g % 2], 16)

        @p.on("tensor")
        def _(e):
            e.wait_ge(wl, 16 * 8)
            e.wait_ge(ed, 1)
            for m in range(8):
                e.matmul(PS[:, 6, m:m + 1], W1U[:, 128 * m:128 * m + 128], UT[:], start=True, stop=True)
            e.matmul(PS[:, 6, 8:9], WW[:], AT[:, 0:1], start=True, stop=True)
            e.matmul(PS[:, 6, 9:10], WW[:], AT[:, 1:2], start=True, stop=True).then_inc(pre, 1)

            def turn0(g):
                n = grows[g]
                e.wait_ge(n0.f, g + 1)
                if g:
                    e.wait_ge(c0, g)
                for j in range(4):
                    i = e.transpose(PS[:, 3, n * j:n * j + n], H0[g % 2][0:n, j, :], ID[0:n, 0:n])
                i.then_inc(t0, 1)

            def mlp(g):
                n = grows[g]
                e.wait_ge(c0, g + 1)
                if g == 0:
                    e.wait_ge(prd, 1)
                for m in range(8):
                    k = 8 * g + m
                    if k >= 2:
                        e.wait_ge(hd, k - 1)
                    e.matmul(PS[:, m % 2, 0:4 * n].rearrange("h (j p) -> h j p", j=4), W1S[:, 0, 128 * m:128 * m + 128],
                             jp(AB[:, 0, :], g), start=True, stop=False)
                    e.matmul(PS[:, m % 2, 0:4 * n], W1S[:, 1, 128 * m:128 * m + 128], H0T[g % 2][:, 0:4 * n],
                             start=False, stop=True).then_inc(ph, 1)
                if g:
                    e.wait_ge(pb, g)
                for j in range(4):
                    for m in range(8):
                        if j == 0:
                            e.wait_ge(hd, 8 * g + m + 1)
                        e.matmul(PS[0:n, 2, 128 * j:128 * j + 128], HID[m][:, n * j:n * j + n], W2S[:, m, :],
                                 start=(m == 0), stop=False)
                    i = e.matmul(PS[0:n, 2, 128 * j:128 * j + 128], ONE[0:1, 0:n], B2[:], start=False, stop=True)
                i.then_inc(py, 1)

            def turn1(g):
                n = grows[g]
                e.wait_ge(n1.f, g + 1)
                if g:
                    e.wait_ge(c1, g)
                for j in range(4):
                    i = e.transpose(PS[:, 5, n * j:n * j + n], HT[g % 2][0:n, j, 0:D], ID[0:n, 0:n])
                i.then_inc(t1, 1)
                e.wait_ge(c1, g + 1)
                if g:
                    e.wait_ge(c2, g)
                for j in range(4):
                    e.matmul(PS[0:n, 6, j:j + 1], H1T[0][:, n * j:n * j + n], V12[:, 0:1], start=True, stop=True)
                    e.matmul(PS[0:n, 6, 4 + j:5 + j], jp(R[0:1, :], g)[:, j, :], ONE[0:1, 0:1], start=True, stop=True)
                e.matmul(PS[0:1, 7, 0:4 * n], V12[:, 1:2], H1T[0][:, 0:4 * n], start=True, stop=True).then_inc(t2, 1)
            turn0(0)
            for g in range(NG):
                if g + 1 < NG:
                    turn0(g + 1)
                mlp(g)
                if g:
                    turn1(g - 1)
            turn1(NG - 1)

        @p.on("scalar")
        def _(e):
            def root0(g):
                n0.root(e, g)

            def app0(g):
                if g >= 2:
                    e.wait_ge(t0, g - 1)
                n0.apply(e, H0[g % 2], XT[g % 3], g)

            def hid(g):
                n = grows[g]
                if g == 0:
                    e.wait_ge(prd, 1)
                for m in range(8):
                    e.wait_ge(ph, 8 * g + m + 1)
                    e.activation(HID[m][:, 0:4 * n], PS[:, m % 2, 0:4 * n], ACT.Relu, bias=B1E[:, m:m + 1]).then_inc(hd, 1)

            def app1(g):
                if g >= 2:
                    e.wait_ge(hs[g % 2], 16 * (g // 2))
                n1.apply(e, HT[g % 2], XT[g % 3], g)
            root0(0)
            e.wait_ge(pre, 1)
            app0(0)
            for g in range(NG):
                if g:
                    n1.root(e, g - 1)
                if g + 1 < NG:
                    root0(g + 1)
                    app0(g + 1)
                hid(g)
                if g:
                    app1(g - 1)
            n1.root(e, NG - 1)
            app1(NG - 1)

        @p.on("vector")
        def _(e):
            def first(g):
                e.wait_ge(xl[g % 3], 16 * (g // 3 + 1))
                n0.moments(e, XT[g % 3], g)
                n0.scale(e, g)

            def copy0(g):
                n = grows[g]
                e.wait_ge(t0, g + 1)
                e.tensor_copy(H0T[g % 2][:, 0:4 * n], PS[:, 3, 0:4 * n]).then_inc(c0, 1)

            def post(g):
                n = grows[g]
                e.wait_ge(py, g + 1)
                e.wait_ge(n0.f, g + 1)
                e.tensor_tensor(XT[g % 3][0:n], XT[g % 3][0:n], PS[0:n, 2, :].rearrange("p (j f) -> p j f", j=4),
                                ALU.add).then_inc(pb, 1)
                e.wait_ge(pb, g + 1)
                n1.moments(e, XT[g % 3], g)

            def tail(g):
                n = grows[g]
                e.wait_ge(t1, g + 1)
                e.tensor_copy(H1T[0][:, 0:4 * n], PS[:, 5, 0:4 * n]).then_inc(c1, 1)
                e.wait_ge(t2, g + 1)
                e.tensor_copy(HT[g % 2][0:n, :, D], PS[0:n, 6, 0:4])
                e.tensor_copy(DIN[0:n, 4 * g:4 * g + 4], PS[0:n, 6, 4:8])
                e.tensor_copy(jp(R[0:1, :], g), PS[0:1, 7, 0:4 * n].rearrange("o (j p) -> o j p", j=4)).then_inc(c2, 1)
            e.wait_ge(ed, 1)
            e.memset(HT[0][:, :, D:TW], 0.0)
            e.memset(HT[1][:, :, D:TW], 0.0)
            e.wait_ge(pre, 1)
            e.tensor_copy(V12[:], PS[:, 6, 8:10])
            e.tensor_tensor(B1E[:], B1[:], PS[:, 6, 0:8], ALU.add).then_inc(prd, 1)
            first(0)
            copy0(0)
            for g in range(NG):
                if g:
                    n1.scale(e, g - 1)
                if g + 1 < NG:
                    first(g + 1)
                    copy0(g + 1)
                if g:
                    tail(g - 1)
                post(g)
            n1.scale(e, NG - 1)
            tail(NG - 1)
            e.wait_ge(c2, NG)

    FLAG = sb("FLAG", [1, 2], I32)
    FT = AB[0:1, 0, 0:NR]
    ONB3 = sb("ONB3", [3, 128], BF16)
    sdf = dram("sdf", (NC,))
    sdd = dram("sdd", (3, NC), BF16)

    def p_flag():
        p = Phase()
        c = p.sem("c")

        @p.on("vector")
        def _(e):
            link = chain(e, c)
            v = RNG[0:1, 0:2 * NR].rearrange("o (b t) -> o b t", t=2)
            link(e.tensor_tensor(FT, v[:, :, 1], v[:, :, 0], ALU.subtract))
            e.tensor_copy(FLAG[:, 1:2], FT[:, 0:1])
            link(e.tensor_reduce(FLAG[:, 0:1], FT, AX, ALU.max))
            e.wait_ge(ld, 32)
            link(e.tensor_copy(Q[0][:], T[:]))
            link(e.tensor_tensor(T[:], T[:], Q[0][:], ALU.subtract))
            link(e.tensor_copy(Q[1][:], T[:]))
            link(e.tensor_tensor(T[:], T[:], Q[1][:], ALU.subtract))
            e.tensor_copy(ONB3[:], ONE[0:3, :])
            e.tensor_copy(Q[2][:], T[:]).then_inc(pr, 1)
        NK = NC // 8
        T, Q = p.tile([8, NK]), [p.tile([8, NK], BF16) for _ in range(3)]
        ld, pr = p.sem("ld"), p.sem("pr")

        @p.on("sync")
        def _(e):
            e.dma_start(sdf.rearrange("(o f) -> o f", o=1), R[0:1, :]).then_inc(ld, 16)
            e.wait_ge(ld, 16)
            e.dma_start(T[:], sdf.rearrange("(p f) -> p f", p=8)).then_inc(ld, 16)
            e.wait_ge(pr, 1)
            for i in range(3):
                e.dma_start(sdd[i].rearrange("(p f) -> p f", p=8), Q[i][:]).then_inc(ld, 16)
            e.wait_ge(ld, 80)
        p.run()

    def p_l1():
        p = Phase()
        bd = p.sem("bd")
        fr, fz, s7, pg = (p.sem(k) for k in ("fr", "fz", "s7", "pg"))
        ear = load_ea(p, fr)
        gr = gather(p, fr, t1d[0:NN, :], IDX[:], TW)
        SW = [p.tile([128, 48]) for _ in range(2)]
        SDT = [p.tile([3, 48], BF16) for _ in range(3)]
        sdl, sdg = [p.sem(f"sd{i}") for i in range(3)], p.sem("sdg")
        s1, s2, s2a, s3, s4, s4a, s4b, s5, s6a, zz = (p.sem(k) for k in (
            "s1", "s2", "s2a", "s3", "s4", "s4a", "s4b", "s5", "s6a", "zz"))
        pu, pt, pr, pbc, pm = (p.sem(k) for k in ("pu", "pt", "pr", "pbc", "pm"))
        au, ac, acs, aw, kx = (p.sem(k) for k in ("au", "ac", "acs", "aw", "kx"))
        WD = 48
        NQ = [p.tile([128, 4, WD], BF16) for _ in range(2)]
        ZC = [p.tile([128, 4]) for _ in range(2)]
        U1 = [p.tile([128, 4, WD]) for _ in range(2)]
        LL = [p.tile([128, 4, WD]) for _ in range(6)]
        LM = [p.tile([128, 128]) for _ in range(2)]
        ZM = [p.tile([128, 1]) for _ in range(2)]
        MC = [p.tile([33, 2 * WD]) for _ in range(2)]
        DM = [p.tile([33, WD]) for _ in range(2)]
        CS = [p.tile([128, WD]) for _ in range(3)]
        T6 = p.tile([128, 2, WD])
        T6R = p.tile([65, WD])
        KX, TY = p.tile([128, 4]), p.tile([1, 1])
        M = R[32:33, :]
        DEN = R[64:65, :]

        def uv(i):
            return PS[:, i, 0:4 * WD].rearrange("p (r n) -> p r n", r=4)

        def sd_load(e, j, lo):
            e.dma_start(SDT[j][:], sdd[:, bass.ds(lo, WD)]).then_inc(sdl[j], 16)

        def d1(e, i, s, kl, b):
            e.tensor_tensor(ZC[i][:], GS[:, s, :, D], SREL[:, bass.ds(b * 4, 4)], ALU.add)
            for r in range(4):
                n = e.tensor_scalar(NQ[i][:, r, :], IOB[:, 0:WD], kl[:, r:r + 1], -BIG, ALU.not_equal, ALU.mult)
            n.then_inc(s1, 1)

        def t1_(e, i, j):
            u4 = uv(i)
            e.matmul(u4, IDB[:], NQ[i][:], start=True, stop=False)
            e.matmul(u4, ONB3[:], SDT[j][:].unsqueeze(1).to_broadcast([3, 4, WD]), start=False, stop=True
                     ).then_inc(pu, 1)

        def a1(e, i):
            for r in range(4):
                n = e.activation(U1[i][:, r, :], uv(i)[:, r, :], ACT.Identity, bias=ZC[i][:, r:r + 1])
            n.then_inc(au, 1)

        def d2(e, i, l, n):
            e.scalar_tensor_tensor(out=LL[l][:], in0=U1[i][:], scalar=0.01, in1=U1[i][:], op0=ALU.mult, op1=ALU.max
                                   ).then_inc(s2a, 1)
            e.wait_ge(s2a, n)
            e.tensor_reduce(LM[i][:, 0:WD], LL[l][:].rearrange("p r n -> p n r"), AX, ALU.max).then_inc(s2, 1)

        def t2_(e, i, m):
            e.transpose(PS[:, 2, 0:m], LM[i][0:m, :], ID[0:m, 0:m]).then_inc(pt, 1)

        def d3(e, i, m):
            e.tensor_reduce(ZM[i][:], PS[:, 2, 0:m], AX, ALU.max).then_inc(s3, 1)

        def t3_(e, i):
            e.matmul(PS[0:1, 6, 0:WD], ZM[i][:], ID[:, 0:WD], start=True, stop=True).then_inc(pr, 1)

        def d4(e, i, w_, n):
            mn = MC[i][32:33, 0:WD]
            e.tensor_tensor(mn, M[:, bass.ds(w_, WD)], PS[0:1, 6, 0:WD], ALU.max).then_inc(s4a, 1)
            e.wait_ge(s4a, n)
            e.tensor_tensor(DM[i][32:33, :], M[:, bass.ds(w_, WD)], mn, ALU.subtract).then_inc(s4b, 1)
            e.wait_ge(s4b, n)
            e.tensor_scalar(M[:, bass.ds(w_, WD)], mn, 1.0, None, ALU.mult).then_inc(s4, 1)

        def a2(e, i):
            e.activation(MC[i][32:33, WD:2 * WD], DM[i][32:33, :], ACT.Exp).then_inc(ac, 1)

        def t4_(e, i):
            e.matmul(PS[:, 3 + 4 * i, 0:2 * WD], ONE[32:33, :], MC[i][32:33, :], start=True, stop=True).then_inc(pbc, 1)

        def a3(e, i, j):
            e.activation(CS[j][:], PS[:, 3 + 4 * i, WD:2 * WD], ACT.Copy).then_inc(acs, 1)

        def d5(e, i, l):
            e.tensor_tensor(LL[l][:], LL[l][:], PS[:, 3 + 4 * i, 0:WD].unsqueeze(1).to_broadcast([128, 4, WD]),
                            ALU.subtract).then_inc(s5, 1)

        def a4(e, l, more=None):
            e.activation(LL[l][:], LL[l][:], ACT.Exp).then_inc(aw, 1)
            if more:
                e.activation(MC[1][32:33, 0:1], MC[0][32:33, 0:1], ACT.Copy).then_inc(more, 1)

        def t5g(e, i, l, s, m):
            for r in range(4):
                n = e.matmul(PS[:, 4 + i, 0:WD], GS[0:m, s, r, 0:D], LL[l][0:m, r, :], start=(r == 0), stop=(r == 3))
            n.then_inc(pg, 1)

        def t5e(e, i, l, s, m, free):
            for r in range(4):
                n = e.matmul(PS[:, 4 + i, WD:2 * WD], EA[0:m, s, r, :], LL[l][0:m, r, :], start=(r == 0), stop=(r == 3))
            n.then_inc(free, 1)
            e.matmul(PS[0:1, 4 + i, 2 * WD:3 * WD], ONE[0:m, 0:1], SW[i][0:m, :], start=True, stop=True).then_inc(pm, 1)

        def d7(e, i, l):
            e.tensor_reduce(SW[i][:], LL[l][:].rearrange("p r n -> p n r"), AX, ALU.add).then_inc(s7, 1)

        def d6(e, i, j, w_, n, done):
            cur = AB[:, :, bass.ds(w_, WD)]
            dn = DEN[:, bass.ds(w_, WD)]
            e.tensor_tensor(T6R[64:65, :], dn, CS[j][64:65, :], ALU.mult)
            e.tensor_tensor(T6[:], cur, CS[j][:].unsqueeze(1).to_broadcast([128, 2, WD]), ALU.mult).then_inc(s6a, 1)
            e.wait_ge(s6a, n)
            e.tensor_tensor(dn, T6R[64:65, :], PS[0:1, 4 + i, 2 * WD:3 * WD], ALU.add)
            e.tensor_tensor(cur, T6[:], PS[:, 4 + i, 0:2 * WD].rearrange("p (a n) -> p a n", a=2), ALU.add
                            ).then_inc(done, 1)

        def fast(e, ops, begin=None, end=None):
            def at(k, s, it):
                if begin:
                    begin(k, s, it)
                for op, lag in ops:
                    b = k - lag
                    if isinstance(b, int) and not 0 <= b <= NBF:
                        continue
                    r = b // UN if isinstance(b, int) else it + (s - lag) // UN
                    op(b, (s - lag) % UN, r, s)
                if end:
                    end(k, s)
            for k in range(-1, UN):
                at(k, k % UN, 0)
            if NIT > 1:
                with e.Fori(1, NIT) as it:
                    for s in range(UN):
                        at(it * UN + s, s, it)
            for k in range(NBF, NBF + 4):
                at(k, k % UN, NIT)

        def need(e, sem, b, back=0, more=0):
            n = b + 1 - back
            if not isinstance(n, int) or n > 0:
                e.wait_ge(sem, n + more)

        def rows(k):
            return TP if isinstance(k, int) and k == NBF else 128

        def general(e, unit, first=None, after=None):
            n = reg(e, "units")
            e.reg_mov(n, 1)
            get = unit_ranges(e, 0)

            def step(b, s, it, last):
                lo, hi = get(b, s, it, last)
                if first:
                    first(b, s, it)
                with e.Fori(lo, hi, WD) as w_:
                    unit(s, w_, e.snap(n), TP if last else 128, b, it)
                    e.reg_add(n, n, 1)
                if after:
                    after()
            batches(e, step)

        def flag(e):
            return nc.values_load_multi_w_load_instructions(
                FLAG[0:1, 0:1], engines=[e.engine], min_val=0, max_val=NN + 1,
                skip_runtime_bounds_check_because="a difference of node numbers")[1][0]

        @p.on("vector")
        def _(e):
            e.memset(AB[:], 0.0)
            e.memset(DEN, 0.0)
            for t in LM:
                e.memset(t[:], 0.0)
            e.memset(R[32:33, :], M0)
            e.memset(TY[:], 0.0).then_inc(zz, 1)
            e.wait_ge(zz, 1)
            e.nop().then_inc(bd, 1)
            e.nop().then_inc(fr, 1)
            fl = flag(e)
            w1, w2, w3 = reg(e, "w1"), reg(e, "w2"), reg(e, "w3")
            nk = reg(e, "nkx")
            with e.If(fl <= WD):
                e.reg_mov(w1, 0)
                e.reg_mov(w2, 0)
                e.reg_mov(w3, 0)
                held = {}

                def begin(k, s, it):
                    if s == 0 and not (isinstance(k, int) and k > NBF):
                        n = 2 if isinstance(k, int) and k == NBF else 2 * UN
                        held["lo"] = ranges(e, 0, k * 2, n)[0::2]

                def end(k, s):
                    e.reg_mov(w3, w2)
                    e.reg_mov(w2, w1)
                    if isinstance(k, int) and not 0 <= k <= NBF:
                        return
                    e.reg_mov(w1, held["lo"][s])

                def v1(b, s, r, _):
                    e.wait_ge(gr[s], r * 64 + 64)
                    need(e, au, b, 2)
                    d1(e, s % 2, s, KLD[:, bass.ds(b * 4, 4)], b)

                def v2(b, s, r, _):
                    need(e, au, b)
                    need(e, pm, b, 6)
                    d2(e, s % 2, s, b + 1)

                def v3(b, s, r, _):
                    need(e, pt, b)
                    d3(e, s % 2, rows(b))

                def v4(b, s, r, _):
                    need(e, pr, b)
                    need(e, s4, b, 1)
                    need(e, pbc, b, 2)
                    d4(e, s % 2, e.snap(w1, min_val=0, max_val=NN + 1), b + 1)

                def v5(b, s, r, _):
                    need(e, acs, b)
                    d5(e, s % 2, s)

                def v7(b, s, r, _):
                    need(e, aw, b)
                    need(e, pm, b, 2)
                    d7(e, s % 2, s)

                def v6(b, s, r, _):
                    need(e, pm, b)
                    need(e, bd, b, 1, 1)
                    d6(e, s % 2, s % 3, e.snap(w3, min_val=0, max_val=NN + 1), b + 1, bd)
                fast(e, [(v4, 1), (v2, 0), (v7, 2), (v1, -1), (v3, 0), (v5, 1), (v6, 3)], begin, end)
                e.wait_ge(bd, NR + 1)
            with e.Else():
                e.reg_mov(nk, 0)

                def before(b, s, it):
                    e.wait_ge(gr[s], it * 64 + 64)
                    e.tensor_copy(KX[:], KLD[:, bass.ds(b * 4, 4)]).then_inc(kx, 1)
                    e.reg_add(nk, nk, 1)

                def unit(s, w_, n, m, b, it):
                    e.wait_ge(kx, e.snap(nk))
                    d1(e, 0, s, KX[:], b)
                    e.wait_ge(s1, n)
                    e.tensor_scalar(KX[:], KX[:], float(WD), None, ALU.subtract).then_inc(kx, 1)
                    e.reg_add(nk, nk, 1)
                    e.wait_ge(au, n)
                    d2(e, 0, 0, n)
                    e.wait_ge(pt, n)
                    d3(e, 0, m)
                    e.wait_ge(pr, n)
                    d4(e, 0, w_, n)
                    e.wait_ge(acs, n)
                    d5(e, 0, 0)
                    e.wait_ge(aw, n)
                    d7(e, 0, 0)
                    e.wait_ge(pm, n)
                    d6(e, 0, 0, w_, n, zz)
                    e.wait_ge(zz, n + 1)

                def after():
                    e.memset(TY[:], 0.0).then_inc(fr, 1)
                general(e, unit, before, after)

        @p.on("tensor")
        def _(e):
            fl = flag(e)
            e.wait_ge(zz, 1)
            with e.If(fl <= WD):
                def w1_(b, s, r, _):
                    need(e, s1, b)
                    need(e, au, b, 2)
                    e.wait_ge(sdl[s % 3], 16 * (2 * r + s // 3) + 16)
                    t1_(e, s % 2, s % 3)

                def w2_(b, s, r, _):
                    need(e, s2, b)
                    need(e, s3, b, 1)
                    t2_(e, s % 2, rows(b))

                def w3_(b, s, r, _):
                    need(e, s3, b)
                    need(e, s4, b, 1)
                    t3_(e, s % 2)

                def w4_(b, s, r, _):
                    need(e, ac, b)
                    need(e, s5, b, 2)
                    need(e, acs, b, 2)
                    t4_(e, s % 2)

                def w5_(b, s, r, _):
                    need(e, aw, b)
                    need(e, bd, b, 2, 1)
                    t5g(e, s % 2, s, s, rows(b))

                def w6_(b, s, r, _):
                    e.wait_ge(ear[s], r * 16 + 16)
                    need(e, s7, b)
                    t5e(e, s % 2, s, s, rows(b), fr)
                fast(e, [(w4_, 1), (w2_, 0), (w5_, 2), (w3_, 0), (w1_, -1), (w6_, 2)])
            with e.Else():
                def unit(s, w_, n, m, b, it):
                    e.wait_ge(s1, n)
                    e.wait_ge(sdl[0], n * 16)
                    t1_(e, 0, 0)
                    e.wait_ge(s2, n)
                    t2_(e, 0, m)
                    e.wait_ge(s3, n)
                    t3_(e, 0)
                    e.wait_ge(ac, n)
                    t4_(e, 0)
                    e.wait_ge(aw, n)
                    e.wait_ge(ear[s], it * 16 + 16)
                    e.wait_ge(s7, n)
                    t5g(e, 0, 0, s, m)
                    t5e(e, 0, 0, s, m, fz)
                general(e, unit)

        @p.on("scalar")
        def _(e):
            fl = flag(e)
            e.wait_ge(zz, 1)
            with e.If(fl <= WD):
                nx = {}

                def begin(k, s, it):
                    if isinstance(k, int) and k < 0:
                        for b, v in enumerate(ranges(e, 0, 0, 4)[0::2]):
                            sd_load(e, b, v)
                    elif s == 0 and not (isinstance(k, int) and k >= NBF):
                        v = ranges(e, 0, k * 2 + 4, 2 * UN)
                        for i in range(UN):
                            nx[i] = v[2 * i]

                def x0(b, s, r, at):
                    if isinstance(b, int) and b < 2:
                        return
                    need(e, pu, b, 3)
                    sd_load(e, s % 3, nx[at])

                def x1(b, s, r, _):
                    need(e, pu, b)
                    need(e, s2, b, 2)
                    a1(e, s % 2)

                def x2(b, s, r, _):
                    need(e, s4, b)
                    a2(e, s % 2)

                def x3(b, s, r, _):
                    need(e, pbc, b)
                    need(e, bd, b, 3, 1)
                    a3(e, s % 2, s % 3)

                def x4(b, s, r, _):
                    need(e, s5, b)
                    a4(e, s)
                fast(e, [(x2, 1), (x3, 1), (x1, -1), (x0, -2), (x4, 1)], begin)
                for i in range(3):
                    e.wait_ge(sdl[i], 16 * len(range(i, NR + 1, 3)))
            with e.Else():
                e.nop().then_inc(sdg, 1)

                def unit(s, w_, n, m, b, it):
                    e.wait_ge(sdg, n)
                    sd_load(e, 0, w_)
                    e.wait_ge(pu, n)
                    a1(e, 0)
                    e.wait_ge(s4, n)
                    a2(e, 0)
                    e.wait_ge(pbc, n)
                    a3(e, 0, 0)
                    e.wait_ge(s5, n)
                    a4(e, 0, sdg)
                general(e, unit)
        p.run()

    XT3 = [GF[:, 512 * i:512 * i + 512].rearrange("p (j f) -> p j f", j=4) for i in range(3)]
    GI3 = [GF[:, 1536 + 528 * i:1536 + 528 * i + 512].rearrange("p (j f) -> p j f", j=4) for i in range(3)]
    HTT = [XR[:, 512 * i:512 * i + 512] for i in range(2)]
    HO = [XR[:, 1024 + 512 * i:1536 + 512 * i].rearrange("p (j f) -> p j f", j=4) for i in range(2)]
    TO = [XR[:, 2048 + 512 * i:2560 + 512 * i].rearrange("p (j f) -> p j f", j=4) for i in range(2)]

    def flat(t, n):
        return t[0:n].rearrange("p j f -> p (j f)")

    def bank(i, n):
        return PS[0:n, i, :].rearrange("p (j f) -> p j f", j=4)

    def weights(p, specs, rows=()):
        wl, wt, wc = p.sem("wl"), p.sem("wt"), p.sem("wc")
        raw = [p.tile([128, 128]) for _ in specs]
        done = [p.tile([128, 128]) for _ in specs]
        rw = [p.tile([1, 128]) for _ in rows]
        rep = [p.tile([128, 128]) for _ in rows]

        @p.on("sync")
        def _(e):
            for t, d in zip(raw, specs):
                e.dma_start(t[:], d).then_inc(wl, 16)
            for t, d in zip(rw, rows):
                e.dma_start(t[:], d.rearrange("(o f) -> o f", o=1)).then_inc(wl, 16)
        n = len(specs) + len(rows)

        @p.on("tensor")
        def _(e):
            e.wait_ge(wl, 16 * n)
            for k, t in enumerate(raw):
                if k:
                    e.wait_ge(wc, k)
                e.transpose(PS[:, 7, 0:128], t[:], ID[:]).then_inc(wt, 1)
            for k, t in enumerate(rw):
                e.wait_ge(wc, len(raw) + k)
                e.matmul(PS[:, 7, 0:128], ONE[0:1, :], t[:], start=True, stop=True).then_inc(wt, 1)

        @p.on("vector")
        def _(e):
            for k, t in enumerate(done + rep):
                e.wait_ge(wt, k + 1)
                e.tensor_copy(t[:], PS[:, 7, 0:128]).then_inc(wc, 1)
        return raw, done, rw, rep, wc, n

    def nodes(p, xin, hin, hw, xout, turned, mm, evac, combine, finish, souts, ready, norm="act", pre=None):
        xl, gl = [p.sem(f"xl{i}") for i in range(3)], [p.sem(f"gl{i}") for i in range(3)]
        tp_, tc, pmm, ev, cb, fi = (p.sem(k) for k in ("tp", "tc", "pmm", "ev", "cb", "fi"))
        nr = Norm(p, "q")
        st = [[p.sem(f"st{a}_{i}") for i in range(3)] for a in range(len(souts) + 1)]
        rings = [3] + [len(r) for _, r, _ in souts]
        outs = ([(xout, XT3, cb)] if xout is not None else []) + souts
        rings = [len(r) for _, r, _ in outs]

        @p.on("sync")
        def _(e):
            def load(g):
                e.dma_start(flat(XT3[g % 3], grows[g]), rowsl(xin, g)).then_inc(xl[g % 3], 16)
                if hin is not None:
                    n = grows[g]
                    h = hin[512 * g:512 * g + 4 * n, :].rearrange("(p j) f -> p j f", j=4)[:, :, 0:D]
                    e.dma_start(GI3[g % 3][0:n], h).then_inc(gl[g % 3], 16)
            for g in range(min(3, NG)):
                load(g)
            for g in range(NG):
                n = grows[g]
                for a, (d, ring, sem) in enumerate(outs):
                    e.wait_ge(fi if sem is None else sem, g + 1)
                    e.dma_start(rowsl(d, g), flat(ring[g % len(ring)], n)).then_inc(st[a][g % len(ring)], 16)
                if g + 3 < NG:
                    if xout is not None:
                        e.wait_ge(st[0][g % 3], 16 * (g // 3 + 1))
                    e.wait_ge(fi, g + 1)
                    load(g + 3)
            for a, (d, ring, sem) in enumerate(outs):
                k = len(ring)
                for i in range(min(k, NG)):
                    e.wait_ge(st[a][i], 16 * ((NG - 1 - i) // k + 1))

        def stored(e, ring, g):
            for a, (d, r, sem) in enumerate(outs):
                if r is ring and g >= len(r):
                    e.wait_ge(st[a][g % len(r)], 16 * (g // len(r)))

        @p.on("tensor")
        def _(e):
            e.wait_ge(*ready)

            def turn(g):
                n = grows[g]
                e.wait_ge(gl[g % 3], 16 * (g // 3 + 1))
                if g:
                    e.wait_ge(tc, g)
                for j in range(4):
                    i = e.transpose(PS[:, 3, n * j:n * j + n], GI3[g % 3][0:n, j, :], ID[0:n, 0:n])
                i.then_inc(tp_, 1)
            if turned:
                turn(0)
            for g in range(NG):
                if turned and g + 1 < NG:
                    turn(g + 1)
                if turned:
                    e.wait_ge(tc, g + 1)
                if g:
                    e.wait_ge(cb, g)
                mm(e, g, grows[g]).then_inc(pmm, 1)

        @p.on("scalar")
        def _(e):
            for g in range(NG):
                if g:
                    nr.root(e, g - 1)
                e.wait_ge(pmm, g + 1)
                if g:
                    e.wait_ge(cb, g)
                evac(e, g, grows[g]).then_inc(ev, 1)
                if g and norm == "act":
                    if g >= 3:
                        e.wait_ge(fi, g - 2)
                    stored(e, HO, g - 1)
                    nr.apply(e, HO[(g - 1) % 2], XT3[(g - 1) % 3], g - 1)
            nr.root(e, NG - 1)
            if norm == "act":
                if NG >= 3:
                    e.wait_ge(fi, NG - 2)
                stored(e, HO, NG - 1)
                nr.apply(e, HO[(NG - 1) % 2], XT3[(NG - 1) % 3], NG - 1)

        @p.on("vector")
        def _(e):
            def copyt(g):
                e.wait_ge(tp_, g + 1)
                if g >= 2:
                    e.wait_ge(pmm, g - 1)
                e.tensor_copy(HTT[g % 2][:, 0:4 * grows[g]], PS[:, 3, 0:4 * grows[g]]).then_inc(tc, 1)
            if turned:
                copyt(0)

            def fin(g):
                if norm == "act":
                    e.wait_ge(nr.f, g + 1)
                else:
                    e.wait_ge(nr.e_, 2 * g + 2)
                for ring in (TO, HO):
                    if norm != "act" or ring is TO:
                        stored(e, ring, g)
                finish(e, g, grows[g], nr).then_inc(fi, 1)
            for g in range(NG):
                if g:
                    nr.scale(e, g - 1)
                if turned and g + 1 < NG:
                    copyt(g + 1)
                if pre:
                    pre(e, g, grows[g])
                e.wait_ge(ev, g + 1)
                e.wait_ge(xl[g % 3], 16 * (g // 3 + 1))
                if hin is not None:
                    e.wait_ge(gl[g % 3], 16 * (g // 3 + 1))
                if norm != "act" and g >= 3:
                    e.wait_ge(fi, g - 2)
                combine(e, g, grows[g]).then_inc(cb, 1)
                e.wait_ge(cb, g + 1)
                nr_src = XT3[g % 3] if norm == "act" else SC[g % 2]
                nr.moments(e, nr_src, g)
                if g:
                    fin(g - 1)
            nr.scale(e, NG - 1)
            fin(NG - 1)
            e.wait_ge(fi, NG)
        SC = [p.tile([128, 4, D]) for _ in range(2)] if norm != "act" else None
        return SC

    RIN = sb("RIN", [128, NG * 4])
    ROUT = sb("ROUT", [128, NG * 4])

    def p_l1_nodes():
        p = Phase()
        raw, wt_, _, _, wc, nw = weights(p, [w, w_r])
        WT_, WRT = wt_
        LW, WL = p.tile([128, 128]), p.tile([128, 128])
        P2S, T3 = p.tile([128, 4, D]), p.tile([128, 4, D])
        DC = [p.tile([128, 4]) for _ in range(2)]
        MK = [p.tile([128, 4]) for _ in range(2)]
        NM = [p.tile([128, 4]) for _ in range(2)]
        RD = [p.tile([128, 4]) for _ in range(2)]
        Q = p.tile([128, 4, D])
        TMP = p.tile([128, NG * 4])
        ll, wp, wq, dv, rin, rdn = (p.sem(k) for k in ("ll", "wp", "wq", "dv", "rin", "rdn"))
        cc, mkd = p.sem("cc"), p.sem("mkd")
        cn = [0]

        @p.on("sync")
        def _(e):
            e.dma_start(LW[:], loop_w).then_inc(ll, 16)

        @p.on("tensor")
        def _(e):
            e.wait_ge(ll, 16)
            e.wait_ge(wc, nw)
            e.matmul(PS[:, 7, 0:128], raw[0][:], LW[:], start=True, stop=True).then_inc(wp, 1)

        @p.on("scalar")
        def _(e):
            e.wait_ge(rin, 1)
            e.activation(TMP[:], TMP[:], ACT.Sqrt).then_inc(rdn, 1)

        @p.on("vector")
        def _(e):
            e.wait_ge(wp, 1)
            e.tensor_copy(WL[:], PS[:, 7, 0:128]).then_inc(wq, 1)
            e.tensor_scalar(TMP[:], DIN[:], 1.0, None, ALU.max).then_inc(rin, 1)
            e.wait_ge(rdn, 1)
            link = chain(e, dv)
            link(e.reciprocal(RIN[:], TMP[:]))
            link(e.tensor_scalar(TMP[:], DIN[:], 1.0, None, ALU.min))
            link(e.tensor_tensor(RIN[:], RIN[:], TMP[:], ALU.mult))

        def mm(e, g, n):
            ag, ae = jp(AB[:, 0, :], g), jp(AB[:, 1, :], g)
            for j in range(4):
                c = slice(128 * j, 128 * j + 128)
                e.matmul(PS[0:n, 0, c], ag[:, j, :], WT_[:], start=True, stop=False)
                e.matmul(PS[0:n, 0, c], ae[:, j, :], WRT[:], start=False, stop=True)
                h = HTT[g % 2][:, n * j:n * j + n]
                e.matmul(PS[0:n, 1, c], h, WL[:], start=True, stop=True)
                e.matmul(PS[0:n, 2, c], h, WT_[:], start=True, stop=True)
                i = e.matmul(PS[0:n, 6, j:j + 1], jp(R[64:65, :], g)[:, j, :], ONE[64:65, 0:1], start=True, stop=True)
            return i

        def evac(e, g, n):
            e.activation(P2S[0:n], bank(1, n), ACT.Copy)
            e.wait_ge(mkd, g + 1)
            for j in range(4):
                i = e.activation(T3[0:n, j, :], bank(2, n)[:, j, :], ACT.Copy, scale=NM[g % 2][0:n, j:j + 1])
            return i

        def combine(e, g, n):
            s = g % 2
            for j in range(4):
                i = e.scalar_tensor_tensor(out=Q[0:n, j, :], in0=bank(0, n)[:, j, :], scalar=RD[s][0:n, j:j + 1],
                                           in1=P2S[0:n, j, :], op0=ALU.mult, op1=ALU.add)
            i.then_inc(cc, 1)
            e.wait_ge(cc, 2 * g + 1)
            for j in range(4):
                i = e.scalar_tensor_tensor(out=Q[0:n, j, :], in0=Q[0:n, j, :], scalar=MK[s][0:n, j:j + 1],
                                           in1=T3[0:n, j, :], op0=ALU.mult, op1=ALU.add)
            i.then_inc(cc, 1)
            e.wait_ge(cc, 2 * g + 2)
            return e.scalar_tensor_tensor(out=XT3[g % 3][0:n], in0=Q[0:n], scalar=0.0, in1=XT3[g % 3][0:n],
                                          op0=ALU.max, op1=ALU.add)

        def finish(e, g, n, nr):
            for j in range(4):
                i = e.tensor_scalar(TO[g % 2][0:n, j, :], HO[g % 2][0:n, j, :], RIN[0:n, 4 * g + j:4 * g + j + 1],
                                    None, ALU.mult)
            return i

        def pre(e, g, n):
            s = g % 2
            e.wait_ge(p.sem("pmm"), g + 1)
            e.tensor_copy(DC[s][0:n], PS[0:n, 6, 0:4]).then_inc(p.sem("pa"), 1)
            e.wait_ge(p.sem("pa"), g + 1)
            e.tensor_scalar(MK[s][0:n], DC[s][0:n], 0.0, None, ALU.is_gt).then_inc(p.sem("pb"), 1)
            e.wait_ge(p.sem("pb"), g + 1)
            e.tensor_scalar(NM[s][0:n], MK[s][0:n], -1.0, 1.0, ALU.mult, ALU.add).then_inc(mkd, 1)
            e.wait_ge(mkd, g + 1)
            e.tensor_tensor(DC[s][0:n], DC[s][0:n], NM[s][0:n], ALU.add).then_inc(p.sem("pc"), 1)
            e.wait_ge(p.sem("pc"), g + 1)
            e.reciprocal(RD[s][0:n], DC[s][0:n]).then_inc(p.sem("pd"), 1)
            e.wait_ge(p.sem("pd"), g + 1)
        nodes(p, x1d, t1d, TW, x2d, True, mm, evac, combine, finish, [(h2d, HO, p.sem("q5")), (t2d, TO, None)], (wq, 1), pre=pre)
        p.run()

    KLS = XR[:, 0:NR * 4]
    IDXS = XR[:, NR * 4:NR * 8].bitcast(I32)

    def p_sorted():
        p = Phase()
        T = AB[:, 0, 0:NR * 4]
        load_list(p, "sorted", 1, KLS, [(1, T)])

        @p.on("vector")
        def _(e):
            e.tensor_copy(IDXS, T).then_inc(p.sem("ix"), 1)
            e.wait_ge(p.sem("ix"), 1)
        p.run()

    def gathered(s):
        return GS[:, s, :, :]

    def aggregate(table, idx, width, part, keys, ACC, weight=None, count=False):
        p = Phase()
        ready = gather(p, p.sem("bd"), table[0:NN, :], idx, D)
        edge_pass(p, width, part, keys, gathered, ready, 64, ACC, weight=weight, count=count)

        for k in ("vector", "tensor"):
            @p.on(k)
            def _(e):
                e.wait_ge(p.sem("edone"), 1)
        p.run()

    def p_l2f():
        aggregate(t2d, IDXS, 128, 1, KLS, AB[:, 0, :], count=True)

    def p_l2b():
        aggregate(t3d, IDX[:], 64, 0, KLD[:], AB[:, 1, :])

    def p_out_degrees():
        p = Phase()
        TMP = p.tile([128, NG * 4])
        mm, dg, rt, dv, sc = (p.sem(k) for k in ("mm", "dg", "rt", "dv", "sc"))
        NB = 6
        ld, st = [p.sem(f"ld{i}") for i in range(NB)], [p.sem(f"st{i}") for i in range(NB)]
        HB = [GF[:, 512 * i:512 * i + 512].rearrange("p (j f) -> p j f", j=4) for i in range(NB)]

        @p.on("tensor")
        def _(e):
            for g in range(NG):
                n = grows[g]
                for j in range(4):
                    i = e.matmul(PS[0:n, 6, 4 * g + j:4 * g + j + 1], jp(R[0:1, :], g)[:, j, :], ONE[0:1, 0:1],
                                 start=True, stop=True)
            i.then_inc(mm, 1)

        @p.on("scalar")
        def _(e):
            e.wait_ge(dg, 1)
            e.activation(TMP[:], TMP[:], ACT.Sqrt).then_inc(rt, 1)
            for g in range(NG):
                e.wait_ge(sc, g + 1)
                e.dma_start(rowsl(t3d, g), flat(HB[g % NB], grows[g])).then_inc(st[g % NB], 16)
            for i in range(NB):
                if i < NG:
                    e.wait_ge(st[i], 16 * ((NG - 1 - i) // NB + 1))

        @p.on("sync")
        def _(e):
            for g in range(NG):
                if g >= NB:
                    e.wait_ge(st[g % NB], 16 * (g // NB))
                e.dma_start(flat(HB[g % NB], grows[g]), rowsl(h2d, g)).then_inc(ld[g % NB], 16)

        @p.on("vector")
        def _(e):
            link = chain(e, dv)
            n, c = grows[NG - 1], 4 * (NG - 1)
            e.wait_ge(mm, 1)
            if NG > 1:
                e.tensor_copy(DOUT[:, 0:c], PS[:, 6, 0:c])
            link(e.tensor_copy(DOUT[0:n, c:c + 4], PS[0:n, 6, c:c + 4]))
            e.tensor_scalar(TMP[:], DOUT[:], 1.0, None, ALU.max).then_inc(dg, 1)
            e.wait_ge(rt, 1)
            link(e.reciprocal(ROUT[:], TMP[:]))
            link(e.tensor_scalar(TMP[:], DOUT[:], 1.0, None, ALU.min))
            link(e.tensor_tensor(ROUT[:], ROUT[:], TMP[:], ALU.mult))
            for g in range(NG):
                n = grows[g]
                e.wait_ge(ld[g % NB], 16 * (g // NB + 1))
                for j in range(4):
                    i = e.tensor_scalar(HB[g % NB][0:n, j, :], HB[g % NB][0:n, j, :],
                                        ROUT[0:n, 4 * g + j:4 * g + j + 1], None, ALU.mult)
                i.then_inc(sc, 1)
        p.run()

    def p_l2_nodes():
        p = Phase()
        raw, mats, _, rep, wc, nw = weights(p, [Ws, Wd], [bs, bd_])
        Q, P2S, TY = p.tile([128, 4, D]), p.tile([128, 4, D]), p.tile([1, 1])
        dv, cc = p.sem("dv"), p.sem("cc")

        @p.on("vector")
        def _(e):
            link = chain(e, dv)
            e.wait_ge(wc, nw)
            e.tensor_scalar(mats[0][:], mats[0][:], 0.5, None, ALU.mult)
            e.tensor_scalar(mats[1][:], mats[1][:], 0.5, None, ALU.mult)
            link(e.tensor_tensor(rep[0][:], rep[0][:], rep[1][:], ALU.add))
            link(e.tensor_scalar(rep[0][:], rep[0][:], 0.5, None, ALU.mult))

        def mm(e, g, n):
            for a in range(2):
                for j in range(4):
                    i = e.matmul(PS[0:n, a, 128 * j:128 * j + 128], jp(AB[:, a, :], g)[:, j, :], mats[a][:],
                                 start=True, stop=True)
            return i

        def evac(e, g, n):
            for j in range(4):
                i = e.activation(P2S[0:n, j, :], bank(1, n)[:, j, :], ACT.Copy, scale=RIN[0:n, 4 * g + j:4 * g + j + 1])
            return i

        def combine(e, g, n):
            for j in range(4):
                i = e.scalar_tensor_tensor(out=Q[0:n, j, :], in0=bank(0, n)[:, j, :],
                                           scalar=ROUT[0:n, 4 * g + j:4 * g + j + 1],
                                           in1=P2S[0:n, j, :], op0=ALU.mult, op1=ALU.add)
            i.then_inc(cc, 1)
            e.wait_ge(cc, 2 * g + 1)
            e.tensor_tensor(Q[0:n], Q[0:n], rep[0][0:n].unsqueeze(1).to_broadcast([n, 4, D]), ALU.add).then_inc(cc, 1)
            e.wait_ge(cc, 2 * g + 2)
            return e.tensor_tensor(XT3[g % 3][0:n], Q[0:n], XT3[g % 3][0:n], ALU.add)

        def finish(e, g, n, nr):
            return e.memset(TY[:], 0.0)
        nodes(p, x2d, None, D, x3d, False, mm, evac, combine, finish, [(t4d, HO, p.sem("q5"))], (dv, 2))
        p.run()

    EW = XR[:, 0:NR * 4]

    def p_weights():
        p = Phase()
        ld = p.sem("ld")
        T = AB[:, 1, 0:NCH * BE].rearrange("p (c k) -> p c k", c=NCH)
        nld = [0]

        @p.on("sync")
        def _(e):
            def put(o, i):
                e.dma_start(o, i).then_inc(ld, 16)
                nld[0] += 1
            for ci, (c0, n) in enumerate(chunks):
                nf = min(n, NBF - c0)
                if nf:
                    put(T[0:nf, ci, :], ew[c0 * BE:(c0 + nf) * BE].rearrange("(b k) -> b k", k=BE))
            n = (NR - 1) % 128
            put(T[n:n + 1, NCH - 1, 0:4 * TP], ew[NBF * BE:NE].rearrange("(b k) -> b k", b=1))
            put(T[n:n + 1, NCH - 1, 4 * TP:BE], ew[NBF * BE:NBF * BE + BE - 4 * TP].rearrange("(b k) -> b k", b=1))
        nput = sum(1 for c0, n in chunks if min(n, NBF - c0)) + 2
        turn_rows(p, (ld, 16 * nput), [(T, EW)])
        p.run()

    def p_l3():
        aggregate(t4d, IDX[:], 64, 0, KLD[:], AB[:, 0, :], weight=EW)

    def p_l3_nodes():
        p = Phase()
        raw, mats, _, rep, wc, nw = weights(p, [Wrel, Wroot], [brel, gamma, beta])
        Q, P1S, RC = p.tile([128, 4, D]), p.tile([128, 4, D]), p.tile([128, NG * 4])
        dv, cc, ff = p.sem("dv"), p.sem("cc"), p.sem("ff")

        @p.on("vector")
        def _(e):
            link = chain(e, dv)
            e.wait_ge(wc, nw)
            link(e.tensor_scalar(RC[:], DIN[:], 1.0, None, ALU.max))
            link(e.reciprocal(RC[:], RC[:]))

        def mm(e, g, n):
            for j in range(4):
                e.matmul(PS[0:n, 0, 128 * j:128 * j + 128], jp(AB[:, 0, :], g)[:, j, :], mats[0][:], start=True, stop=True)
            for j in range(4):
                i = e.matmul(PS[0:n, 1, 128 * j:128 * j + 128], HTT[g % 2][:, n * j:n * j + n], mats[1][:],
                             start=True, stop=True)
            return i

        def evac(e, g, n):
            return e.activation(P1S[0:n], bank(1, n), ACT.Copy)

        def combine(e, g, n):
            for j in range(4):
                i = e.scalar_tensor_tensor(out=Q[0:n, j, :], in0=bank(0, n)[:, j, :],
                                           scalar=RC[0:n, 4 * g + j:4 * g + j + 1],
                                           in1=P1S[0:n, j, :], op0=ALU.mult, op1=ALU.add)
            i.then_inc(cc, 1)
            e.wait_ge(cc, 2 * g + 1)
            e.tensor_tensor(Q[0:n], Q[0:n], rep[0][0:n].unsqueeze(1).to_broadcast([n, 4, D]), ALU.add).then_inc(cc, 1)
            e.wait_ge(cc, 2 * g + 2)
            return e.tensor_tensor(SC[g % 2][0:n], Q[0:n], GI3[g % 3][0:n], ALU.add)

        def finish(e, g, n, nr):
            s = g % 2
            Y = SC[s][0:n]
            for j in range(4):
                i = e.tensor_scalar(Y[:, j, :], Y[:, j, :], nr.rs[s][0:n, j:j + 1], nr.nm[s][0:n, j:j + 1],
                                    ALU.mult, ALU.add)
            i.then_inc(nr.f, 1)
            e.wait_ge(nr.f, g + 1)
            e.tensor_tensor(Y, Y, rep[1][0:n].unsqueeze(1).to_broadcast([n, 4, D]), ALU.mult).then_inc(ff, 1)
            e.wait_ge(ff, 2 * g + 1)
            e.tensor_tensor(Y, Y, rep[2][0:n].unsqueeze(1).to_broadcast([n, 4, D]), ALU.add).then_inc(ff, 1)
            e.wait_ge(ff, 2 * g + 2)
            return e.scalar_tensor_tensor(out=TO[s][0:n], in0=Y, scalar=0.0, in1=XT3[g % 3][0:n],
                                          op0=ALU.max, op1=ALU.add)
        SC = nodes(p, x3d, t4d, D, None, True, mm, evac, combine, finish, [(out, TO, None)], (dv, 2), norm="dve")
        p.run()

    for phase in (p_const, p_lists, p_prep, p_l0, p_flag, p_l1, p_l1_nodes, p_sorted, p_l2f, p_out_degrees,
                  p_l2b, p_l2_nodes, p_weights, p_l3, p_l3_nodes):
        phase()


_INS = ["x", "src", "dst", "edge_attr_128", "edge_weight", "L0_gnn_u", "L0_gnn_W1", "L0_gnn_b1", "L0_gnn_W2",
        "L0_gnn_b2", "L1_gnn_w", "L1_gnn_w_r", "L1_gnn_att_w", "L1_gnn_loop_w", "L2_gnn_W_src", "L2_gnn_b_src",
        "L2_gnn_W_dst", "L2_gnn_b_dst", "L3_gnn_W_rel", "L3_gnn_b_rel", "L3_gnn_W_root", "L3_gnn_gamma",
        "L3_gnn_beta"]


def kernel(**inputs):
    import numpy as _np
    import concourse.bacc as _bacc
    from concourse import mybir as _mybir
    from concourse.bass_utils import run_bass_kernel_spmd as _run

    nc = _bacc.Bacc("TRN2", target_bir_lowering=False, num_devices=1, dynamic_dma_scratch_size=8192)
    arrays, args = {}, []
    for name in _INS:
        a = _np.ascontiguousarray(inputs[name])
        arrays[f"in_{name}"] = a
        args.append(nc.dram_tensor(f"in_{name}", a.shape, _mybir.dt.from_np(a.dtype), kind="ExternalInput").ap())
    shape = inputs["x"].shape
    out = nc.dram_tensor("out_0", shape, _mybir.dt.float32, kind="ExternalOutput").ap()
    gnn(nc, *args, out)
    r = _run(nc, [arrays], core_ids=[0])
    return r.results[0]["out_0"]
```

```python
import concourse.bass as bass
from concourse import mybir
from contextlib import ExitStack

F32 = mybir.dt.float32
I32 = mybir.dt.int32
U32 = mybir.dt.uint32
BF16 = mybir.dt.bfloat16
ALU = mybir.AluOpType
ACT = mybir.ActivationFunctionType
AX = mybir.AxisListType.X

D = 128
BE = 512
TP = 80
UN = 6
TW = 132
BIG = float(2 ** 100)
M0 = -1.0e20
EPS = 1e-5


def gnn(nc, x, src, dst, ea, ew, u, W1, b1, W2, b2, w, w_r, att, loop_w, Ws, bs, Wd, bd_,
        Wrel, brel, Wroot, gamma, beta, out):
    NN, NE = x.shape[0], src.shape[0]
    NBF = (NE - 4 * TP) // BE
    NR = NBF + 1
    NW = (NN + 127) // 128
    NG = (NN + 511) // 512
    NP = NG * 512
    assert NE == NBF * BE + 4 * TP and NBF % UN == 0 and NN % 4 == 0 and NW <= 98
    grows = [min(512, NN - 512 * g) // 4 for g in range(NG)]
    chunks = [(c, min(128, NR - c)) for c in range(0, NR, 128)]
    NCH = len(chunks)

    def dram(name, shape, dt=F32):
        return nc.dram_tensor(name, shape, dt, kind="Internal").ap()

    x1d, x2d, x3d, h2d = (dram(n, (NP, D)) for n in ("x1d", "x2d", "x3d", "h2d"))
    t1d = dram("t1d", (NP, TW))
    t2d, t3d, t4d = (dram(n, (NP, D)) for n in ("t2d", "t3d", "t4d"))
    sortd = dram("sortd", (NE, 2), I32)
    rngd = dram("rngd", (2, NR, 2), I32)

    top = ExitStack()

    def sb(name, shape, dt=F32):
        return top.enter_context(nc.sbuf_tensor(name, shape, dt))

    NC = max(NN + 132, 12632)
    AB = sb("AB", [128, 2, NC])
    R = sb("R", [128, NC])
    KLD = sb("KLD", [128, NR * 4])
    IDX = sb("IDX", [128, NR * 4], I32)
    SREL = sb("SREL", [128, NR * 4])
    GS = sb("GS", [128, UN, 4, TW])
    XR = sb("XR", [128, max(UN * BE, 2 * NR * 4)])
    RNG = sb("RNG", [64, 2 * NR + 2], I32)
    ID = sb("ID", [128, 128])
    IDB = sb("IDB", [128, 128], BF16)
    ONE = sb("ONE", [128, 128])
    IO = sb("IO", [128, 128])
    IOB = sb("IOB", [128, 64], BF16)
    DIN = sb("DIN", [128, NG * 4])
    DOUT = sb("DOUT", [128, NG * 4])
    EA = XR[:, 0:UN * BE].rearrange("p (s r f) -> p s r f", s=UN, r=4)
    GF = GS[:].rearrange("p s r f -> p (s r f)")
    PS = top.enter_context(nc.psum_tensor("PS", [128, 8, 512], F32))

    nsem = [0]

    def reg(e, name):
        nsem[0] += 1
        return e.alloc_register(f"{name}{nsem[0]}")

    class Phase:

        def __init__(self):
            self.ctx = ExitStack()
            self.q = {k: [] for k in ("sync", "gpsimd", "vector", "scalar", "tensor")}
            self.s = {}
            self.nt = 0

        def sem(self, name):
            if name not in self.s:
                nsem[0] += 1
                self.s[name] = nc.alloc_semaphore(name=f"{name}_{nsem[0]}")
            return self.s[name]

        def on(self, eng):
            def add(f):
                self.q[eng].append(f)
                return f
            return add

        def tile(self, shape, dt=F32, name="w"):
            self.nt += 1
            nsem[0] += 1
            return self.ctx.enter_context(nc.sbuf_tensor(f"{name}{nsem[0]}", shape, dt))

        def run(self):
            with self.ctx:
                with nc.Block() as blk:
                    place = {"sync": blk.sync, "gpsimd": blk.gpsimd, "vector": blk.vector,
                             "scalar": blk.scalar, "tensor": blk.tensor}
                    for eng, fs in self.q.items():
                        def emit(e, fs=fs):
                            for f in fs:
                                f(e)
                        place[eng](emit)
            nc.clear_and_free_semaphores(list(self.s.values()))
            nc.all_engine_barrier()

    def chain(e, sem):
        n = [0]

        def link(ins):
            n[0] += 1
            ins.then_inc(sem, 1)
            e.wait_ge(sem, n[0])
        return link

    def ranges(e, part, col, n):
        return nc.values_load_multi_w_load_instructions(
            RNG[32 * part:32 * part + 1, bass.ds(col, n)], engines=[e.engine], min_val=0, max_val=NN + 1,
            skip_runtime_bounds_check_because="keys are node numbers")[1]

    def p_const():
        p = Phase()
        z, c = p.sem("z"), p.sem("c")

        @p.on("gpsimd")
        def _(e):
            link = chain(e, z)
            e.iota(IO[:], [[1, 128]], base=0, channel_multiplier=0, allow_small_or_imprecise_dtypes=True)
            e.memset(ONE[:], 1.0)
            link(e.memset(ID[:], 0.0))
            link(e.affine_select(out=ID[:], in_=ID[:], compare_op=ALU.not_equal, fill=1.0, base=0,
                                 pattern=[[-1, 128]], channel_multiplier=1))

        @p.on("vector")
        def _(e):
            e.memset(DIN[:], 0.0)
            e.memset(DOUT[:], 0.0)
            e.memset(RNG[:], 0)
            e.wait_ge(z, 2)
            e.tensor_copy(IDB[:], ID[:])
            e.tensor_copy(IOB[:], IO[:, 0:64]).then_inc(c, 1)
            e.wait_ge(c, 1)
        p.run()

    def turn_rows(p, ready, pairs):
        tr, cp = p.sem("tr"), p.sem("cp")
        jobs = [(f, t, ci, r) for f, t in pairs for ci in range(NCH) for r in range(4)]

        @p.on("tensor")
        def _(e):
            e.wait_ge(*ready)
            for k, (f, t, ci, r) in enumerate(jobs):
                n = chunks[ci][1]
                if k >= 8:
                    e.wait_ge(cp, k - 7)
                v = f[0:n, ci, :].rearrange("b (p r) -> b r p", r=4)[:, r, :]
                e.transpose(PS[:, k % 8, 0:n], v, ID[0:n, 0:n]).then_inc(tr, 1)

        @p.on("vector")
        def _(e):
            for k, (f, t, ci, r) in enumerate(jobs):
                c0, n = chunks[ci]
                e.wait_ge(tr, k + 1)
                o = t.rearrange("p (b r) -> p b r", r=4)[:, c0:c0 + n, r]
                e.tensor_copy(o, PS[:, k % 8, 0:n]).then_inc(cp, 1)
            e.wait_ge(cp, len(jobs))

    def load_list(p, kind, part, keys, full):
        B = AB[:, 1, :]
        W = BE * (1 if kind == "in" else 2)
        stg = [B[:, i * NCH * W:(i + 1) * NCH * W].bitcast(I32).rearrange("p (c k) -> p c k", c=NCH)
               for i in range(2 if kind == "in" else 1)]
        o = 2 * NCH * BE
        fl = [B[:, o + i * NCH * BE:o + (i + 1) * NCH * BE].rearrange("p (c k) -> p c k", c=NCH) for i in range(3)]
        mn, mx, rg = p.tile([128, NCH]), p.tile([128, NCH]), p.tile([128, NCH, 2], I32)
        ld, st, dv, rs = (p.sem(n) for n in ("ld", "st", "dv", "rs"))
        nld = [0]

        @p.on("sync")
        def _(e):
            def put(o, i):
                e.dma_start(o, i).then_inc(ld, 16)
                nld[0] += 1
            srcs = [(stg[0], dst, 1), (stg[1], src, 1)] if kind == "in" else [(stg[0], sortd.rearrange("e t -> (e t)"), 2)]
            for t, d, m in srcs:
                for ci, (c0, n) in enumerate(chunks):
                    nf = min(n, NBF - c0)
                    if nf:
                        put(t[0:nf, ci, :], d[c0 * BE * m:(c0 + nf) * BE * m].rearrange("(b k) -> b k", k=BE * m))
                n = (NR - 1) % 128
                put(t[n:n + 1, NCH - 1, 0:4 * TP * m], d[NBF * BE * m:NE * m].rearrange("(b k) -> b k", b=1))
                put(t[n:n + 1, NCH - 1, 4 * TP * m:BE * m],
                    d[NBF * BE * m:NBF * BE * m + (BE - 4 * TP) * m].rearrange("(b k) -> b k", b=1))

        @p.on("vector")
        def _(e):
            e.wait_ge(ld, 16 * nld[0])
            if kind == "in":
                a, b = stg[0], stg[1]
            else:
                v = stg[0].rearrange("p c (k t) -> p c k t", t=2)
                b, a = v[:, :, :, 0], v[:, :, :, 1]
            link = chain(e, dv)
            for ci, (c0, n) in enumerate(chunks):
                e.tensor_copy(fl[0][0:n, ci, :], a[0:n, ci, :])
                last = e.tensor_copy(fl[1][0:n, ci, :], b[0:n, ci, :])
            link(last)
            for ci, (c0, n) in enumerate(chunks):
                e.tensor_reduce(mn[0:n, ci:ci + 1], fl[0][0:n, ci, :], AX, ALU.min)
                last = e.tensor_reduce(mx[0:n, ci:ci + 1], fl[0][0:n, ci, :], AX, ALU.max)
            link(last)
            for ci, (c0, n) in enumerate(chunks):
                e.tensor_copy(rg[0:n, ci, 0:1], mn[0:n, ci:ci + 1])
                e.tensor_scalar(rg[0:n, ci, 1:2], mx[0:n, ci:ci + 1], 1.0, None, ALU.add)
                last = e.tensor_scalar(fl[2][0:n, ci, :], fl[0][0:n, ci, :], mn[0:n, ci:ci + 1], None, ALU.subtract)
            link(last)

        @p.on("scalar")
        def _(e):
            e.wait_ge(dv, 3)
            for ci, (c0, n) in enumerate(chunks):
                e.dma_start(rngd[part, c0:c0 + n, :], rg[0:n, ci, :]).then_inc(st, 16)
            e.wait_ge(st, 16 * NCH)
            e.dma_start(RNG[32 * part:32 * part + 1, 0:2 * NR], rngd[part].rearrange("(o r) t -> o (r t)", o=1)).then_inc(rs, 16)
            e.wait_ge(rs, 16)

        turn_rows(p, (dv, 3), [(fl[2], keys)] + [(fl[i], t) for i, t in full])

    B0 = AB[:, 1, :]
    _o = [0]

    def take(n, dt=F32):
        v = B0[:, _o[0]:_o[0] + n]
        _o[0] += n
        return v if dt == F32 else v.bitcast(dt)

    PAY = take(NR * 8, I32).rearrange("p (b t) -> p b t", t=2)
    AW = take(NR * 4)
    POS = take(NR * 4, I32)
    LOW, UPI, ONB = (take(64, BF16) for _ in range(3))
    IOA = take(49, BF16)
    BASE = take(392)
    V3 = take(128)
    OH = [take(196, BF16) for _ in range(2)]
    PR = [take(392) for _ in range(2)]
    LISTEND = _o[0]

    def p_lists():
        p = Phase()
        load_list(p, "in", 0, KLD[:], [(0, AB[:, 0, 0:NR * 4]), (1, AB[:, 0, NR * 4:NR * 8])])
        p.run()

    def p_prep():
        p = Phase()
        dn, oh, mm, g = p.sem("dn"), p.sem("oh"), p.sem("mm"), p.sem("g")
        JK = [p.tile([128, NBF], BF16) for _ in range(4)]
        cn = p.sem("cn")
        DF, SF = AB[:, 0, 0:NR * 4], AB[:, 0, NR * 4:NR * 8]

        @p.on("gpsimd")
        def _(e):
            link = chain(e, g)
            T = AB[:, 0, NR * 8:NR * 8 + 256]
            e.memset(T[:, 128:256], 1.0)
            link(e.memset(T[:, 0:128], 1.0))
            e.affine_select(out=T[:, 0:128], in_=T[:, 0:128], compare_op=ALU.is_gt, fill=0.0, base=0,
                            pattern=[[1, 128]], channel_multiplier=-1)
            link(e.affine_select(out=T[:, 128:256], in_=T[:, 128:256], compare_op=ALU.is_ge, fill=0.0, base=0,
                                 pattern=[[-1, 128]], channel_multiplier=1))

        wr, at3 = p.tile([128, 128]), p.tile([128, 1])
        ld = p.sem("ld")

        @p.on("sync")
        def _(e):
            e.dma_start(wr[:], w_r).then_inc(ld, 16)
            e.dma_start(at3[:], att[2 * D:3 * D].rearrange("(p o) -> p o", o=1)).then_inc(ld, 16)

        TI = AB[:, 0, NR * 8 + 256:NR * 12 + 256].bitcast(I32)

        @p.on("vector")
        def _(e):
            link = chain(e, dn)
            e.tensor_copy(IDX[:], SF)
            e.tensor_copy(PAY[:, :, 0], DF)
            e.tensor_copy(ONB, ONE[:])
            e.tensor_copy(IOA, IO[:, 0:98])
            link(e.tensor_copy(PAY[:, :, 1], SF))
            link(e.tensor_scalar(TI, IDX[:], 7, None, ALU.arith_shift_right))
            e.wait_ge(g, 2)
            e.tensor_copy(LOW, AB[:, 0, NR * 8:NR * 8 + 128])
            e.tensor_copy(UPI, AB[:, 0, NR * 8 + 128:NR * 8 + 256])
            link(e.tensor_copy(AW, TI))
            v = AW.rearrange("p (b r) -> p r b", r=4)
            for a in range(NW):
                for r in range(4):
                    if a:
                        e.wait_ge(cn, 4 * a + r - 3)
                    e.tensor_scalar(JK[r][:], v[:, r, 0:NBF], float(a), None, ALU.is_equal, ALU.add,
                                    accum_out=PR[0][:, 98 * r + a:98 * r + a + 1]).then_inc(cn, 1)
            for r in range(4):
                if NW < 98:
                    e.memset(PR[0][:, 98 * r + NW:98 * r + 98], 0.0)
                i = e.tensor_scalar(OH[0][:, 98 * r:98 * r + 98], IOA, AW[:, 4 * NBF + r:4 * NBF + r + 1], None,
                                    ALU.is_equal)
            i.then_inc(oh, 1)
            e.wait_ge(mm, 2)
            tot = PR[0].rearrange("p (a r) -> p r a", r=4)
            link(e.tensor_copy(tot, PS[:, 0, 0:392].rearrange("p (r a) -> p r a", r=4)))
            link(e.memset(BASE, 1.0))
            link(e.tensor_tensor_scan(PR[1], BASE, PR[0], 0.0, ALU.mult, ALU.add))
            link(e.tensor_tensor(PR[1], PR[1], PR[0], ALU.subtract))
            e.tensor_copy(V3, PS[:, 1, 0:128])
            link(e.tensor_copy(BASE.rearrange("p (r a) -> p r a", r=4), PR[1].rearrange("p (a r) -> p r a", r=4)))

        @p.on("tensor")
        def _(e):
            e.wait_ge(ld, 32)
            e.matmul(PS[:, 1, 0:128], at3[:, 0:1].to_broadcast([128, 128]), wr[:], start=True, stop=True).then_inc(mm, 1)
            e.wait_ge(oh, 1)
            e.matmul(PS[:, 0, 0:392], ONE[:], PR[0], start=True, stop=False, skip_group_check=True)
            e.matmul(PS[:, 0, 0:392], ONB[0:TP, :], OH[0][0:TP, :], start=False, stop=True, skip_group_check=True).then_inc(mm, 1)
        p.run()

    NIT = NBF // UN

    def batches(e, step):
        with e.Fori(0, NIT) as it:
            for s in range(UN):
                step(it * UN + s, s, it, False)
        step(NBF, 0, NIT, True)

    def unit_ranges(e, part):
        held = {}

        def get(b, s, it, last):
            if last:
                return ranges(e, part, 2 * NBF, 2)
            if s == 0:
                held[0] = ranges(e, part, it * (2 * UN), 2 * UN)
            return held[0][2 * s:2 * s + 2]
        return get

    def edge_pass(p, width, part, keys, feats, ready, rstep, ACC, weight=None, count=True, rank=False):
        acc, mmd, oh, bd, dv, kx = (p.sem(n) for n in ("acc", "mmd", "oh", "bd", "dv", "kx"))
        SEL = [p.tile([128, 4, width]) for _ in range(2)]
        KX, TY = p.tile([128, 4]), p.tile([1, 1])
        if rank:
            ohr, low, rd, sr, rz = (p.sem(n) for n in ("ohr", "low", "rd", "sr", "rz"))
            PF = [p.tile([128, 4]) for _ in range(2)]
            SF = [p.tile([128, 4]) for _ in range(2)]
            JK = p.tile([128, 4, 128])
            sk = p.sem("sk")
            SELB, ohb = p.tile([128, 4, width], BF16), p.sem("ohb")

        def sel(e, s, kl, b):
            o = SEL[s % 2]
            if weight is None:
                return e.tensor_tensor(o[:], IO[:, 0:width].unsqueeze(1).to_broadcast([128, 4, width]),
                                       kl.unsqueeze(2).to_broadcast([128, 4, width]), ALU.is_equal)
            for r in range(4):
                i = e.tensor_scalar(o[:, r, :], IO[:, 0:width], kl[:, r:r + 1],
                                    weight[:, bass.ds(b * 4 + r, 1)], ALU.is_equal, ALU.mult)
            return i

        @p.on("vector")
        def _(e):
            link = chain(e, dv)
            if count and not rank:
                e.memset(R[0:1, :], 0.0)
            e.memset(ACC, 0.0)
            if rank:
                e.memset(SF[0][:], 0.0)
                e.memset(SF[1][:], 0.0)
            link(e.memset(SEL[1][:], 0.0))
            nu, na, nk, wp = (reg(e, x_) for x_ in ("nu", "na", "nk", "wp"))
            e.reg_mov(nu, 1)
            e.reg_mov(na, 1)
            e.reg_mov(nk, 1)
            e.nop().then_inc(kx, 1)
            e.reg_mov(wp, 0)
            e.nop().then_inc(acc, 1)
            get = unit_ranges(e, part)
            if rank:
                e.wait_ge(rz, 1)

            def linked(ins):
                ins.then_inc(kx, 1)
                e.reg_add(nk, nk, 1)

            def accumulate(q, wv, ends=True):
                n_mm, n_acc = e.snap(nu), e.snap(na)
                e.wait_ge(mmd, n_mm)
                e.wait_ge(acc, n_acc)
                if count:
                    i = e.tensor_tensor(R[0:1, bass.ds(wv, width)], R[0:1, bass.ds(wv, width)],
                                        PS[0:1, 2 + q, 0:width], ALU.add)
                elif ends:
                    i = e.memset(TY[:], 0.0)
                if ends:
                    i.then_inc(bd, 1)
                i = e.tensor_tensor(ACC[:, bass.ds(wv, width)], ACC[:, bass.ds(wv, width)],
                                    PS[:, q, 0:width], ALU.add).then_inc(acc, 1)
                e.reg_add(na, na, 1)
                return i

            def step(b, s, it, last):
                lo, hi = get(b, s, it, last)
                kl = keys[:, bass.ds(b * 4, 4)]
                with e.If(lo + width < hi):
                    e.wait_ge(kx, e.snap(nk))
                    linked(e.tensor_scalar(KX[:], kl, float(width), None, ALU.subtract))
                    with e.Fori(lo + width, hi, width) as wv:
                        e.wait_ge(kx, e.snap(nk))
                        sel(e, s, KX[:], b).then_inc(oh, 1)
                        e.reg_add(nu, nu, 1)
                        accumulate(s % 2, wv, False)
                        linked(e.tensor_scalar(KX[:], KX[:], float(width), None, ALU.subtract))
                e.end_ifs()
                sel(e, s, kl, b).then_inc(oh, 1)
                accumulate((s + 1) % 2, e.snap(wp, min_val=0, max_val=NN + 1))
                e.reg_add(nu, nu, 1)
                e.reg_mov(wp, lo)
                if rank:
                    e.wait_ge(low, b + 2)
                    for r in range(4):
                        i = e.tensor_tensor_reduce(PR[0][:, 98 * r:98 * r + 98], PS[:, 4, 98 * r:98 * r + 98],
                                                   OH[s % 2][:, 98 * r:98 * r + 98], 1.0, 0.0, ALU.mult, ALU.add,
                                                   PF[s % 2][:, r:r + 1])
                    i.then_inc(rd, 1)
                    e.wait_ge(rd, b * 2 + 1)
                    e.tensor_copy(POS[:, bass.ds(b * 4, 4)], PF[s % 2][:]).then_inc(rd, 1)
                    e.wait_ge(sk, b + 1)
                    e.wait_ge(ready[s], it * rstep + rstep)
                    m = TP if last else 128
                    for r in range(4):
                        i = e.tensor_tensor_reduce(JK[0:m, r, :], feats(s)[0:m, r, 0:D], V3[0:m, :], 1.0, 0.0,
                                                   ALU.mult, ALU.add, SF[s % 2][0:m, r:r + 1])
                    i.then_inc(sr, 1)
            batches(e, step)
            accumulate(0, e.snap(wp, min_val=0, max_val=NN + 1))
            n_acc = e.snap(na)
            e.wait_ge(acc, n_acc)
            e.memset(TY[:], 0.0).then_inc(p.sem("edone"), 1)

        @p.on("tensor")
        def _(e):
            e.wait_ge(dv, 1)
            ku = reg(e, "ku")
            e.reg_mov(ku, 1)
            get = unit_ranges(e, part)
            if count:
                e.matmul(PS[0:1, 3, 0:width], ONE[:, 0:1], SEL[1][:, 0, :], start=True, stop=True)
            e.matmul(PS[:, 1, 0:width], ONE[:], SEL[1][:, 0, :], start=True, stop=True).then_inc(mmd, 1)
            if rank:
                e.matmul(PS[:, 4, 0:392], ID[:], BASE, start=True, stop=False, skip_group_check=True).then_inc(low, 1)

            def unit(s, m):
                k = e.snap(ku)
                e.wait_ge(oh, k)
                e.wait_ge(acc, k)
                if count and not rank:
                    for r in range(4):
                        e.matmul(PS[0:1, 2 + s % 2, 0:width], ONE[0:m, 0:1], SEL[s % 2][0:m, r, :],
                                 start=(r == 0), stop=(r == 3))
                for r in range(4):
                    i = e.matmul(PS[:, s % 2, 0:width], feats(s)[0:m, r, 0:D], SEL[s % 2][0:m, r, :],
                                 start=(r == 0), stop=(r == 3))
                if rank:
                    e.wait_ge(ohb, k)
                    for r in range(4):
                        i = e.matmul(PS[0:1, 2 + s % 2, 0:width], ONB[0:m, 0:1], SELB[0:m, r, :],
                                     start=(r == 0), stop=(r == 3))
                i.then_inc(mmd, 1)
                e.reg_add(ku, ku, 1)

            def step(b, s, it, last):
                m = TP if last else 128
                lo, hi = get(b, s, it, last)
                e.wait_ge(ready[s], it * rstep + rstep)
                with e.If(lo + width < hi):
                    with e.Fori(lo + width, hi, width):
                        unit(s, m)
                e.end_ifs()
                if rank:
                    e.wait_ge(ohr, b + 1)
                    e.matmul(PS[:, 4, 0:392], LOW[0:m, :], OH[s % 2][0:m, :], start=False, stop=False,
                             skip_group_check=True).then_inc(low, 1)
                unit(s, m)
                if rank and not last:
                    e.wait_ge(rd, b * 2 + 1)
                    e.matmul(PS[:, 4, 0:392], UPI, OH[s % 2], start=False, stop=False, skip_group_check=True)
            batches(e, step)

        if rank:
            NA, AD = [p.tile([128, 4]) for _ in range(2)], [p.tile([128, 392], BF16) for _ in range(2)]
            na, ad = p.sem("na"), p.sem("ad")

            @p.on("scalar")
            def _(e):
                e.activation(R[0:1, :], ONE[0:1, 0:1].to_broadcast([1, NC]), ACT.Copy, scale=0.0).then_inc(rz, 1)

                get = unit_ranges(e, part)
                for _ in range(2):
                    e.nop().then_inc(sk, 1)
                kb = reg(e, "kb")
                e.reg_mov(kb, 1)

                def again(s):
                    k = e.snap(kb)
                    e.wait_ge(oh, k)
                    e.wait_ge(mmd, k)
                    e.activation(SELB[:], SEL[s % 2][:], ACT.Copy).then_inc(ohb, 1)
                    e.reg_add(kb, kb, 1)

                def step(b, s, it, last):
                    lo, hi = get(b, s, it, last)
                    e.activation(NA[s % 2][:], AW[:, bass.ds(b * 4, 4)], ACT.Copy, scale=-1.0).then_inc(na, 1)
                    e.wait_ge(na, b + 1)
                    for r in range(4):
                        i = e.activation(AD[s % 2][:, 98 * r:98 * r + 98], IOA, ACT.Abs, bias=NA[s % 2][:, r:r + 1])
                    i.then_inc(ad, 1)
                    if not (isinstance(b, int) and b == 0):
                        again(s + 1)
                    e.wait_ge(ad, b + 1)
                    e.wait_ge(low, b + 1)
                    e.activation(OH[s % 2], AD[s % 2][:], ACT.Relu, bias=ONE[:, 0:1], scale=-1.0).then_inc(ohr, 1)
                    if not (isinstance(b, int) and b == 0):
                        e.wait_ge(sr, b)
                        e.activation(SREL[:, bass.ds((b - 1) * 4, 4)], SF[(s + 1) % 2][:], ACT.Copy).then_inc(sk, 1)
                    with e.If(lo + width < hi):
                        with e.Fori(lo + width, hi, width):
                            again(s)
                    e.end_ifs()
                for s in range(UN):
                    step(s, s, 0, False)
                if NIT > 1:
                    with e.Fori(1, NIT) as it:
                        for s in range(UN):
                            step(it * UN + s, s, it, False)
                step(NBF, 0, NIT, True)
                again(0)
                e.wait_ge(sr, NR)
                e.activation(SREL[:, 4 * NBF:4 * NR], SF[0][:], ACT.Copy).then_inc(sk, 1)
                e.wait_ge(sk, NR + 2)
        return bd

    def load_ea(p, bd):
        ready = [p.sem(f"ea{s}") for s in range(UN)]

        @p.on("sync")
        def _(e):
            v = ea[0:NBF * BE, :].rearrange("(b p r) f -> b p (r f)", p=128, r=4)
            t = ea[NBF * BE:NE, :].rearrange("(p r) f -> p (r f)", r=4)

            def one(b, s):
                e.dma_start(XR[:, s * BE:(s + 1) * BE], v[bass.ds(b, 1)].rearrange("b p k -> (b p) k")).then_inc(ready[s], 16)
            for s in range(UN):
                one(s, s)
            if NIT > 1:
                with e.Fori(1, NIT) as it:
                    for s in range(UN):
                        e.wait_ge(bd, (it - 1) * UN + (s + 2))
                        one(it * UN + s, s)
            e.wait_ge(bd, (NIT - 1) * UN + 2)
            e.dma_start(XR[0:TP, 0:BE], t).then_inc(ready[0], 16)
            for s in range(UN):
                e.wait_ge(ready[s], 16 * (NIT + (s == 0)))
        return ready

    def gather(p, bd, table, idx, wide):
        ready = [p.sem(f"g{s}") for s in range(UN)]

        @p.on("gpsimd")
        def _(e):
            for b in range(NR):
                s = b % UN
                m = TP if b == NBF else 128
                if b >= UN:
                    e.wait_ge(bd, b - UN + 2)
                for r in range(4):
                    c = 4 * b + r
                    e.indirect_dma_start(GS[0:m, s, r, 0:wide], None, table,
                                         bass.IndirectOffsetOnAxis(ap=idx[0:m, c:c + 1].bitcast(U32), axis=0)
                                         ).then_inc(ready[s], 16)
            for s in range(UN):
                e.wait_ge(ready[s], 64 * (NIT + (s == 0)))
        return ready

    def p_l0():
        p = Phase()
        ready = load_ea(p, p.sem("bd"))
        edge_pass(p, 48, 0, KLD[:], lambda s: EA[:, s], ready, 16, AB[:, 0, :], rank=True)
        rd = p.sem("rd")
        sc = [p.sem(f"sc{i}") for i in range(4)]

        @p.on("gpsimd")
        def _(e):
            e.memset(R[32:33, :], M0).then_inc(p.sem("mi"), 1)
            e.memset(R[64:65, :], 0.0).then_inc(p.sem("mi"), 1)
            e.wait_ge(p.sem("mi"), 2)
            for b in range(NR):
                m = TP if b == NBF else 128
                e.wait_ge(rd, 2 * b + 2)
                for r in range(4):
                    c = 4 * b + r
                    e.indirect_dma_start(sortd, bass.IndirectOffsetOnAxis(ap=POS[0:m, c:c + 1].bitcast(U32), axis=0),
                                         PAY[0:m, c, :], None).then_inc(sc[r], 16)
            for r in range(4):
                e.wait_ge(sc[r], 16 * NR)
        l0_nodes(p)
        p.run()

    def rowsl(ap, g):
        n = grows[g]
        return ap[512 * g:512 * g + 4 * n, :].rearrange("(p j) f -> p (j f)", j=4)

    def jp(ap, g):
        return ap[:, 512 * g:512 * g + 4 * grows[g]].rearrange("f (p j) -> f j p", j=4)

    class Norm:

        def __init__(self, p, tag):
            self.p, self.t = p, tag
            self.st = [p.tile([128, 4, 6]) for _ in range(2)]
            self.mv = [p.tile([128, 4, 2]) for _ in range(2)]
            self.sd = [p.tile([128, 4]) for _ in range(2)]
            self.rs = [p.tile([128, 4]) for _ in range(2)]
            self.nm = [p.tile([128, 4]) for _ in range(2)]
            self.a, self.b, self.c, self.d, self.e_, self.f = (p.sem(f"{tag}{i}") for i in range(6))

        def moments(self, e, xt, g):
            n, s = grows[g], g % 2
            for j in range(4):
                i = e.bn_stats(self.st[s][0:n, j, :], xt[0:n, j, :])
            i.then_inc(self.a, 1)
            e.wait_ge(self.a, g + 1)
            if g >= 2:
                e.wait_ge(self.f, g - 1)
            for j in range(4):
                i = e.bn_aggr(self.mv[s][0:n, j, :], self.st[s][0:n, j, :])
            i.then_inc(self.b, 1)
            e.wait_ge(self.b, g + 1)
            e.tensor_scalar(self.sd[s][0:n, :], self.mv[s][0:n, :, 1], EPS, None, ALU.add).then_inc(self.c, 1)

        def root(self, e, g):
            n, s = grows[g], g % 2
            e.wait_ge(self.c, g + 1)
            e.activation(self.sd[s][0:n, :], self.sd[s][0:n, :], ACT.Sqrt).then_inc(self.d, 1)

        def scale(self, e, g):
            n, s = grows[g], g % 2
            e.wait_ge(self.d, g + 1)
            e.reciprocal(self.rs[s][0:n, :], self.sd[s][0:n, :]).then_inc(self.e_, 1)
            e.wait_ge(self.e_, 2 * g + 1)
            e.scalar_tensor_tensor(out=self.nm[s][0:n, :], in0=self.mv[s][0:n, :, 0], scalar=-1.0,
                                   in1=self.rs[s][0:n, :], op0=ALU.mult, op1=ALU.mult).then_inc(self.e_, 1)

        def apply(self, e, out, xt, g):
            n, s = grows[g], g % 2
            e.wait_ge(self.e_, 2 * g + 2)
            for j in range(4):
                i = e.activation(out[0:n, j, 0:D], xt[0:n, j, :], ACT.Relu, bias=self.nm[s][0:n, j:j + 1],
                                 scale=self.rs[s][0:n, j:j + 1])
            i.then_inc(self.f, 1)

    def l0_nodes(p):
        XT = [XR[:, 1024 + 512 * i:1536 + 512 * i].rearrange("p (j f) -> p j f", j=4) for i in range(2)]
        XT += [p.tile([128, 4, D]) for _ in range(2)]
        H0 = [XR[:, 2048 + 512 * i:2560 + 512 * i].rearrange("p (j f) -> p j f", j=4) for i in range(2)]
        HID = [GF[:, 512 * m:512 * m + 512] if m < 6 else XR[:, 512 * (m - 6):512 * (m - 5)] for m in range(8)]
        W1S = B0[:, LISTEND:LISTEND + 2048].rearrange("p (k h) -> p k h", k=2)
        W2S = B0[:, LISTEND + 2048:LISTEND + 3072].rearrange("p (m f) -> p m f", m=8)
        H0T = [B0[:, LISTEND + 3072 + 512 * i:LISTEND + 3584 + 512 * i] for i in range(2)]
        assert LISTEND + 4096 <= NC and NR * 4 >= 2 * 4 * TW or NBF < 300
        HT = [p.tile([128, 4, TW]) if NBF < 300 else AW[:, 528 * i:528 * i + 528].rearrange("p (j f) -> p j f", j=4)
              for i in range(2)]
        H1T = [B0[:, LISTEND - 784:LISTEND - 272]]
        UT, B1, B1E, AT, V12, B2 = (p.tile([16, 1]), p.tile([128, 8]), p.tile([128, 8]),
                                    p.tile([128, 2]), p.tile([128, 2]), p.tile([1, 128]))
        WW = p.tile([128, 128])
        W1U = XR[0:16, 2048:3072]
        ed, wl, dd = p.sem("edone"), p.sem("wl"), p.sem("dd")
        degd = dram("degd", (min(NP, NC),))
        xl = [p.sem(f"xl{i}") for i in range(4)]
        xs, hs = [p.sem(f"xs{i}") for i in range(4)], [p.sem(f"hs{i}") for i in range(2)]
        n0, n1 = Norm(p, "n"), Norm(p, "m")
        t0, c0, ph, hd, py, pb = (p.sem(k) for k in ("t0", "c0", "ph", "hd", "py", "pb"))
        t1, c1, t2, c2, pre, prd = (p.sem(k) for k in ("t1", "c1", "t2", "c2", "pre", "prd"))

        @p.on("sync")
        def _(e):
            for t, d in ((UT[:], u.rearrange("o k -> k o")),
                         (B1[:], b1.rearrange("(m p) -> p m", p=128)), (WW[:], w),
                         (AT[:], att[0:256].rearrange("(k p) -> p k", p=128)), (B2[:], b2.rearrange("(o f) -> o f", o=1)),
                         (W1S, W1[0:256, :].rearrange("(k p) h -> p k h", p=128)),
                         (W2S, W2.rearrange("(m p) f -> p m f", p=128))):
                e.dma_start(t, d, allow_slow_non_contiguous=True).then_inc(wl, 16)
            e.wait_ge(ed, 1)
            e.dma_start(W1U, W1[256:272, :]).then_inc(wl, 16)
            e.dma_start(degd.rearrange("(o f) -> o f", o=1), R[0:1, 0:NP if NP <= NC else NC]).then_inc(dd, 16)
            def load(g):
                n = grows[g]
                e.dma_start(XT[g % 4][0:n].rearrange("p j f -> p (j f)"), rowsl(x, g)).then_inc(xl[g % 4], 16)
            for g in range(min(4, NG)):
                load(g)
            for g in range(NG):
                store(e, g)
                if g + 4 < NG:
                    e.wait_ge(n1.f, g + 1)
                    e.wait_ge(xs[g % 4], 16 * (g // 4 + 1))
                    load(g + 4)
            e.wait_ge(dd, 16)
            n = grows[NG - 1]
            if NG > 1:
                e.dma_start(DIN[:, 0:4 * (NG - 1)].rearrange("p (g j) -> p g j", j=4),
                            degd[0:512 * (NG - 1)].rearrange("(g p j) -> p g j", p=128, j=4)).then_inc(dd, 16)
            e.dma_start(DIN[0:n, 4 * (NG - 1):4 * NG],
                        degd[512 * (NG - 1):512 * (NG - 1) + 4 * n].rearrange("(p j) -> p j", j=4)).then_inc(dd, 16)
            e.wait_ge(dd, 48 if NG > 1 else 32)
            for i in range(4):
                e.wait_ge(xs[i], 16 * ((NG + 3 - i) // 4))
            for i in range(2):
                e.wait_ge(hs[i], 16 * ((NG + 1 - i) // 2))

        def store(e, g):
            n = grows[g]
            e.wait_ge(pb, g + 1)
            e.dma_start(rowsl(x1d, g), XT[g % 4][0:n].rearrange("p j f -> p (j f)")).then_inc(xs[g % 4], 16)
            e.wait_ge(c2, g + 1)
            e.dma_start(rowsl(t1d, g), HT[g % 2][0:n].rearrange("p j f -> p (j f)")).then_inc(hs[g % 2], 16)

        @p.on("tensor")
        def _(e):
            e.wait_ge(wl, 16 * 8)
            e.wait_ge(ed, 1)
            for m in range(8):
                e.matmul(PS[:, 6, m:m + 1], W1U[:, 128 * m:128 * m + 128], UT[:], start=True, stop=True)
            e.matmul(PS[:, 6, 8:9], WW[:], AT[:, 0:1], start=True, stop=True)
            e.matmul(PS[:, 6, 9:10], WW[:], AT[:, 1:2], start=True, stop=True).then_inc(pre, 1)

            def turn0(g):
                n = grows[g]
                e.wait_ge(n0.f, g + 1)
                if g:
                    e.wait_ge(c0, g)
                for j in range(4):
                    i = e.transpose(PS[:, 3, n * j:n * j + n], H0[g % 2][0:n, j, :], ID[0:n, 0:n])
                i.then_inc(t0, 1)

            def mlp(g):
                n = grows[g]
                e.wait_ge(c0, g + 1)
                if g == 0:
                    e.wait_ge(prd, 1)
                for m in range(8):
                    k = 8 * g + m
                    if k >= 2:
                        e.wait_ge(hd, k - 1)
                    e.matmul(PS[:, m % 2, 0:4 * n].rearrange("h (j p) -> h j p", j=4), W1S[:, 0, 128 * m:128 * m + 128],
                             jp(AB[:, 0, :], g), start=True, stop=False)
                    e.matmul(PS[:, m % 2, 0:4 * n], W1S[:, 1, 128 * m:128 * m + 128], H0T[g % 2][:, 0:4 * n],
                             start=False, stop=True).then_inc(ph, 1)
                if g:
                    e.wait_ge(pb, g)
                e.matmul(PS[0:n, 2, :], ONE[0:1, 0:n], B2[:].unsqueeze(1).to_broadcast([1, 4, D]), start=True, stop=False,
                         skip_group_check=True)
                for j in range(4):
                    for m in range(8):
                        if j == 0:
                            e.wait_ge(hd, 8 * g + m + 1)
                        i = e.matmul(PS[0:n, 2, 128 * j:128 * j + 128], HID[m][:, n * j:n * j + n], W2S[:, m, :],
                                 start=False, stop=(m == 7), skip_group_check=True)
                i.then_inc(py, 1)

            def turn1(g):
                n = grows[g]
                e.wait_ge(n1.f, g + 1)
                if g:
                    e.wait_ge(c1, g)
                for j in range(4):
                    i = e.transpose(PS[:, 5, n * j:n * j + n], HT[g % 2][0:n, j, 0:D], ID[0:n, 0:n])
                i.then_inc(t1, 1)
                e.wait_ge(c1, g + 1)
                if g:
                    e.wait_ge(c2, g)
                for j in range(4):
                    e.matmul(PS[0:n, 6, j:j + 1], H1T[0][:, n * j:n * j + n], V12[:, 0:1], start=True, stop=True)
                e.matmul(PS[0:1, 7, 0:4 * n], V12[:, 1:2], H1T[0][:, 0:4 * n], start=True, stop=True).then_inc(t2, 1)
            turn0(0)
            for g in range(NG):
                if g + 1 < NG:
                    turn0(g + 1)
                mlp(g)
                if g:
                    turn1(g - 1)
            turn1(NG - 1)

        @p.on("scalar")
        def _(e):
            def root0(g):
                n0.root(e, g)

            def app0(g):
                if g >= 2:
                    e.wait_ge(t0, g - 1)
                n0.apply(e, H0[g % 2], XT[g % 4], g)

            def hid(g):
                n = grows[g]
                if g == 0:
                    e.wait_ge(prd, 1)
                for m in range(8):
                    e.wait_ge(ph, 8 * g + m + 1)
                    e.activation(HID[m][:, 0:4 * n], PS[:, m % 2, 0:4 * n], ACT.Relu, bias=B1E[:, m:m + 1]).then_inc(hd, 1)

            def app1(g):
                if g >= 2:
                    e.wait_ge(hs[g % 2], 16 * (g // 2))
                n1.apply(e, HT[g % 2], XT[g % 4], g)
            root0(0)
            e.wait_ge(pre, 1)
            app0(0)
            if NG > 1:
                root0(1)
                app0(1)
            for g in range(NG):
                hid(g)
                if g + 2 < NG:
                    root0(g + 2)
                if g:
                    n1.root(e, g - 1)
                if g + 2 < NG:
                    app0(g + 2)
                if g:
                    app1(g - 1)
            n1.root(e, NG - 1)
            app1(NG - 1)

        @p.on("vector")
        def _(e):
            def first(g):
                e.wait_ge(xl[g % 4], 16 * (g // 4 + 1))
                n0.moments(e, XT[g % 4], g)
                n0.scale(e, g)

            def copy0(g):
                n = grows[g]
                e.wait_ge(t0, g + 1)
                e.tensor_copy(H0T[g % 2][:, 0:4 * n], PS[:, 3, 0:4 * n]).then_inc(c0, 1)

            def post(g):
                n = grows[g]
                e.wait_ge(py, g + 1)
                e.wait_ge(n0.f, g + 1)
                e.tensor_tensor(XT[g % 4][0:n], XT[g % 4][0:n], PS[0:n, 2, :].rearrange("p (j f) -> p j f", j=4),
                                ALU.add).then_inc(pb, 1)
                e.wait_ge(pb, g + 1)
                n1.moments(e, XT[g % 4], g)

            def tail(g):
                n = grows[g]
                e.wait_ge(t1, g + 1)
                e.tensor_copy(H1T[0][:, 0:4 * n], PS[:, 5, 0:4 * n]).then_inc(c1, 1)
                e.wait_ge(t2, g + 1)
                e.tensor_copy(HT[g % 2][0:n, :, D], PS[0:n, 6, 0:4])
                if g == 0:
                    e.wait_ge(dd, 16)
                e.tensor_copy(jp(R[0:1, :], g), PS[0:1, 7, 0:4 * n].rearrange("o (j p) -> o j p", j=4)).then_inc(c2, 1)
            e.wait_ge(ed, 1)
            e.memset(HT[0][:, :, D:TW], 0.0)
            e.memset(HT[1][:, :, D:TW], 0.0)
            e.wait_ge(pre, 1)
            e.tensor_copy(V12[:], PS[:, 6, 8:10])
            e.tensor_tensor(B1E[:], B1[:], PS[:, 6, 0:8], ALU.add).then_inc(prd, 1)
            first(0)
            if NG > 1:
                first(1)
            copy0(0)
            for g in range(NG):
                if g + 1 < NG:
                    copy0(g + 1)
                if g + 2 < NG:
                    first(g + 2)
                if g:
                    n1.scale(e, g - 1)
                    tail(g - 1)
                post(g)
            n1.scale(e, NG - 1)
            tail(NG - 1)
            e.wait_ge(c2, NG)

    FLAG = sb("FLAG", [1, 2], I32)
    FT = AB[0:1, 0, 0:NR]
    ONB3 = sb("ONB3", [3, 128], BF16)
    sdf = dram("sdf", (NC,))
    sdd = dram("sdd", (3, NC), BF16)

    def p_flag():
        p = Phase()
        c = p.sem("c")

        @p.on("vector")
        def _(e):
            link = chain(e, c)
            v = RNG[0:1, 0:2 * NR].rearrange("o (b t) -> o b t", t=2)
            link(e.tensor_tensor(FT, v[:, :, 1], v[:, :, 0], ALU.subtract))
            e.tensor_copy(FLAG[:, 1:2], FT[:, 0:1])
            link(e.tensor_reduce(FLAG[:, 0:1], FT, AX, ALU.max))
            e.wait_ge(ld, 32)
            link(e.tensor_copy(Q[0][:], T[:]))
            link(e.tensor_tensor(T[:], T[:], Q[0][:], ALU.subtract))
            link(e.tensor_copy(Q[1][:], T[:]))
            link(e.tensor_tensor(T[:], T[:], Q[1][:], ALU.subtract))
            e.tensor_copy(ONB3[:], ONE[0:3, :])
            e.tensor_copy(Q[2][:], T[:]).then_inc(pr, 1)
        NK = NC // 8
        T, Q = p.tile([8, NK]), [p.tile([8, NK], BF16) for _ in range(3)]
        ld, pr = p.sem("ld"), p.sem("pr")

        @p.on("sync")
        def _(e):
            e.dma_start(sdf.rearrange("(o f) -> o f", o=1), R[0:1, :]).then_inc(ld, 16)
            e.wait_ge(ld, 16)
            e.dma_start(T[:], sdf.rearrange("(p f) -> p f", p=8)).then_inc(ld, 16)
            e.wait_ge(pr, 1)
            for i in range(3):
                e.dma_start(sdd[i].rearrange("(p f) -> p f", p=8), Q[i][:]).then_inc(ld, 16)
            e.wait_ge(ld, 80)
        p.run()

    def p_l1():
        p = Phase()
        bd = p.sem("bd")
        fr, fz, s7, pg = (p.sem(k) for k in ("fr", "fz", "s7", "pg"))
        ear = load_ea(p, fr)
        gr = gather(p, fr, t1d[0:NN, :], IDX[:], TW)
        SW = [p.tile([128, 48]) for _ in range(2)]
        SDT = [p.tile([3, 48], BF16) for _ in range(3)]
        sdl, sdg = [p.sem(f"sd{i}") for i in range(3)], p.sem("sdg")
        s1, s2, s2a, s3, s4, s4a, s4b, s5, s6a, zz = (p.sem(k) for k in (
            "s1", "s2", "s2a", "s3", "s4", "s4a", "s4b", "s5", "s6a", "zz"))
        pu, pt, pr, pbc, pm = (p.sem(k) for k in ("pu", "pt", "pr", "pbc", "pm"))
        au, ac, acs, aw, kx = (p.sem(k) for k in ("au", "ac", "acs", "aw", "kx"))
        WD = 48
        NQ = [p.tile([128, 4, WD], BF16) for _ in range(2)]
        ZC = [p.tile([128, 4]) for _ in range(2)]
        U1 = [p.tile([128, 4, WD]) for _ in range(2)]
        LL = [p.tile([128, 4, WD]) for _ in range(6)]
        LM = [p.tile([128, 128]) for _ in range(2)]
        ZM = [p.tile([128, 1]) for _ in range(2)]
        MC = [p.tile([33, 2 * WD]) for _ in range(2)]
        DM = [p.tile([33, WD]) for _ in range(2)]
        CS = [p.tile([128, WD]) for _ in range(3)]
        T6 = p.tile([128, 2, WD])
        T6R = p.tile([65, WD])
        KX, TY = p.tile([128, 4]), p.tile([1, 1])
        M = R[32:33, :]
        DEN = R[64:65, :]

        def uv(i):
            return PS[:, i, 0:4 * WD].rearrange("p (r n) -> p r n", r=4)

        def sd_load(e, j, lo):
            e.dma_start(SDT[j][:], sdd[:, bass.ds(lo, WD)]).then_inc(sdl[j], 16)

        def d1(e, i, s, kl, b):
            e.tensor_tensor(ZC[i][:], GS[:, s, :, D], SREL[:, bass.ds(b * 4, 4)], ALU.add)
            for r in range(4):
                n = e.tensor_scalar(NQ[i][:, r, :], IOB[:, 0:WD], kl[:, r:r + 1], -BIG, ALU.not_equal, ALU.mult)
            n.then_inc(s1, 1)

        def t1_(e, i, j):
            u4 = uv(i)
            e.matmul(u4, IDB[:], NQ[i][:], start=True, stop=False)
            e.matmul(u4, ONB3[:], SDT[j][:].unsqueeze(1).to_broadcast([3, 4, WD]), start=False, stop=True
                     ).then_inc(pu, 1)

        def a1(e, i):
            for r in range(4):
                n = e.activation(U1[i][:, r, :], uv(i)[:, r, :], ACT.Identity, bias=ZC[i][:, r:r + 1])
            n.then_inc(au, 1)

        def d2(e, i, l, n):
            e.scalar_tensor_tensor(out=LL[l][:], in0=U1[i][:], scalar=0.01, in1=U1[i][:], op0=ALU.mult, op1=ALU.max
                                   ).then_inc(s2a, 1)
            e.wait_ge(s2a, n)
            e.tensor_reduce(LM[i][:, 0:WD], LL[l][:].rearrange("p r n -> p n r"), AX, ALU.max).then_inc(s2, 1)

        def t2_(e, i, m):
            e.transpose(PS[:, 2, 0:m], LM[i][0:m, :], ID[0:m, 0:m]).then_inc(pt, 1)

        def d3(e, i, m):
            e.tensor_reduce(ZM[i][:], PS[:, 2, 0:m], AX, ALU.max).then_inc(s3, 1)

        def t3_(e, i):
            e.matmul(PS[0:1, 6, 0:WD], ZM[i][:], ID[:, 0:WD], start=True, stop=True).then_inc(pr, 1)

        def d4(e, i, w_, n):
            mn = MC[i][32:33, 0:WD]
            e.tensor_tensor(mn, M[:, bass.ds(w_, WD)], PS[0:1, 6, 0:WD], ALU.max).then_inc(s4a, 1)
            e.wait_ge(s4a, n)
            e.tensor_tensor(DM[i][32:33, :], M[:, bass.ds(w_, WD)], mn, ALU.subtract).then_inc(s4b, 1)
            e.wait_ge(s4b, n)
            e.tensor_scalar(M[:, bass.ds(w_, WD)], mn, 1.0, None, ALU.mult).then_inc(s4, 1)

        def a2(e, i):
            e.activation(MC[i][32:33, WD:2 * WD], DM[i][32:33, :], ACT.Exp).then_inc(ac, 1)

        def t4_(e, i):
            e.matmul(PS[:, 3 + 4 * i, 0:2 * WD], ONE[32:33, :], MC[i][32:33, :], start=True, stop=True).then_inc(pbc, 1)

        def a3(e, i, j):
            e.activation(CS[j][:], PS[:, 3 + 4 * i, WD:2 * WD], ACT.Copy).then_inc(acs, 1)

        def d5(e, i, l):
            e.tensor_tensor(LL[l][:], LL[l][:], PS[:, 3 + 4 * i, 0:WD].unsqueeze(1).to_broadcast([128, 4, WD]),
                            ALU.subtract).then_inc(s5, 1)

        def a4(e, l, more=None):
            e.activation(LL[l][:], LL[l][:], ACT.Exp).then_inc(aw, 1)
            if more:
                e.activation(MC[1][32:33, 0:1], MC[0][32:33, 0:1], ACT.Copy).then_inc(more, 1)

        def t5g(e, i, l, s, m):
            for r in range(4):
                n = e.matmul(PS[:, 4 + i, 0:WD], GS[0:m, s, r, 0:D], LL[l][0:m, r, :], start=(r == 0), stop=(r == 3))
            n.then_inc(pg, 1)

        def t5e(e, i, l, s, m, free):
            for r in range(4):
                n = e.matmul(PS[:, 4 + i, WD:2 * WD], EA[0:m, s, r, :], LL[l][0:m, r, :], start=(r == 0), stop=(r == 3))
            n.then_inc(free, 1)
            e.matmul(PS[0:1, 4 + i, 2 * WD:3 * WD], ONE[0:m, 0:1], SW[i][0:m, :], start=True, stop=True).then_inc(pm, 1)

        def d7(e, i, l):
            e.tensor_reduce(SW[i][:], LL[l][:].rearrange("p r n -> p n r"), AX, ALU.add).then_inc(s7, 1)

        def d6(e, i, j, w_, n, done):
            cur = AB[:, :, bass.ds(w_, WD)]
            dn = DEN[:, bass.ds(w_, WD)]
            e.tensor_tensor(T6R[64:65, :], dn, CS[j][64:65, :], ALU.mult)
            e.tensor_tensor(T6[:], cur, CS[j][:].unsqueeze(1).to_broadcast([128, 2, WD]), ALU.mult).then_inc(s6a, 1)
            e.wait_ge(s6a, n)
            e.tensor_tensor(dn, T6R[64:65, :], PS[0:1, 4 + i, 2 * WD:3 * WD], ALU.add)
            e.tensor_tensor(cur, T6[:], PS[:, 4 + i, 0:2 * WD].rearrange("p (a n) -> p a n", a=2), ALU.add
                            ).then_inc(done, 1)

        def fast(e, ops, begin=None, end=None):
            def at(k, s, it):
                if begin:
                    begin(k, s, it)
                for op, lag in ops:
                    b = k - lag
                    if isinstance(b, int) and not 0 <= b <= NBF:
                        continue
                    r = b // UN if isinstance(b, int) else it + (s - lag) // UN
                    op(b, (s - lag) % UN, r, s)
                if end:
                    end(k, s)
            for k in range(-1, UN):
                at(k, k % UN, 0)
            if NIT > 1:
                with e.Fori(1, NIT) as it:
                    for s in range(UN):
                        at(it * UN + s, s, it)
            for k in range(NBF, NBF + 4):
                at(k, k % UN, NIT)

        def need(e, sem, b, back=0, more=0):
            n = b + 1 - back
            if not isinstance(n, int) or n > 0:
                e.wait_ge(sem, n + more)

        def rows(k):
            return TP if isinstance(k, int) and k == NBF else 128

        def general(e, unit, first=None, after=None):
            n = reg(e, "units")
            e.reg_mov(n, 1)
            get = unit_ranges(e, 0)

            def step(b, s, it, last):
                lo, hi = get(b, s, it, last)
                if first:
                    first(b, s, it)
                with e.Fori(lo, hi, WD) as w_:
                    unit(s, w_, e.snap(n), TP if last else 128, b, it)
                    e.reg_add(n, n, 1)
                if after:
                    after()
            batches(e, step)

        def flag(e):
            return nc.values_load_multi_w_load_instructions(
                FLAG[0:1, 0:1], engines=[e.engine], min_val=0, max_val=NN + 1,
                skip_runtime_bounds_check_because="a difference of node numbers")[1][0]

        @p.on("vector")
        def _(e):
            e.memset(AB[:, 0, :], 0.0)
            for t in LM:
                e.memset(t[:], 0.0)
            e.memset(TY[:], 0.0).then_inc(zz, 1)
            e.wait_ge(zz, 1)
            e.wait_ge(za, 1)
            e.nop().then_inc(bd, 1)
            e.nop().then_inc(fr, 1)
            fl = flag(e)
            w1, w2, w3 = reg(e, "w1"), reg(e, "w2"), reg(e, "w3")
            nk = reg(e, "nkx")
            with e.If(fl <= WD):
                e.reg_mov(w1, 0)
                e.reg_mov(w2, 0)
                e.reg_mov(w3, 0)
                held = {}

                def begin(k, s, it):
                    if s == 0 and not (isinstance(k, int) and k > NBF):
                        n = 2 if isinstance(k, int) and k == NBF else 2 * UN
                        held["lo"] = ranges(e, 0, k * 2, n)[0::2]

                def end(k, s):
                    e.reg_mov(w3, w2)
                    e.reg_mov(w2, w1)
                    if isinstance(k, int) and not 0 <= k <= NBF:
                        return
                    e.reg_mov(w1, held["lo"][s])

                def v1(b, s, r, _):
                    e.wait_ge(gr[s], r * 64 + 64)
                    need(e, au, b, 2)
                    d1(e, s % 2, s, KLD[:, bass.ds(b * 4, 4)], b)

                def v2(b, s, r, _):
                    need(e, au, b)
                    need(e, pm, b, 6)
                    d2(e, s % 2, s, b + 1)

                def v3(b, s, r, _):
                    need(e, pt, b)
                    d3(e, s % 2, rows(b))

                def v4(b, s, r, _):
                    need(e, pr, b)
                    need(e, s4, b, 1)
                    need(e, pbc, b, 2)
                    d4(e, s % 2, e.snap(w1, min_val=0, max_val=NN + 1), b + 1)

                def v5(b, s, r, _):
                    need(e, acs, b)
                    d5(e, s % 2, s)

                def v7(b, s, r, _):
                    need(e, aw, b)
                    need(e, pm, b, 2)
                    d7(e, s % 2, s)

                def v6(b, s, r, _):
                    need(e, pm, b)
                    need(e, bd, b, 1, 1)
                    d6(e, s % 2, s % 3, e.snap(w3, min_val=0, max_val=NN + 1), b + 1, bd)
                fast(e, [(v4, 1), (v2, 0), (v7, 2), (v1, -1), (v3, 0), (v5, 1), (v6, 3)], begin, end)
                e.wait_ge(bd, NR + 1)
            with e.Else():
                e.reg_mov(nk, 0)

                def before(b, s, it):
                    e.wait_ge(gr[s], it * 64 + 64)
                    e.tensor_copy(KX[:], KLD[:, bass.ds(b * 4, 4)]).then_inc(kx, 1)
                    e.reg_add(nk, nk, 1)

                def unit(s, w_, n, m, b, it):
                    e.wait_ge(kx, e.snap(nk))
                    d1(e, 0, s, KX[:], b)
                    e.wait_ge(s1, n)
                    e.tensor_scalar(KX[:], KX[:], float(WD), None, ALU.subtract).then_inc(kx, 1)
                    e.reg_add(nk, nk, 1)
                    e.wait_ge(au, n)
                    d2(e, 0, 0, n)
                    e.wait_ge(pt, n)
                    d3(e, 0, m)
                    e.wait_ge(pr, n)
                    d4(e, 0, w_, n)
                    e.wait_ge(acs, n)
                    d5(e, 0, 0)
                    e.wait_ge(aw, n)
                    d7(e, 0, 0)
                    e.wait_ge(pm, n)
                    d6(e, 0, 0, w_, n, zz)
                    e.wait_ge(zz, n + 1)

                def after():
                    e.memset(TY[:], 0.0).then_inc(fr, 1)
                general(e, unit, before, after)

        @p.on("tensor")
        def _(e):
            fl = flag(e)
            e.wait_ge(zz, 1)
            with e.If(fl <= WD):
                def w1_(b, s, r, _):
                    need(e, s1, b)
                    need(e, au, b, 2)
                    e.wait_ge(sdl[s % 3], 16 * (2 * r + s // 3) + 16)
                    t1_(e, s % 2, s % 3)

                def w2_(b, s, r, _):
                    need(e, s2, b)
                    need(e, s3, b, 1)
                    t2_(e, s % 2, rows(b))

                def w3_(b, s, r, _):
                    need(e, s3, b)
                    need(e, s4, b, 1)
                    t3_(e, s % 2)

                def w4_(b, s, r, _):
                    need(e, ac, b)
                    need(e, s5, b, 2)
                    need(e, acs, b, 2)
                    t4_(e, s % 2)

                def w5_(b, s, r, _):
                    need(e, aw, b)
                    need(e, bd, b, 2, 1)
                    t5g(e, s % 2, s, s, rows(b))

                def w6_(b, s, r, _):
                    e.wait_ge(ear[s], r * 16 + 16)
                    need(e, s7, b)
                    t5e(e, s % 2, s, s, rows(b), fr)
                fast(e, [(w4_, 1), (w2_, 0), (w5_, 2), (w3_, 0), (w1_, -1), (w6_, 2)])
            with e.Else():
                def unit(s, w_, n, m, b, it):
                    e.wait_ge(s1, n)
                    e.wait_ge(sdl[0], n * 16)
                    t1_(e, 0, 0)
                    e.wait_ge(s2, n)
                    t2_(e, 0, m)
                    e.wait_ge(s3, n)
                    t3_(e, 0)
                    e.wait_ge(ac, n)
                    t4_(e, 0)
                    e.wait_ge(aw, n)
                    e.wait_ge(ear[s], it * 16 + 16)
                    e.wait_ge(s7, n)
                    t5g(e, 0, 0, s, m)
                    t5e(e, 0, 0, s, m, fz)
                general(e, unit)

        za = p.sem("za")

        @p.on("scalar")
        def _(e):
            e.activation(AB[:, 1, :], ONE[:, 0:1].to_broadcast([128, NC]), ACT.Copy, scale=0.0).then_inc(za, 1)
            fl = flag(e)
            e.wait_ge(zz, 1)
            with e.If(fl <= WD):
                nx = {}

                def begin(k, s, it):
                    if isinstance(k, int) and k < 0:
                        for b, v in enumerate(ranges(e, 0, 0, 4)[0::2]):
                            sd_load(e, b, v)
                    elif s == 0 and not (isinstance(k, int) and k >= NBF):
                        v = ranges(e, 0, k * 2 + 4, 2 * UN)
                        for i in range(UN):
                            nx[i] = v[2 * i]

                def x0(b, s, r, at):
                    if isinstance(b, int) and b < 2:
                        return
                    need(e, pu, b, 3)
                    sd_load(e, s % 3, nx[at])

                def x1(b, s, r, _):
                    need(e, pu, b)
                    need(e, s2, b, 2)
                    a1(e, s % 2)

                def x2(b, s, r, _):
                    need(e, s4, b)
                    a2(e, s % 2)

                def x3(b, s, r, _):
                    need(e, pbc, b)
                    need(e, bd, b, 3, 1)
                    a3(e, s % 2, s % 3)

                def x4(b, s, r, _):
                    need(e, s5, b)
                    a4(e, s)
                fast(e, [(x2, 1), (x3, 1), (x1, -1), (x0, -2), (x4, 1)], begin)
                for i in range(3):
                    e.wait_ge(sdl[i], 16 * len(range(i, NR + 1, 3)))
            with e.Else():
                e.nop().then_inc(sdg, 1)

                def unit(s, w_, n, m, b, it):
                    e.wait_ge(sdg, n)
                    sd_load(e, 0, w_)
                    e.wait_ge(pu, n)
                    a1(e, 0)
                    e.wait_ge(s4, n)
                    a2(e, 0)
                    e.wait_ge(pbc, n)
                    a3(e, 0, 0)
                    e.wait_ge(s5, n)
                    a4(e, 0, sdg)
                general(e, unit)
        p.run()

    XT3 = [GF[:, 512 * i:512 * i + 512].rearrange("p (j f) -> p j f", j=4) for i in range(3)]
    GI3 = [GF[:, 1536 + 528 * i:1536 + 528 * i + 512].rearrange("p (j f) -> p j f", j=4) for i in range(3)]
    HTT = [XR[:, 512 * i:512 * i + 512] for i in range(2)]
    HO = [XR[:, 1024 + 512 * i:1536 + 512 * i].rearrange("p (j f) -> p j f", j=4) for i in range(2)]
    TO = [XR[:, 2048 + 512 * i:2560 + 512 * i].rearrange("p (j f) -> p j f", j=4) for i in range(2)]

    def flat(t, n):
        return t[0:n].rearrange("p j f -> p (j f)")

    def bk(i, g):
        return (0, 1, 2)[i] if g % 2 == 0 else (4, 5, 7)[i]

    def bank(i, n, g):
        return PS[0:n, bk(i, g), :].rearrange("p (j f) -> p j f", j=4)

    def weights(p, specs, rows=()):
        wl, wt, wc = p.sem("wl"), p.sem("wt"), p.sem("wc")
        raw = [p.tile([128, 128]) for _ in specs]
        done = [p.tile([128, 128]) for _ in specs]
        rw = [p.tile([1, 128]) for _ in rows]
        rep = [p.tile([128, 128]) for _ in rows]

        @p.on("sync")
        def _(e):
            for t, d in zip(raw, specs):
                e.dma_start(t[:], d).then_inc(wl, 16)
            for t, d in zip(rw, rows):
                e.dma_start(t[:], d.rearrange("(o f) -> o f", o=1)).then_inc(wl, 16)
        n = len(specs) + len(rows)

        @p.on("tensor")
        def _(e):
            e.wait_ge(wl, 16 * n)
            for k, t in enumerate(raw):
                if k:
                    e.wait_ge(wc, k)
                e.transpose(PS[:, 7, 0:128], t[:], ID[:]).then_inc(wt, 1)
            for k, t in enumerate(rw):
                e.wait_ge(wc, len(raw) + k)
                e.matmul(PS[:, 7, 0:128], ONE[0:1, :], t[:], start=True, stop=True).then_inc(wt, 1)

        @p.on("vector")
        def _(e):
            for k, t in enumerate(done + rep):
                e.wait_ge(wt, k + 1)
                e.tensor_copy(t[:], PS[:, 7, 0:128]).then_inc(wc, 1)
        return raw, done, rw, rep, wc, n

    def nodes(p, xin, hin, xout, turned, mm, evac, combine, finish, souts, ready, norm="act"):
        xl, gl = [p.sem(f"xl{i}") for i in range(3)], [p.sem(f"gl{i}") for i in range(3)]
        tp_, tc, pmm, ev, cb, fi = (p.sem(k) for k in ("tp", "tc", "pmm", "ev", "cb", "fi"))
        nr = Norm(p, "q")
        st = [[p.sem(f"st{a}_{i}") for i in range(3)] for a in range(len(souts) + 1)]
        outs = ([(xout, XT3, cb)] if xout is not None else []) + souts

        @p.on("sync")
        def _(e):
            def loadx(g):
                if g >= 3:
                    e.wait_ge(fi, g - 2)
                    if xout is not None:
                        e.wait_ge(st[0][g % 3], 16 * (g // 3))
                e.dma_start(flat(XT3[g % 3], grows[g]), rowsl(xin, g)).then_inc(xl[g % 3], 16)

            def loadh(g):
                if hin is None or g >= NG:
                    return
                if g >= 3:
                    e.wait_ge(cb, g - 2)
                n = grows[g]
                h = hin[512 * g:512 * g + 4 * n, :].rearrange("(p j) f -> p j f", j=4)[:, :, 0:D]
                e.dma_start(GI3[g % 3][0:n], h).then_inc(gl[g % 3], 16)
            loadh(0)
            loadh(1)
            for g in range(NG):
                loadh(g + 2)
                loadx(g)

        @p.on("gpsimd")
        def _(e):
            for g in range(NG):
                n = grows[g]
                for a, (d, ring, sem) in enumerate(outs):
                    e.wait_ge(fi if sem is None else sem, g + 1)
                    e.dma_start(rowsl(d, g), flat(ring[g % len(ring)], n)).then_inc(st[a][g % len(ring)], 16)
            for a, (d, ring, sem) in enumerate(outs):
                k = len(ring)
                for i in range(min(k, NG)):
                    e.wait_ge(st[a][i], 16 * ((NG - 1 - i) // k + 1))

        def stored(e, ring, g):
            for a, (d, r, sem) in enumerate(outs):
                if r is ring and g >= len(r):
                    e.wait_ge(st[a][g % len(r)], 16 * (g // len(r)))

        @p.on("tensor")
        def _(e):
            e.wait_ge(*ready)

            def turn(g):
                n = grows[g]
                e.wait_ge(gl[g % 3], 16 * (g // 3 + 1))
                if g:
                    e.wait_ge(tc, g)
                for j in range(4):
                    i = e.transpose(PS[:, 3, n * j:n * j + n], GI3[g % 3][0:n, j, :], ID[0:n, 0:n])
                i.then_inc(tp_, 1)
            if turned:
                turn(0)
            for g in range(NG):
                if turned and g + 1 < NG:
                    turn(g + 1)
                if turned:
                    e.wait_ge(tc, g + 1)
                if g >= 2:
                    e.wait_ge(cb, g - 1)
                mm(e, g, grows[g]).then_inc(pmm, 1)

        @p.on("scalar")
        def _(e):
            for g in range(NG):
                if g:
                    nr.root(e, g - 1)
                e.wait_ge(pmm, g + 1)
                if g:
                    e.wait_ge(cb, g)
                evac(e, g, grows[g]).then_inc(ev, 1)
                if g and norm == "act":
                    if g >= 3:
                        e.wait_ge(fi, g - 2)
                    stored(e, HO, g - 1)
                    nr.apply(e, HO[(g - 1) % 2], XT3[(g - 1) % 3], g - 1)
            nr.root(e, NG - 1)
            if norm == "act":
                if NG >= 3:
                    e.wait_ge(fi, NG - 2)
                stored(e, HO, NG - 1)
                nr.apply(e, HO[(NG - 1) % 2], XT3[(NG - 1) % 3], NG - 1)

        @p.on("vector")
        def _(e):
            def copyt(g):
                e.wait_ge(tp_, g + 1)
                if g >= 2:
                    e.wait_ge(pmm, g - 1)
                e.tensor_copy(HTT[g % 2][:, 0:4 * grows[g]], PS[:, 3, 0:4 * grows[g]]).then_inc(tc, 1)
            if turned:
                copyt(0)

            def fin(g):
                if norm == "act":
                    e.wait_ge(nr.f, g + 1)
                else:
                    e.wait_ge(nr.e_, 2 * g + 2)
                for ring in (TO, HO):
                    if norm != "act" or ring is TO:
                        stored(e, ring, g)
                finish(e, g, grows[g], nr).then_inc(fi, 1)
            for g in range(NG):
                if g:
                    nr.scale(e, g - 1)
                if turned and g + 1 < NG:
                    copyt(g + 1)
                e.wait_ge(ev, g + 1)
                e.wait_ge(xl[g % 3], 16 * (g // 3 + 1))
                if hin is not None:
                    e.wait_ge(gl[g % 3], 16 * (g // 3 + 1))
                if norm != "act" and g >= 3:
                    e.wait_ge(fi, g - 2)
                combine(e, g, grows[g]).then_inc(cb, 1)
                e.wait_ge(cb, g + 1)
                nr_src = XT3[g % 3] if norm == "act" else SC[g % 2]
                nr.moments(e, nr_src, g)
                if g:
                    fin(g - 1)
            nr.scale(e, NG - 1)
            fin(NG - 1)
            e.wait_ge(fi, NG)
        SC = [p.tile([128, 4, D]) for _ in range(2)] if norm != "act" else None
        return SC

    RIN = sb("RIN", [128, NG * 4])
    ROUT = sb("ROUT", [128, NG * 4])

    def p_l1_nodes():
        p = Phase()
        raw, wt_, _, _, wc, nw = weights(p, [w, w_r])
        WT_, WRT = wt_
        LW, WL = p.tile([128, 128]), p.tile([128, 128])
        P2S, T3 = p.tile([128, 4, D]), p.tile([128, 4, D])
        DC, MK, NM, RD = (p.tile([128, NG * 4]) for _ in range(4))
        dend = dram("dend", (min(NP, NC),))
        Q = p.tile([128, 4, D])
        TMP, TZ = p.tile([128, NG * 4]), p.tile([1, 1])
        ll, wp, wq, dv, rin, rdn = (p.sem(k) for k in ("ll", "wp", "wq", "dv", "rin", "rdn"))
        cc, mkd = p.sem("cc"), p.sem("mkd")
        cn = [0]

        dz, dn, dw = p.sem("dz"), p.sem("dn"), p.sem("dw")

        @p.on("sync")
        def _(e):
            e.dma_start(LW[:], loop_w).then_inc(ll, 16)
            e.dma_start(dend.rearrange("(o f) -> o f", o=1), R[64:65, 0:min(NP, NC)]).then_inc(dn, 16)
            e.wait_ge(dn, 16)
            e.wait_ge(dz, 1)
            n = grows[NG - 1]
            if NG > 1:
                e.dma_start(DC[:, 0:4 * (NG - 1)].rearrange("p (g j) -> p g j", j=4),
                            dend[0:512 * (NG - 1)].rearrange("(g p j) -> p g j", p=128, j=4)).then_inc(dn, 16)
            e.dma_start(DC[0:n, 4 * (NG - 1):4 * NG],
                        dend[512 * (NG - 1):512 * (NG - 1) + 4 * n].rearrange("(p j) -> p j", j=4)).then_inc(dn, 16)

        @p.on("tensor")
        def _(e):
            e.wait_ge(ll, 16)
            e.wait_ge(wc, nw)
            e.matmul(PS[:, 7, 0:128], raw[0][:], LW[:], start=True, stop=True).then_inc(wp, 1)

        @p.on("scalar")
        def _(e):
            e.wait_ge(rin, 1)
            e.activation(TMP[:], TMP[:], ACT.Sqrt).then_inc(rdn, 1)

        @p.on("vector")
        def _(e):
            e.memset(DC[:], 0.0).then_inc(dz, 1)
            e.wait_ge(wp, 1)
            e.tensor_copy(WL[:], PS[:, 7, 0:128]).then_inc(wq, 1)
            e.tensor_scalar(TMP[:], DIN[:], 1.0, None, ALU.max).then_inc(rin, 1)
            e.wait_ge(rdn, 1)
            link = chain(e, dv)
            link(e.reciprocal(RIN[:], TMP[:]))
            link(e.tensor_scalar(TMP[:], DIN[:], 1.0, None, ALU.min))
            link(e.tensor_tensor(RIN[:], RIN[:], TMP[:], ALU.mult))
            e.wait_ge(dn, 48 if NG > 1 else 32)
            link(e.tensor_scalar(MK[:], DC[:], 0.0, None, ALU.is_gt))
            link(e.tensor_scalar(NM[:], MK[:], -1.0, 1.0, ALU.mult, ALU.add))
            link(e.tensor_tensor(DC[:], DC[:], NM[:], ALU.add))
            link(e.reciprocal(RD[:], DC[:]))
            e.memset(TZ[:], 0.0).then_inc(mkd, 1)

        def mm(e, g, n):
            ag, ae = jp(AB[:, 0, :], g), jp(AB[:, 1, :], g)
            for j in range(4):
                c = slice(128 * j, 128 * j + 128)
                e.matmul(PS[0:n, bk(0, g), c], ag[:, j, :], WT_[:], start=True, stop=False)
                e.matmul(PS[0:n, bk(0, g), c], ae[:, j, :], WRT[:], start=False, stop=True)
                h = HTT[g % 2][:, n * j:n * j + n]
                e.matmul(PS[0:n, bk(1, g), c], h, WL[:], start=True, stop=True)
                i = e.matmul(PS[0:n, bk(2, g), c], h, WT_[:], start=True, stop=True)
            return i

        def evac(e, g, n):
            e.activation(P2S[0:n], bank(1, n, g), ACT.Copy)
            e.wait_ge(mkd, 1)
            for j in range(4):
                i = e.activation(T3[0:n, j, :], bank(2, n, g)[:, j, :], ACT.Copy, scale=NM[0:n, 4 * g + j:4 * g + j + 1])
            return i

        def combine(e, g, n):
            s = g % 2
            for j in range(4):
                i = e.scalar_tensor_tensor(out=Q[0:n, j, :], in0=bank(0, n, g)[:, j, :], scalar=RD[0:n, 4 * g + j:4 * g + j + 1],
                                           in1=P2S[0:n, j, :], op0=ALU.mult, op1=ALU.add)
            i.then_inc(cc, 1)
            e.wait_ge(cc, 2 * g + 1)
            for j in range(4):
                i = e.scalar_tensor_tensor(out=Q[0:n, j, :], in0=Q[0:n, j, :], scalar=MK[0:n, 4 * g + j:4 * g + j + 1],
                                           in1=T3[0:n, j, :], op0=ALU.mult, op1=ALU.add)
            i.then_inc(cc, 1)
            e.wait_ge(cc, 2 * g + 2)
            return e.scalar_tensor_tensor(out=XT3[g % 3][0:n], in0=Q[0:n], scalar=0.0, in1=XT3[g % 3][0:n],
                                          op0=ALU.max, op1=ALU.add)

        def finish(e, g, n, nr):
            for j in range(4):
                i = e.tensor_scalar(TO[g % 2][0:n, j, :], HO[g % 2][0:n, j, :], RIN[0:n, 4 * g + j:4 * g + j + 1],
                                    None, ALU.mult)
            return i

        nodes(p, x1d, t1d, x2d, True, mm, evac, combine, finish, [(h2d, HO, p.sem("q5")), (t2d, TO, None)], (wq, 1))
        p.run()

    KLS = XR[:, 0:NR * 4]
    IDXS = XR[:, NR * 4:NR * 8].bitcast(I32)

    def p_sorted():
        p = Phase()
        T = AB[:, 0, 0:NR * 4]
        load_list(p, "sorted", 1, KLS, [(1, T)])

        @p.on("vector")
        def _(e):
            e.tensor_copy(IDXS, T).then_inc(p.sem("ix"), 1)
            e.wait_ge(p.sem("ix"), 1)
        p.run()

    def gathered(s):
        return GS[:, s, :, :]

    HK = [AB[:, 1, 512 * g:512 * g + 512].rearrange("p (j f) -> p j f", j=4) for g in range(NG - 1)]

    def aggregate(table, idx, width, part, keys, ACC, weight=None, count=False, keep=False):
        p = Phase()
        if keep:
            @p.on("sync")
            def _(e):
                for g in range(NG - 1):
                    e.dma_start(flat(HK[g], grows[g]), rowsl(h2d, g)).then_inc(p.sem("hk"), 16)
                if NG > 1:
                    e.wait_ge(p.sem("hk"), 16 * (NG - 1))
        ready = gather(p, p.sem("bd"), table[0:NN, :], idx, D)
        edge_pass(p, width, part, keys, gathered, ready, 64, ACC, weight=weight, count=count)

        for k in ("vector", "tensor"):
            @p.on(k)
            def _(e):
                e.wait_ge(p.sem("edone"), 1)
        p.run()

    def p_l2f():
        aggregate(t2d, IDXS, 128, 1, KLS, AB[:, 0, :], count=True, keep=True)

    def p_l2b():
        aggregate(t3d, IDX[:], 48, 0, KLD[:], AB[:, 1, :])

    def p_out_degrees():
        p = Phase()
        TMP = p.tile([128, NG * 4])
        TZ = p.tile([1, 1])
        mm, dg, rt, dv, sc, ro = (p.sem(k) for k in ("mm", "dg", "rt", "dv", "sc", "ro"))
        ld, st, sa = p.sem("ld"), p.sem("st"), p.sem("sa")
        HB = HK + [GF[:, 0:512].rearrange("p (j f) -> p j f", j=4)]

        @p.on("tensor")
        def _(e):
            for g in range(NG):
                n = grows[g]
                for j in range(4):
                    i = e.matmul(PS[0:n, 6, 4 * g + j:4 * g + j + 1], jp(R[0:1, :], g)[:, j, :], ONE[0:1, 0:1],
                                 start=True, stop=True)
            i.then_inc(mm, 1)

        @p.on("scalar")
        def _(e):
            e.wait_ge(dg, 1)
            e.activation(TMP[:], TMP[:], ACT.Sqrt).then_inc(rt, 1)
            e.wait_ge(ro, 1)
            for g in range(1, NG, 3):
                e.wait_ge(ld, 16)
                for j in range(4):
                    i = e.activation(HB[g][0:grows[g], j, :], HB[g][0:grows[g], j, :], ACT.Copy,
                                     scale=ROUT[0:grows[g], 4 * g + j:4 * g + j + 1])
                i.then_inc(sa, 1)

        @p.on("sync")
        def _(e):
            e.dma_start(flat(HB[NG - 1], grows[NG - 1]), rowsl(h2d, NG - 1)).then_inc(ld, 16)
            a, b = 0, 0
            for g in range(NG):
                if g % 3 == 1:
                    a += 1
                    e.wait_ge(sa, a)
                else:
                    b += 1
                    e.wait_ge(sc, b)
                e.dma_start(rowsl(t3d, g), flat(HB[g], grows[g])).then_inc(st, 16)
            e.wait_ge(st, 16 * NG)

        @p.on("vector")
        def _(e):
            link = chain(e, dv)
            n, c = grows[NG - 1], 4 * (NG - 1)
            e.wait_ge(mm, 1)
            if NG > 1:
                e.tensor_copy(DOUT[:, 0:c], PS[:, 6, 0:c])
            link(e.tensor_copy(DOUT[0:n, c:c + 4], PS[0:n, 6, c:c + 4]))
            e.tensor_scalar(TMP[:], DOUT[:], 1.0, None, ALU.max).then_inc(dg, 1)
            e.wait_ge(rt, 1)
            link(e.reciprocal(ROUT[:], TMP[:]))
            link(e.tensor_scalar(TMP[:], DOUT[:], 1.0, None, ALU.min))
            link(e.tensor_tensor(ROUT[:], ROUT[:], TMP[:], ALU.mult))
            e.memset(TZ[:], 0.0).then_inc(ro, 1)
            e.wait_ge(ld, 16)
            for g in range(NG):
                n = grows[g]
                if g % 3 == 1:
                    continue
                for j in range(4):
                    i = e.tensor_scalar(HB[g][0:n, j, :], HB[g][0:n, j, :], ROUT[0:n, 4 * g + j:4 * g + j + 1],
                                        None, ALU.mult)
                i.then_inc(sc, 1)
        p.run()

    def p_l2_nodes():
        p = Phase()
        raw, mats, _, rep, wc, nw = weights(p, [Ws, Wd], [bs, bd_])
        Q, P2S, TY = p.tile([128, 4, D]), p.tile([128, 4, D]), p.tile([1, 1])
        dv, cc = p.sem("dv"), p.sem("cc")

        @p.on("vector")
        def _(e):
            link = chain(e, dv)
            e.wait_ge(wc, nw)
            e.tensor_scalar(mats[0][:], mats[0][:], 0.5, None, ALU.mult)
            e.tensor_scalar(mats[1][:], mats[1][:], 0.5, None, ALU.mult)
            link(e.tensor_tensor(rep[0][:], rep[0][:], rep[1][:], ALU.add))
            link(e.tensor_scalar(rep[0][:], rep[0][:], 0.5, None, ALU.mult))

        def mm(e, g, n):
            for a in range(2):
                for j in range(4):
                    i = e.matmul(PS[0:n, bk(a, g), 128 * j:128 * j + 128], jp(AB[:, a, :], g)[:, j, :], mats[a][:],
                                 start=True, stop=True)
            return i

        def evac(e, g, n):
            for j in range(4):
                i = e.activation(P2S[0:n, j, :], bank(1, n, g)[:, j, :], ACT.Copy, scale=RIN[0:n, 4 * g + j:4 * g + j + 1])
            return i

        def combine(e, g, n):
            for j in range(4):
                i = e.scalar_tensor_tensor(out=Q[0:n, j, :], in0=bank(0, n, g)[:, j, :],
                                           scalar=ROUT[0:n, 4 * g + j:4 * g + j + 1],
                                           in1=P2S[0:n, j, :], op0=ALU.mult, op1=ALU.add)
            i.then_inc(cc, 1)
            e.wait_ge(cc, 2 * g + 1)
            e.tensor_tensor(Q[0:n], Q[0:n], rep[0][0:n].unsqueeze(1).to_broadcast([n, 4, D]), ALU.add).then_inc(cc, 1)
            e.wait_ge(cc, 2 * g + 2)
            return e.tensor_tensor(XT3[g % 3][0:n], Q[0:n], XT3[g % 3][0:n], ALU.add)

        def finish(e, g, n, nr):
            return e.memset(TY[:], 0.0)
        nodes(p, x2d, None, x3d, False, mm, evac, combine, finish, [(t4d, HO, p.sem("q5"))], (dv, 2))
        p.run()

    EW = XR[:, 0:NR * 4]

    def p_weights():
        p = Phase()
        ld = p.sem("ld")
        T = AB[:, 1, 0:NCH * BE].rearrange("p (c k) -> p c k", c=NCH)
        nld = [0]

        @p.on("sync")
        def _(e):
            def put(o, i):
                e.dma_start(o, i).then_inc(ld, 16)
                nld[0] += 1
            for ci, (c0, n) in enumerate(chunks):
                nf = min(n, NBF - c0)
                if nf:
                    put(T[0:nf, ci, :], ew[c0 * BE:(c0 + nf) * BE].rearrange("(b k) -> b k", k=BE))
            n = (NR - 1) % 128
            put(T[n:n + 1, NCH - 1, 0:4 * TP], ew[NBF * BE:NE].rearrange("(b k) -> b k", b=1))
            put(T[n:n + 1, NCH - 1, 4 * TP:BE], ew[NBF * BE:NBF * BE + BE - 4 * TP].rearrange("(b k) -> b k", b=1))
        nput = sum(1 for c0, n in chunks if min(n, NBF - c0)) + 2
        turn_rows(p, (ld, 16 * nput), [(T, EW)])
        p.run()

    def p_l3():
        aggregate(t4d, IDX[:], 48, 0, KLD[:], AB[:, 0, :], weight=EW)

    def p_l3_nodes():
        p = Phase()
        raw, mats, rw, rep, wc, nw = weights(p, [Wrel, Wroot], [brel, gamma, beta])
        P1S, RC = p.tile([128, 4, D]), p.tile([128, NG * 4])
        dv, ff = p.sem("dv"), p.sem("ff")

        @p.on("vector")
        def _(e):
            link = chain(e, dv)
            e.wait_ge(wc, nw)
            link(e.tensor_scalar(RC[:], DIN[:], 1.0, None, ALU.max))
            e.tensor_tensor(mats[1][:], mats[1][:], ID[:], ALU.add)
            link(e.reciprocal(RC[:], RC[:]))

        def mm(e, g, n):
            e.matmul(PS[0:n, bk(1, g), :], ONE[0:1, 0:n], rw[0][:].unsqueeze(1).to_broadcast([1, 4, D]),
                     start=True, stop=False, skip_group_check=True)
            for j in range(4):
                e.matmul(PS[0:n, bk(0, g), 128 * j:128 * j + 128], jp(AB[:, 0, :], g)[:, j, :], mats[0][:], start=True, stop=True)
            for j in range(4):
                i = e.matmul(PS[0:n, bk(1, g), 128 * j:128 * j + 128], HTT[g % 2][:, n * j:n * j + n], mats[1][:],
                             start=False, stop=True, skip_group_check=True)
            return i

        def evac(e, g, n):
            return e.activation(P1S[0:n], bank(1, n, g), ACT.Copy)

        def combine(e, g, n):
            for j in range(4):
                i = e.scalar_tensor_tensor(out=SC[g % 2][0:n, j, :], in0=bank(0, n, g)[:, j, :],
                                           scalar=RC[0:n, 4 * g + j:4 * g + j + 1],
                                           in1=P1S[0:n, j, :], op0=ALU.mult, op1=ALU.add)
            return i

        def finish(e, g, n, nr):
            s = g % 2
            Y = SC[s][0:n]
            for j in range(4):
                i = e.tensor_scalar(Y[:, j, :], Y[:, j, :], nr.rs[s][0:n, j:j + 1], nr.nm[s][0:n, j:j + 1],
                                    ALU.mult, ALU.add)
            i.then_inc(nr.f, 1)
            e.wait_ge(nr.f, g + 1)
            e.tensor_tensor(Y, Y, rep[1][0:n].unsqueeze(1).to_broadcast([n, 4, D]), ALU.mult).then_inc(ff, 1)
            e.wait_ge(ff, 2 * g + 1)
            e.tensor_tensor(Y, Y, rep[2][0:n].unsqueeze(1).to_broadcast([n, 4, D]), ALU.add).then_inc(ff, 1)
            e.wait_ge(ff, 2 * g + 2)
            return e.scalar_tensor_tensor(out=TO[s][0:n], in0=Y, scalar=0.0, in1=XT3[g % 3][0:n],
                                          op0=ALU.max, op1=ALU.add)
        SC = nodes(p, x3d, t4d, None, True, mm, evac, combine, finish, [(out, TO, None)], (dv, 2), norm="dve")
        p.run()

    for phase in (p_const, p_lists, p_prep, p_l0, p_flag, p_l1, p_l1_nodes, p_sorted, p_l2f, p_out_degrees,
                  p_l2b, p_l2_nodes, p_weights, p_l3, p_l3_nodes):
        phase()


_INS = ["x", "src", "dst", "edge_attr_128", "edge_weight", "L0_gnn_u", "L0_gnn_W1", "L0_gnn_b1", "L0_gnn_W2",
        "L0_gnn_b2", "L1_gnn_w", "L1_gnn_w_r", "L1_gnn_att_w", "L1_gnn_loop_w", "L2_gnn_W_src", "L2_gnn_b_src",
        "L2_gnn_W_dst", "L2_gnn_b_dst", "L3_gnn_W_rel", "L3_gnn_b_rel", "L3_gnn_W_root", "L3_gnn_gamma",
        "L3_gnn_beta"]


def kernel(**inputs):
    import numpy as _np
    import concourse.bacc as _bacc
    from concourse import mybir as _mybir
    from concourse.bass_utils import run_bass_kernel_spmd as _run

    nc = _bacc.Bacc("TRN2", target_bir_lowering=False, num_devices=1, dynamic_dma_scratch_size=8192)
    arrays, args = {}, []
    for name in _INS:
        a = _np.ascontiguousarray(inputs[name])
        arrays[f"in_{name}"] = a
        args.append(nc.dram_tensor(f"in_{name}", a.shape, _mybir.dt.from_np(a.dtype), kind="ExternalInput").ap())
    shape = inputs["x"].shape
    out = nc.dram_tensor("out_0", shape, _mybir.dt.float32, kind="ExternalOutput").ap()
    gnn(nc, *args, out)
    r = _run(nc, [arrays], core_ids=[0])
    return r.results[0]["out_0"]
```
